# Optimizing a Trainium2 kernel written in Bass

```python
import numpy as np
import jax
import jax.numpy as jnp

def _softmax(x, axis=-1):
    return jax.nn.softmax(x, axis=axis)

def _gelu(x):
    return jax.nn.gelu(x, approximate=True)

def _silu(x):
    return jax.nn.silu(x)

def _sigmoid(x):
    return jax.nn.sigmoid(x)

def _layernorm(x, axis=-1, eps=1e-05):
    m = jnp.mean(x, axis=axis, keepdims=True)
    v = jnp.var(x, axis=axis, keepdims=True)
    return (x - m) / jnp.sqrt(v + eps)

def _scatter_add(tgt, idx, src, axis=0):
    return tgt.at[idx].add(src)

def _segment_sum(src, seg, n):
    return jax.ops.segment_sum(src, seg, n)
kernel_name = 'mk_early_fusion_d1_tok_img768_r4_f88055'

def setup_inputs(seed: int=0):
    np.random.seed(seed)
    _w = jnp.asarray

    def _rec_inputs():
        import jax
        import jax.numpy as jnp
        _rk = jax.random.key(seed)
        x = -0.000222058 + 0.999998 * jax.random.normal(jax.random.fold_in(_rk, 1), (8, 3, 64, 64), jnp.float32)
        txt = 0.00457738 + 10 * jax.random.normal(jax.random.fold_in(_rk, 2), (8, 512, 192), jnp.float32)
        return (x, txt)
    x, txt = _rec_inputs()

    def _L0_tok_setup():
        import jax, jax.numpy as jnp
        import numpy as np
        B, C, IMG, P = (128, 3, 64, 16)
        HP = IMG // P
        EMBED = 192

        def dct_basis(N, dtype=jnp.float32):
            n = jnp.arange(N, dtype=dtype)
            k = jnp.arange(N, dtype=dtype)[:, None]
            return 2.0 * jnp.cos(jnp.pi * (2.0 * n + 1.0) * k / (2.0 * N))
        key = jax.random.key(seed)
        k1, k2 = jax.random.split(key)
        x = jax.random.normal(k1, (B, C, IMG, IMG), dtype=jnp.float32)
        W = jax.random.normal(k2, (EMBED, C * P * P), dtype=jnp.float32) / np.sqrt(C * P * P)
        return {'x': x, 'W': W}
    _L0_tok_all = _L0_tok_setup()
    _L0_tok_in = {k: v for k, v in _L0_tok_all.items() if k in ('W',)}
    del _L0_tok_all

    def _L0_attn_setup():
        import jax, jax.numpy as jnp
        import numpy as np
        EPS = 1e-05
        B, T, C = (8, 512, 192)
        H = 4 * C
        LAYER_ID, N_LAYER = (4, 12)

        def _ln(x, w, b):
            mu = x.mean(-1, keepdims=True)
            var = ((x - mu) ** 2).mean(-1, keepdims=True)
            return (x - mu) / jnp.sqrt(var + EPS) * w + b

        def _wkv_scan(w, k, v):
            a0 = jnp.zeros(k.shape[1:], k.dtype)
            b0 = jnp.zeros_like(a0)
            m0 = jnp.full_like(a0, -1e+38)

            def step(carry, kv):
                a, b, m = carry
                kt, vt = kv
                mm = jnp.maximum(m + w, kt)
                e1 = jnp.exp(m + w - mm)
                e2 = jnp.exp(kt - mm)
                return ((e1 * a + e2 * vt, e1 * b + e2, mm), (a, b, m))
            _, (A, Bd, M) = jax.lax.scan(step, (a0, b0, m0), (k, v))
            return (A, Bd, M)

        def bi_wkv(w, u, k, v):
            kt = jnp.swapaxes(k, 0, 1)
            vt = jnp.swapaxes(v, 0, 1)
            af, bf, mf = _wkv_scan(w, kt, vt)
            ab, bb, mb = _wkv_scan(w, kt[::-1], vt[::-1])
            ab, bb, mb = (ab[::-1], bb[::-1], mb[::-1])
            kk = kt + u
            M = jnp.maximum(jnp.maximum(mf, mb), kk)
            ef = jnp.exp(mf - M)
            eb = jnp.exp(mb - M)
            ec = jnp.exp(kk - M)
            y = (ef * af + eb * ab + ec * vt) / (ef * bf + eb * bb + ec)
            return jnp.swapaxes(y, 0, 1)
        key = jax.random.key(seed)
        ks = jax.random.split(key, 9)
        x = jax.random.normal(ks[0], (B, T, C), jnp.float32)
        r01 = LAYER_ID / (N_LAYER - 1)
        h = np.arange(C, dtype=np.float64)
        decay = (-5.0 + 8.0 * (h / (C - 1)) ** (0.7 + 1.3 * r01)).astype(np.float32)
        zigzag = ((np.arange(C) + 1) % 3 - 1).astype(np.float32) * 0.5
        first = (np.float32(np.log(0.3)) + zigzag).astype(np.float32)
        s = 0.02
        return {'x': x, 'ln1_w': jnp.ones((C,), jnp.float32), 'ln1_b': jnp.zeros((C,), jnp.float32), 'ln2_w': jnp.ones((C,), jnp.float32), 'ln2_b': jnp.zeros((C,), jnp.float32), 'decay': jnp.asarray(decay), 'first': jnp.asarray(first), 'Wk_a': s * jax.random.normal(ks[1], (C, C), jnp.float32), 'Wv_a': s * jax.random.normal(ks[2], (C, C), jnp.float32), 'Wr_a': s * jax.random.normal(ks[3], (C, C), jnp.float32), 'Wo_a': s * jax.random.normal(ks[4], (C, C), jnp.float32), 'Wk_f': s * jax.random.normal(ks[5], (H, C), jnp.float32), 'Wv_f': s * jax.random.normal(ks[6], (C, H), jnp.float32), 'Wr_f': s * jax.random.normal(ks[7], (C, C), jnp.float32)}
    _L0_attn_all = _L0_attn_setup()
    _L0_attn_in = {k: v for k, v in _L0_attn_all.items() if k in ('ln1_w', 'ln1_b', 'ln2_w', 'ln2_b', 'decay', 'first', 'Wk_a', 'Wv_a', 'Wr_a', 'Wo_a', 'Wk_f', 'Wv_f', 'Wr_f')}
    del _L0_attn_all

    def _L0_ffn_setup():
        import jax, jax.numpy as jnp
        import numpy as np
        QN, QP = (-8, 7)

        def round_pass(x):
            return x + jax.lax.stop_gradient(jnp.round(x) - x)

        def _quant_act(x, alpha_a):
            a = alpha_a.mean()
            return round_pass(jnp.clip(x / a, QN, QP))

        def _quant_w(w, alpha_w):
            return round_pass(jnp.clip(w / alpha_w[:, None], QN, QP))
        key = jax.random.key(seed)
        ks = jax.random.split(key, 9)
        B, S, D, H = (16, 256, 192, 768)

        def unif(k, shape):
            return jax.random.uniform(k, shape, jnp.float32, 0.02, 0.1)
        return {'x0': jax.random.normal(ks[0], (B, S, D), jnp.float32), 'w1': jax.random.normal(ks[1], (H, D), jnp.float32) * 0.02, 'b1': jax.random.normal(ks[2], (H,), jnp.float32) * 0.02, 'alpha_w1': unif(ks[3], (H,)), 'alpha_a1': unif(ks[4], (D,)), 'w2': jax.random.normal(ks[5], (D, H), jnp.float32) * 0.02, 'b2': jax.random.normal(ks[6], (D,), jnp.float32) * 0.02, 'alpha_w2': unif(ks[7], (D,)), 'alpha_a2': unif(ks[8], (H,))}
    _L0_ffn_all = _L0_ffn_setup()
    _L0_ffn_in = {k: v for k, v in _L0_ffn_all.items() if k in ('w1', 'b1', 'alpha_w1', 'alpha_a1', 'w2', 'b2', 'alpha_w2', 'alpha_a2')}
    del _L0_ffn_all
    return {'x': x, 'txt': txt, 'L0_tok_W': _L0_tok_in['W'], 'L0_attn_ln1_w': _L0_attn_in['ln1_w'], 'L0_attn_ln1_b': _L0_attn_in['ln1_b'], 'L0_attn_ln2_w': _L0_attn_in['ln2_w'], 'L0_attn_ln2_b': _L0_attn_in['ln2_b'], 'L0_attn_decay': _L0_attn_in['decay'], 'L0_attn_first': _L0_attn_in['first'], 'L0_attn_Wk_a': _L0_attn_in['Wk_a'], 'L0_attn_Wv_a': _L0_attn_in['Wv_a'], 'L0_attn_Wr_a': _L0_attn_in['Wr_a'], 'L0_attn_Wo_a': _L0_attn_in['Wo_a'], 'L0_attn_Wk_f': _L0_attn_in['Wk_f'], 'L0_attn_Wv_f': _L0_attn_in['Wv_f'], 'L0_attn_Wr_f': _L0_attn_in['Wr_f'], 'L0_ffn_w1': _L0_ffn_in['w1'], 'L0_ffn_b1': _L0_ffn_in['b1'], 'L0_ffn_alpha_w1': _L0_ffn_in['alpha_w1'], 'L0_ffn_alpha_a1': _L0_ffn_in['alpha_a1'], 'L0_ffn_w2': _L0_ffn_in['w2'], 'L0_ffn_b2': _L0_ffn_in['b2'], 'L0_ffn_alpha_w2': _L0_ffn_in['alpha_w2'], 'L0_ffn_alpha_a2': _L0_ffn_in['alpha_a2']}

def reference(x, txt, L0_tok_W, L0_attn_ln1_w, L0_attn_ln1_b, L0_attn_ln2_w, L0_attn_ln2_b, L0_attn_decay, L0_attn_first, L0_attn_Wk_a, L0_attn_Wv_a, L0_attn_Wr_a, L0_attn_Wo_a, L0_attn_Wk_f, L0_attn_Wv_f, L0_attn_Wr_f, L0_ffn_w1, L0_ffn_b1, L0_ffn_alpha_w1, L0_ffn_alpha_a1, L0_ffn_w2, L0_ffn_b2, L0_ffn_alpha_w2, L0_ffn_alpha_a2):
    import jax
    import jax.numpy as jnp

    def _L0_tok_ref(x, W):
        import jax, jax.numpy as jnp
        import numpy as np
        B, C, IMG, P = (128, 3, 64, 16)
        HP = IMG // P
        EMBED = 192

        def dct_basis(N, dtype=jnp.float32):
            n = jnp.arange(N, dtype=dtype)
            k = jnp.arange(N, dtype=dtype)[:, None]
            return 2.0 * jnp.cos(jnp.pi * (2.0 * n + 1.0) * k / (2.0 * N))
        b = x.shape[0]
        xp = x.reshape(b, C, HP, P, HP, P).transpose(0, 2, 4, 1, 3, 5)
        D = dct_basis(P, xp.dtype)
        y = jnp.einsum('bhwcnm,kn,lm->bhwckl', xp, D, D)
        y = y.reshape(b, HP, HP, C * P * P)
        y = jnp.einsum('bhwf,ef->bhwe', y, W)
        return y.reshape(b, HP * HP, EMBED)

    def _L0_attn_ref(x, ln1_w, ln1_b, ln2_w, ln2_b, decay, first, Wk_a, Wv_a, Wr_a, Wo_a, Wk_f, Wv_f, Wr_f):
        import jax, jax.numpy as jnp
        import numpy as np
        EPS = 1e-05
        B, T, C = (8, 512, 192)
        H = 4 * C
        LAYER_ID, N_LAYER = (4, 12)

        def _ln(x, w, b):
            mu = x.mean(-1, keepdims=True)
            var = ((x - mu) ** 2).mean(-1, keepdims=True)
            return (x - mu) / jnp.sqrt(var + EPS) * w + b

        def _wkv_scan(w, k, v):
            a0 = jnp.zeros(k.shape[1:], k.dtype)
            b0 = jnp.zeros_like(a0)
            m0 = jnp.full_like(a0, -1e+38)

            def step(carry, kv):
                a, b, m = carry
                kt, vt = kv
                mm = jnp.maximum(m + w, kt)
                e1 = jnp.exp(m + w - mm)
                e2 = jnp.exp(kt - mm)
                return ((e1 * a + e2 * vt, e1 * b + e2, mm), (a, b, m))
            _, (A, Bd, M) = jax.lax.scan(step, (a0, b0, m0), (k, v))
            return (A, Bd, M)

        def bi_wkv(w, u, k, v):
            kt = jnp.swapaxes(k, 0, 1)
            vt = jnp.swapaxes(v, 0, 1)
            af, bf, mf = _wkv_scan(w, kt, vt)
            ab, bb, mb = _wkv_scan(w, kt[::-1], vt[::-1])
            ab, bb, mb = (ab[::-1], bb[::-1], mb[::-1])
            kk = kt + u
            M = jnp.maximum(jnp.maximum(mf, mb), kk)
            ef = jnp.exp(mf - M)
            eb = jnp.exp(mb - M)
            ec = jnp.exp(kk - M)
            y = (ef * af + eb * ab + ec * vt) / (ef * bf + eb * bb + ec)
            return jnp.swapaxes(y, 0, 1)
        Bn, Tn, Cn = x.shape
        h = _ln(x, ln1_w, ln1_b)
        k = h @ Wk_a.T
        v = h @ Wv_a.T
        sr = jax.nn.sigmoid(h @ Wr_a.T)
        y = bi_wkv(decay / Tn, first / Tn, k, v)
        x = x + sr * y @ Wo_a.T
        h = _ln(x, ln2_w, ln2_b)
        kf = jnp.square(jax.nn.relu(h @ Wk_f.T))
        x = x + jax.nn.sigmoid(h @ Wr_f.T) * (kf @ Wv_f.T)
        return x

    def _L0_ffn_ref(x0, w1, b1, alpha_w1, alpha_a1, w2, b2, alpha_w2, alpha_a2):
        import jax, jax.numpy as jnp
        import numpy as np
        QN, QP = (-8, 7)

        def round_pass(x):
            return x + jax.lax.stop_gradient(jnp.round(x) - x)

        def _quant_act(x, alpha_a):
            a = alpha_a.mean()
            return round_pass(jnp.clip(x / a, QN, QP))

        def _quant_w(w, alpha_w):
            return round_pass(jnp.clip(w / alpha_w[:, None], QN, QP))
        xq = _quant_act(x0, alpha_a1)
        wq1 = _quant_w(w1, alpha_w1)
        x1 = jnp.einsum('bsd,hd->bsh', xq, wq1)
        x1 = x1 * alpha_w1 * alpha_a1.mean() + b1
        x1 = jax.nn.gelu(x1, approximate=False)
        x1 = jnp.clip(x1, -10.0, 10.0)
        hq = _quant_act(x1, alpha_a2)
        wq2 = _quant_w(w2, alpha_w2)
        x2 = jnp.einsum('bsh,dh->bsd', hq, wq2)
        x2 = x2 * alpha_w2 * alpha_a2.mean() + b2
        return x2
    h = _L0_tok_ref(x, L0_tok_W)
    h = jnp.concatenate([h, txt], axis=1)
    h = h + _L0_attn_ref(_layernorm(h, axis=-1), L0_attn_ln1_w, L0_attn_ln1_b, L0_attn_ln2_w, L0_attn_ln2_b, L0_attn_decay, L0_attn_first, L0_attn_Wk_a, L0_attn_Wv_a, L0_attn_Wr_a, L0_attn_Wo_a, L0_attn_Wk_f, L0_attn_Wv_f, L0_attn_Wr_f)
    h = h + _L0_ffn_ref(_layernorm(h, axis=-1), L0_ffn_w1, L0_ffn_b1, L0_ffn_alpha_w1, L0_ffn_alpha_a1, L0_ffn_w2, L0_ffn_b2, L0_ffn_alpha_w2, L0_ffn_alpha_a2)
    return h

_drawn_inputs = setup_inputs


def setup_inputs(seed=0):
    import zlib

    import numpy as np

    out = dict(_drawn_inputs(seed))
    spreads = {'L0_attn_ln1_w': (1.0, 0.6),
     'L0_attn_ln1_b': (0.0, 0.8),
     'L0_attn_ln2_w': (1.0, 0.6),
     'L0_attn_ln2_b': (0.0, 0.8)}
    factors = {'L0_attn_decay': 8.0,
     'L0_attn_first': 200.0,
     'L0_attn_Wk_a': 8.0,
     'L0_attn_Wv_a': 8.0,
     'L0_attn_Wr_a': 8.0,
     'L0_attn_Wo_a': 8.0,
     'L0_attn_Wk_f': 8.0,
     'L0_attn_Wv_f': 8.0,
     'L0_attn_Wr_f': 8.0,
     'L0_ffn_w1': 8.0,
     'L0_ffn_b1': 37.981,
     'L0_ffn_alpha_w1': 8.0,
     'L0_ffn_w2': 8.0,
     'L0_ffn_b2': 64.0,
     'L0_ffn_alpha_w2': 8.0,
     'L0_ffn_alpha_a2': 200.0}
    for name, (base, spread) in spreads.items():
        noise = np.random.default_rng([zlib.crc32(name.encode()), seed]).standard_normal(out[name].shape)
        drawn = base * np.exp(spread * noise) if base else spread * noise
        out[name] = jnp.asarray(drawn.astype(out[name].dtype))
    for name, factor in factors.items():
        out[name] = (out[name] * factor).astype(out[name].dtype)
    return out
```

```python
from contextlib import ExitStack

import concourse.bass as bass
from concourse import mybir

F32 = mybir.dt.float32
F16 = mybir.dt.float16
BF16 = mybir.dt.bfloat16
ALU = mybir.AluOpType
ACT = mybir.ActivationFunctionType
AX_X = mybir.AxisListType.X

P = 128
B, TXT, C, HID = 8, 512, 192, 768
IMG = 16
T = IMG + TXT
CA, CB = 128, C - 128
PAIRS = B // 2
SLOTS = B + PAIRS
QT = TXT // P
TILES = 1 + B * QT
G = HID // P
EPS = 1e-5
WSCALE = 256.0
MAGIC = 1.5 * 2.0 ** 23
QN, QP = -8.0, 7.0
CLIP = 10.0
NEG = -1e38
KVR = 3 * C
GB = 3 * CA
PATCHES = P


COLS = {name: i for i, name in enumerate(
    ["ln1_w", "ln1_wb", "ln1_b", "ln1_bb", "ln2_w", "ln2_wb", "ln2_b", "ln2_bb", "decay", "decay_b", "first", "first_b"])}
NCOL = len(COLS) + 2 * G
ROWS = {"alpha_w1": (0, HID), "alpha_a2": (HID, HID), "alpha_a1": (2 * HID, C),
        "alpha_w2": (2 * HID + C, C), "b2": (2 * HID + 2 * C, C)}
NROW = 2 * HID + 3 * C


def fusion_kernel(nc, txt, xt, kron, tok_w, ident, cols, rows, attn_w, kf_src, rf_src, wo_src, vf_src, w1, w2, out):
    with ExitStack() as ctx:
        def sb(name, shape, dt=F32):
            return ctx.enter_context(nc.sbuf_tensor(name, shape, dt))

        def sem(name):
            return ctx.enter_context(nc.semaphore(name))

        hid = sb("hid", [P, TILES, C])
        x1 = sb("x1", [P, TILES, C])
        k_all = sb("k_all", [P, SLOTS, T])
        v_all = sb("v_all", [P, SLOTS, T])
        r_all = sb("r_all", [P, SLOTS, T])

        id32 = sb("id32", [P, P])
        id16 = sb("id16", [P, P], F16)
        idb = sb("idb", [P, P], BF16)
        kvr_w = sb("kvr_w", [P, 4, KVR], F16)
        kf_w = sb("kf_w", [P, 4, HID], F16)
        rf_w = sb("rf_w", [P, 4, C], F16)
        rf_bias = sb("rf_bias", [P, 2, C], F16)
        vf_w = sb("vf_w", [P, G, C])
        wo_w = sb("wo_w", [P, 2, C])
        q1_w = sb("q1_w", [P, 2, HID], BF16)
        q2_w = sb("q2_w", [P, G, C], BF16)
        col = sb("col", [P, NCOL])
        lnw = sb("lnw", [P, 4])
        rate = sb("rate", [P, 2, SLOTS])
        bias = sb("bias", [P, 16])
        aw1c = col[:, len(COLS):len(COLS) + G]
        b1s = col[:, len(COLS) + G:NCOL]
        scale1 = sb("scale1", [P, G])
        scale2 = sb("scale2", [P, C])
        b2s = sb("b2s", [P, C])
        aq = sb("aq", [P, 8])
        minus_half = sb("minus_half", [P, 2 * QT])

        st = sb("st", [P, 2, QT, 6])
        mv2 = sb("mv2", [P, 2, QT, 2])
        rs2 = sb("rs2", [P, 2, 2, QT])
        z = sb("z", [P, QT, 2, P])
        za = sb("za", [P, 2, TXT], F16)
        zb = sb("zb", [P, TXT], F16)

        ARENA = 12688
        arena = sb("arena", [P, ARENA])

        class Carve:
            def __init__(self):
                self.at = 0

            def __call__(self, n):
                self.at += n
                assert self.at <= ARENA
                return arena[:, self.at - n:self.at]

        carve = Carve()
        xt_sb = carve(2 * 3 * PATCHES).rearrange("p (a n) -> p a n", a=2)
        kron_sb = carve(2 * 256).rearrange("p (a n) -> p a n", a=2)
        tokw_sb = carve(6 * C).rearrange("p (a n) -> p a n", a=6)
        yt = carve(2 * 3 * PATCHES).rearrange("p (a c n) -> p a c n", a=2, c=3)
        wa_raw = carve(2 * KVR).rearrange("p (a n) -> p a n", a=2)
        kf_raw = carve(2 * HID).rearrange("p (a n) -> p a n", a=2)
        rf_raw = carve(2 * C).rearrange("p (a n) -> p a n", a=2)
        wtmp = z[:].rearrange("p q a n -> p (q a n)")[:, 0:HID]
        w1_raw = carve(2 * HID).rearrange("p (a n) -> p a n", a=2)
        w2_raw = carve(G * C).rearrange("p (a n) -> p a n", a=G)
        row = carve(NROW)
        aw1_row, a2_row, a1_row, aw2, b2_row = (row[:, a:a + n] for a, n in ROWS.values())
        inv_row = carve(HID)
        inv2_row = carve(C)

        carve = Carve()
        W2 = 2 * (T + 1)
        env = [carve(W2) for _ in range(2)]
        sa = carve(W2)
        sbk = carve(W2)
        decay = [carve(2 * T) for _ in range(2)]
        gain = [carve(2 * T) for _ in range(2)]
        peak = [carve(T) for _ in range(2)]
        mix = [carve(3 * T) for _ in range(2)]
        gain_v = kvr_w[:].rearrange("p a n -> p (a n)").bitcast(F32)[:, 0:2 * T]

        carve = Carve()
        kf = carve(G * TXT).rearrange("p (g n) -> p g n", g=G)
        ge = carve(G * TXT).rearrange("p (g n) -> p g n", g=G)
        hq = carve(G * TXT // 2).bitcast(BF16).rearrange("p (g n) -> p g n", g=G)
        rya = carve(TXT)
        ryb = carve(TXT)
        th = carve(2 * C).rearrange("p (a n) -> p a n", a=2)
        gv = carve(2 * C).rearrange("p (a n) -> p a n", a=2)
        xs = carve(QT * C).rearrange("p (q n) -> p q n", q=QT)
        xq = carve(QT * P).bitcast(BF16).rearrange("p (q a n) -> p q a n", q=QT, a=2)
        xqt = carve(TXT).bitcast(BF16).rearrange("p (a n) -> p a n", a=2)
        y2 = carve(2 * C).rearrange("p (a n) -> p a n", a=2)

        bank = [ctx.enter_context(nc.psum_tensor(f"bank{i}", [P, 512], F32)) for i in range(8)]

        tok_loaded, attn_loaded, mlp_loaded, ffn_loaded = (sem(n) for n in ("tok_loaded", "attn_loaded", "mlp_loaded", "ffn_loaded"))
        text_even_loaded, text_odd_loaded = sem("text_even_loaded"), sem("text_odd_loaded")
        setup_dve, setup_pool, constants_ready = sem("setup_dve"), sem("setup_pool"), sem("constants_ready")
        dct_done, dct_copied, img_done, img_copied = (sem(n) for n in ("dct_done", "dct_copied", "img_done", "img_copied"))
        bias_done, bias_copied = sem("bias_done"), sem("bias_copied")
        stat_step, stats_ready, power_step, powers_ready, z_ready, z_turned = (
            sem(n) for n in ("stat_step", "stats_ready", "power_step", "powers_ready", "z_ready", "z_turned"))
        hi_ready, lo_ready = sem("hi_ready"), sem("lo_ready")
        ka_done, va_done, ra_done, kb_done, vb_done, projected = (
            sem(n) for n in ("ka_done", "va_done", "ra_done", "kb_done", "vb_done", "projected"))
        k_stored, v_stored, r_stored = sem("k_stored"), sem("v_stored"), sem("r_stored")
        k_copied, env_ready, peak_step, peak_ready = sem("k_copied"), sem("env_ready"), sem("peak_step"), sem("peak_ready")
        decay_arg, gain_arg, mix_arg = sem("decay_arg"), sem("gain_arg"), sem("mix_arg")
        decay_exp, gain_exp, mix_exp = sem("decay_exp"), sem("gain_exp"), sem("mix_exp")
        gain_v_ready, sums_b_ready, sums_a_ready = sem("gain_v_ready"), sem("sums_b_ready"), sem("sums_a_ready")
        den_parts, num_parts, own_num, comb_step, y_ready = (sem(n) for n in ("den_parts", "num_parts", "own_num", "comb_step", "y_ready"))
        ry_ready, attn_done, x2_ready, hx_ready = (sem(n) for n in ("ry_ready", "attn_done", "x2_ready", "hx_ready"))
        z2_ready, z2_turned, hi2_ready, lo2_ready = (sem(n) for n in ("z2_ready", "z2_turned", "hi2_ready", "lo2_ready"))
        stat2_step, stats2_ready, power2_step, powers2_ready = (sem(n) for n in ("stat2_step", "stats2_ready", "power2_step", "powers2_ready"))
        kf_done, kf_relu, kf_ready, gate_done, gate_tanh, gated, h3_ready = (
            sem(n) for n in ("kf_done", "kf_relu", "kf_ready", "gate_done", "gate_tanh", "gated", "h3_ready"))
        stat3_step, stats3_ready, power3_step, powers3_ready, xs_ready, xs_clipped, xq_ready = (
            sem(n) for n in ("stat3_step", "stats3_ready", "power3_step", "powers3_ready", "xs_ready", "xs_clipped", "xq_ready"))
        xq_turned, xqt_ready, up_done, gelu_ready, ge_scaled, ge_rounded, hq_ready = (
            sem(n) for n in ("xq_turned", "xqt_ready", "up_done", "gelu_ready", "ge_scaled", "ge_rounded", "hq_ready"))
        held = sem("held")
        h3b_ready, down_done, y2_ready, out_ready, stored = (
            sem(n) for n in ("h3b_ready", "down_done", "y2_ready", "out_ready", "stored"))

        def tiles_of(n):
            return 1 if isinstance(n, int) and n == 0 else QT

        def tile0(n):
            return 0 if isinstance(n, int) and n == 0 else (n - 1) * QT + 1

        def width(n):
            return P * tiles_of(n)

        def excl(buf):
            return _two(buf, 0, T + 2)

        def incl(buf):
            return _two(buf, 1, T)

        def _two(buf, at, step):
            return bass.AP(buf.tensor, buf.offset + at, [list(buf.ap[0]), [step, 2], [1, T]])

        def vec(name):
            return col[:, COLS[name]:COLS[name] + 1]

        def two_before(t):
            return t - 1 if not isinstance(t, int) or t > 1 else t

        def twice(ap):
            return bass.AP(ap.tensor, ap.offset, [list(ap.ap[0]), [0, 2], list(ap.ap[1])])

        def halves(ap, n=T):
            return ap.rearrange("p (a n) -> p a n", n=n)

        def img_slots(a):
            return a[:, 0:B, 0:IMG].rearrange("p (g a) t -> p a g t", a=2)

        def img_cols(ps):
            return ps.rearrange("p (a g t) -> p a g t", a=2, g=PAIRS)

        def img_b(a):
            return a[:, B:SLOTS, 0:IMG]

        def hold(eng, semaphore, value):
            eng.wait_ge(semaphore, value)
            if not isinstance(value, int):
                eng.sem_inc(held, 1)

        block = ctx.enter_context(nc.Block())

        @block.sync
        def _(sp):
            for dst, src in ((xt_sb, xt), (kron_sb, kron), (tokw_sb, tok_w), (id32[:], ident)):
                sp.dma_start(dst, src).then_inc(tok_loaded, 16)
            with sp.Fori(0, PAIRS) as p:
                for parity, loaded in ((0, text_even_loaded), (1, text_odd_loaded)):
                    b = p * 2 + parity
                    sp.dma_start(hid[:, bass.ds(b * QT + 1, QT), :],
                                 txt[bass.ds(b, 1)].rearrange("a (q p) c -> p (a q) c", p=P)).then_inc(loaded, 16)
                    hold(sp, loaded, p * 16 + 16)
            def image_out():
                sp.wait_ge(out_ready, 1)
                for parity in range(2):
                    for g in range(PAIRS):
                        at = 64 * parity + IMG * g
                        sp.dma_start(out[2 * g + parity, 0:IMG, :], hid[at:at + IMG, 0, :]).then_inc(stored, 16)

            image_out()
            with sp.Fori(0, B) as b:
                hold(sp, out_ready, b * QT + QT + 1)
                sp.dma_start(out[bass.ds(b, 1), IMG:T, :].rearrange("a (q p) c -> p (a q) c", p=P),
                             hid[:, bass.ds(b * QT + 1, QT), :]).then_inc(stored, 16)
            sp.wait_ge(stored, 16 * (B + B))

        @block.gpsimd
        def _(pool):
            nc.gpsimd.memset(minus_half[:], -0.5).then_inc(setup_pool, 1)
            pool.wait_ge(setup_pool, 1)

            def tile(a, t):
                return a[:, bass.ds(t, 1), :].rearrange("p a c -> p (a c)")

            def powers(n, par):
                nt = tiles_of(n)
                var, rs = mv2[:, par, 0:nt, 1], rs2[:, par]
                hold(pool, stats_ready, n + 1)
                nc.gpsimd.tensor_scalar(rs[:, 0, 0:nt], var, EPS, None, ALU.add).then_inc(power_step, 1)
                nc.gpsimd.tensor_scalar(rs[:, 1, 0:nt], var, 1.0 + EPS, EPS * EPS, ALU.mult, ALU.add).then_inc(power_step, 1)
                pool.wait_ge(power_step, 2 * n + 2)
                nc.gpsimd.tensor_tensor(rs[:, :, 0:nt], rs[:, :, 0:nt],
                                        minus_half[:].rearrange("p (a n) -> p a n", a=2)[:, :, 0:nt], ALU.pow).then_inc(powers_ready, 1)

            powers(0, 0)
            with pool.Fori(0, PAIRS) as p:
                powers(p * 2 + 1, 1)
                powers(p * 2 + 2, 0)

            def arguments(j, par):
                pool.wait_ge(env_ready, j + 1)
                k_t = slot(k_all, j)
                nc.gpsimd.tensor_tensor(halves(decay[par]), excl(env[par]), incl(env[par]), ALU.subtract).then_inc(decay_arg, 1)
                nc.gpsimd.tensor_tensor(halves(gain[par]), twice(k_t), incl(env[par]), ALU.subtract).then_inc(gain_arg, 1)
                pool.wait_ge(peak_ready, j + 1)
                nc.gpsimd.tensor_tensor(halves(mix[par])[:, 0:2], excl(env[par]), twice(peak[par]), ALU.subtract).then_inc(mix_arg, 1)

            def products(j, par):
                pool.wait_ge(mix_exp, j + 1)
                m = halves(mix[par])
                pool.wait_ge(sums_b_ready, j + 1)
                nc.gpsimd.tensor_tensor(excl(sbk), m[:, 0:2], excl(sbk), ALU.mult).then_inc(den_parts, 1)
                nc.gpsimd.tensor_tensor(peak[par], m[:, 2], slot(v_all, j), ALU.mult).then_inc(own_num, 1)

            def slot(a, j):
                return a[:, bass.ds(j, 1), :].rearrange("p a t -> p (a t)")

            pool.wait_ge(k_stored, 2 + B + PAIRS)
            pool.wait_ge(v_stored, 2 + B + PAIRS)
            arguments(0, 0)
            with pool.Fori(0, SLOTS // 2 - 1) as i:
                arguments(i * 2 + 1, 1)
                products(i * 2, 0)
                arguments(i * 2 + 2, 0)
                products(i * 2 + 1, 1)
            arguments(SLOTS - 1, 1)
            products(SLOTS - 2, 0)
            products(SLOTS - 1, 1)

            def norm2(n):
                nt, t0 = tiles_of(n), tile0(n)
                hold(pool, stats2_ready, n + 1)
                nc.gpsimd.tensor_scalar(rs2[:, 0, 0, 0:nt], mv2[:, 0, 0:nt, 1], EPS, None, ALU.add).then_inc(power2_step, 1)
                pool.wait_ge(power2_step, n + 1)
                nc.gpsimd.tensor_tensor(rs2[:, 0, 0, 0:nt], rs2[:, 0, 0, 0:nt], minus_half[:, 0:nt], ALU.pow).then_inc(powers2_ready, 1)
                for q in range(nt):
                    nc.gpsimd.tensor_tensor(tile(hid, t0 + q), tile(hid, t0 + q), tile(x1, t0 + q), ALU.add).then_inc(hx_ready, 1)

            def norm3(n):
                nt, t0 = tiles_of(n), tile0(n)
                rs = rs2[:, 1, 0, 0:nt]
                hold(pool, stats3_ready, n + 1)
                nc.gpsimd.tensor_scalar(rs, mv2[:, 1, 0:nt, 1], EPS, None, ALU.add).then_inc(power3_step, 1)
                pool.wait_ge(power3_step, n * 2 + 1)
                nc.gpsimd.tensor_tensor(rs, rs, minus_half[:, 0:nt], ALU.pow).then_inc(power3_step, 1)
                hold(pool, power3_step, n * 2 + 2)
                nc.gpsimd.tensor_scalar(rs, rs, aq[:, 1:2], None, ALU.mult).then_inc(powers3_ready, 1)
                hold(pool, xs_ready, tile0(n) + nt)
                for q in range(nt):
                    nc.gpsimd.tensor_tensor(tile(hid, t0 + q), tile(hid, t0 + q), b2s[:], ALU.add).then_inc(h3b_ready, 1)

            def finish(n):
                nt, t0 = tiles_of(n), tile0(n)
                for q in range(nt):
                    pool.wait_ge(y2_ready, t0 + q + 1)
                    hold(pool, h3b_ready, t0 + q + 1)
                    nc.gpsimd.tensor_tensor(tile(hid, t0 + q), tile(hid, t0 + q), y2[:, q % 2], ALU.add).then_inc(out_ready, 1)

            pool.wait_ge(constants_ready, 1)
            norm2(0)
            norm3(0)
            norm2(1)
            finish(0)
            norm3(1)
            with pool.Fori(0, PAIRS - 1) as p:
                for odd in range(2):
                    n = p * 2 + 2 + odd
                    norm2(n)
                    finish(n - 1)
                    norm3(n)
            norm2(B)
            finish(B - 1)
            norm3(B)
            finish(B)

        @block.vector
        def _(dve):
            count = [0]

            def did(ins):
                count[0] += 1
                ins.then_inc(setup_dve, 1)

            def settled():
                dve.wait_ge(setup_dve, count[0])

            V = nc.vector
            dve.wait_ge(tok_loaded, 64)
            did(V.tensor_copy(id16[:], id32[:]))
            did(V.tensor_copy(idb[:], id32[:]))

            def split(raw, lw, dst, n):
                did(V.tensor_scalar(wtmp[:, 0:n], raw, lw, None, ALU.mult))
                settled()
                did(V.tensor_copy(dst[:, 0], wtmp[:, 0:n]))
                settled()
                did(V.tensor_tensor(dst[:, 1], wtmp[:, 0:n], dst[:, 0], ALU.subtract))
                settled()

            dve.wait_ge(attn_loaded, 16 * 2)
            for j, name in enumerate(("ln1_w", "ln1_wb", "ln2_w", "ln2_wb")):
                did(V.tensor_scalar(lnw[:, j:j + 1], vec(name), WSCALE, None, ALU.mult))
            settled()
            for h in range(2):
                split(wa_raw[:, h], lnw[:, h:h + 1], kvr_w[:, 2 * h:2 * h + 2], KVR)
            for h in range(2):
                dve.wait_ge(dct_done, h + 1)
                V.tensor_copy(yt[:, h].rearrange("p c n -> p (c n)"), bank[h][:, 0:3 * PATCHES]).then_inc(dct_copied, 1)
            dve.wait_ge(img_done, 1)
            V.tensor_copy(hid[:, 0], bank[2][:, 0:C]).then_inc(img_copied, 1)

            dve.wait_ge(mlp_loaded, 16 * 4)
            for h in range(2):
                split(kf_raw[:, h], lnw[:, 2 + h:3 + h], kf_w[:, 2 * h:2 * h + 2], HID)
                split(rf_raw[:, h], lnw[:, 2 + h:3 + h], rf_w[:, 2 * h:2 * h + 2], C)
            dve.wait_ge(bias_done, 1)
            V.tensor_copy(bias[:, 0:12], bank[3][:, 0:12]).then_inc(bias_copied, 1)
            dve.wait_ge(bias_copied, 1)
            did(V.tensor_scalar(bias[:, 12:13], bias[:, 2:3], 0.5, None, ALU.mult))
            did(V.tensor_scalar(bias[:, 13:14], bias[:, 5:6], 0.5, None, ALU.mult))
            did(V.tensor_scalar(wtmp[:, 0:C], bank[4][:, 0:C], WSCALE, None, ALU.mult))
            settled()
            did(V.tensor_copy(rf_bias[:, 0], wtmp[:, 0:C]))
            settled()
            did(V.tensor_tensor(rf_bias[:, 1], wtmp[:, 0:C], rf_bias[:, 0], ALU.subtract))
            for which, name in enumerate(("decay", "first")):
                for at, n, tail_ in ((0, B, ""), (B, PAIRS, "_b")):
                    did(V.tensor_scalar(rate[:, which, at:at + n], vec(name + tail_).to_broadcast([P, n]), 1.0 / T, None, ALU.mult))

            dve.wait_ge(ffn_loaded, 16 * 3)
            did(V.reciprocal(inv_row, aw1_row))
            did(V.reciprocal(inv2_row, aw2))
            settled()

            def quantize(dst, raw, inv):
                did(V.tensor_tensor(raw, raw, inv, ALU.mult))
                settled()
                did(V.tensor_scalar(raw, raw, QP, QN, ALU.min, ALU.max))
                settled()
                did(V.tensor_scalar(dst, raw, MAGIC, MAGIC, ALU.add, ALU.subtract))

            for h in range(2):
                quantize(q1_w[:, h], w1_raw[:, h], inv_row)
            quantize(q2_w[:], w2_raw, bass.AP(inv2_row.tensor, inv2_row.offset, [list(inv2_row.ap[0]), [0, G], [1, C]]))
            did(V.reduce_sum(aq[:, 0:1], a1_row, AX_X))
            did(V.reduce_sum(aq[:, 2:3], a2_row, AX_X))
            settled()
            did(V.tensor_scalar(aq[:, 0:1], aq[:, 0:1], 1.0 / C, None, ALU.mult))
            did(V.tensor_scalar(aq[:, 2:3], aq[:, 2:3], 1.0 / HID, None, ALU.mult))
            settled()
            did(V.reciprocal(aq[:, 1:2], aq[:, 0:1]))
            did(V.reciprocal(aq[:, 3:4], aq[:, 2:3]))
            did(V.tensor_copy(b2s[:], b2_row))
            did(V.tensor_scalar(scale1[:], aw1c, aq[:, 0:1], None, ALU.mult))
            did(V.tensor_scalar(scale2[:], aw2, aq[:, 2:3], None, ALU.mult))
            settled()
            did(V.tensor_scalar(aq[:, 7:8], aq[:, 3:4], CLIP, None, ALU.mult))
            settled()
            did(V.scalar_tensor_tensor(aq[:, 6:7], aq[:, 3:4], -CLIP, aq[:, 7:8], ALU.mult, ALU.max))
            settled()
            did(V.tensor_scalar(aq[:, 4:5], aq[:, 6:7], QP, None, ALU.min))
            settled()
            V.tensor_scalar(aq[:, 5:6], aq[:, 6:7], -1.0, QN, ALU.mult, ALU.max).then_inc(constants_ready, 1)
            dve.wait_ge(constants_ready, 1)

            def tile(a, t):
                return a[:, bass.ds(t, 1), :].rearrange("p a c -> p (a c)")

            def statistics(n, par, before, step, ready, data):
                nt, t0 = tiles_of(n), tile0(n)
                for q in range(nt):
                    before(q)
                    V.bn_stats(st[:, par, q], tile(data, t0 + q)).then_inc(step, 1)
                hold(dve, step, t0 + nt)
                for q in range(nt):
                    ins = V.bn_aggr(mv2[:, par, q], st[:, par, q])
                ins.then_inc(ready, 1)

            def write_z(src, t0, nt, par, which):
                for q in range(nt):
                    x = tile(src, t0 + q)
                    V.tensor_scalar(z[:, q, 0], x[:, 0:CA], mv2[:, par, q, 0:1], rs2[:, par, which, q:q + 1], ALU.subtract, ALU.mult)
                    ins = V.tensor_scalar(z[:, q, 1].rearrange("p (a c) -> p a c", a=2), twice(x[:, CA:C]),
                                          mv2[:, par, q, 0:1], rs2[:, par, which, q:q + 1], ALU.subtract, ALU.mult)
                return ins

            def low_half(n, hi, lo, nw):
                dve.wait_ge(hi, n + 1)
                V.tensor_tensor(za[:, 1, 0:nw], bank[0][:, 0:nw], za[:, 0, 0:nw], ALU.subtract)
                V.tensor_tensor(zb[CB:P, 0:nw], bank[1][CB:P, 0:nw], zb[CB:P, 0:nw], ALU.subtract).then_inc(lo, 1)

            def project(n, par):
                first = isinstance(n, int) and n == 0
                nt, t0 = tiles_of(n), tile0(n)
                if not first:
                    dve.wait_ge(z_turned, n)
                dve.wait_ge(powers_ready, n + 1)
                write_z(hid, t0, nt, par, 1).then_inc(z_ready, 1)
                for q in range(nt):
                    V.tensor_scalar(tile(x1, t0 + q), tile(hid, t0 + q), mv2[:, par, q, 0:1], rs2[:, par, 0, q:q + 1],
                                    ALU.subtract, ALU.mult)
                low_half(n, hi_ready, lo_ready, width(n))
                dve.wait_ge(va_done, n + 1)
                if first:
                    V.tensor_scalar(img_slots(v_all), img_cols(bank[3][:, 0:P]), 1 / WSCALE, bias[:, 1:2], ALU.mult, ALU.add).then_inc(v_stored, 1)
                    dve.wait_ge(vb_done, 1)
                    V.tensor_scalar(img_b(v_all), bank[6][:, 0:64].rearrange("p (g t) -> p g t", g=PAIRS),
                                    1 / WSCALE, bias[:, 4:5], ALU.mult, ALU.add).then_inc(v_stored, 1)
                else:
                    V.tensor_scalar(v_all[:, bass.ds(n - 1, 1), IMG:T].rearrange("p a t -> p (a t)"), bank[3][:],
                                    1 / WSCALE, bias[:, 1:2], ALU.mult, ALU.add).then_inc(v_stored, 1)

            def project_b(p):
                dve.wait_ge(vb_done, p + 2)
                V.tensor_scalar(v_all[:, bass.ds(p + B, 1), IMG:T].rearrange("p a t -> p (a t)"), bank[6][:],
                                1 / WSCALE, bias[:, 4:5], ALU.mult, ALU.add).then_inc(v_stored, 1)

            def measure(n, par):
                statistics(n, par, lambda q: None, stat_step, stats_ready, hid)

            def even_loaded(p):
                hold(dve, text_even_loaded, p * 16 + 16)

            def odd_loaded(p):
                hold(dve, text_odd_loaded, p * 16 + 16)

            dve.wait_ge(img_copied, 1)
            measure(0, 0)
            even_loaded(0)
            measure(1, 1)
            project(0, 0)
            with dve.Fori(0, PAIRS - 1) as p:
                odd_loaded(p)
                measure(p * 2 + 2, 0)
                project(p * 2 + 1, 1)
                even_loaded(p + 1)
                measure(p * 2 + 3, 1)
                project(p * 2 + 2, 0)
                project_b(p)
            odd_loaded(PAIRS - 1)
            measure(B, 0)
            project(B - 1, 1)
            project(B, 0)
            project_b(PAIRS - 1)

            def slot(a, j):
                return a[:, bass.ds(j, 1), :].rearrange("p a t -> p (a t)")

            F0, B0 = 1, T + 1
            dve.wait_ge(projected, 1 + B)
            for buf, val in ((env[0], NEG), (env[1], NEG), (sa, 0.0), (sbk, 0.0)):
                V.memset(buf[:, 0:1], val).then_inc(comb_step, 1)
                V.memset(buf[:, 2 * T + 1:2 * T + 2], val).then_inc(comb_step, 1)
            INIT = 8
            dve.wait_ge(comb_step, INIT)
            dve.wait_ge(k_stored, 2 + B + PAIRS)

            def envelopes(j, par):
                w = rate[:, 0, bass.ds(j, 1)]
                k_t = slot(k_all, j)
                wb = w.to_broadcast([P, T])
                V.tensor_tensor_scan(env[par][:, F0:F0 + T], wb, k_t, NEG, ALU.add, ALU.max)
                dve.wait_ge(k_copied, j + 1)
                V.tensor_tensor_scan(env[par][:, B0:B0 + T][:, ::-1], wb, gain[par][:, T:2 * T][:, ::-1], NEG, ALU.add, ALU.max).then_inc(env_ready, 1)
                dve.wait_ge(env_ready, j + 1)
                V.tensor_tensor(peak[par], env[par][:, 0:T], env[par][:, T + 2:2 * T + 2], ALU.max).then_inc(peak_step, 1)
                dve.wait_ge(peak_step, j * 2 + 1)
                u = rate[:, 1, bass.ds(j, 1)]
                V.scalar_tensor_tensor(peak[par], k_t, u, peak[par], ALU.add, ALU.max).then_inc(peak_step, 1)
                dve.wait_ge(peak_step, j * 2 + 2)
                V.scalar_tensor_tensor(halves(mix[par])[:, 2], k_t, u, peak[par], ALU.add, ALU.subtract).then_inc(peak_ready, 1)

            def combine(j, par):
                v_t = slot(v_all, j)
                dve.wait_ge(gain_exp, j + 1)
                V.tensor_tensor(halves(gain_v), halves(gain[par]), twice(v_t), ALU.mult).then_inc(gain_v_ready, 1)
                dve.wait_ge(decay_exp, j + 1)
                d, g = halves(decay[par]), halves(gain[par])
                V.tensor_tensor_scan(sbk[:, F0:F0 + T], d[:, 0], g[:, 0], 0.0, ALU.mult, ALU.add)
                V.tensor_tensor_scan(sbk[:, B0:B0 + T][:, ::-1], d[:, 1][:, ::-1], g[:, 1][:, ::-1], 0.0, ALU.mult, ALU.add).then_inc(sums_b_ready, 1)
                dve.wait_ge(gain_v_ready, j + 1)
                gv2 = halves(gain_v)
                V.tensor_tensor_scan(sa[:, F0:F0 + T], d[:, 0], gv2[:, 0], 0.0, ALU.mult, ALU.add)
                V.tensor_tensor_scan(sa[:, B0:B0 + T][:, ::-1], d[:, 1][:, ::-1], gv2[:, 1][:, ::-1], 0.0, ALU.mult, ALU.add).then_inc(sums_a_ready, 1)
                dve.wait_ge(sums_a_ready, j + 1)
                dve.wait_ge(mix_exp, j + 1)
                V.tensor_tensor(excl(sa), halves(mix[par])[:, 0:2], excl(sa), ALU.mult).then_inc(num_parts, 1)
                dve.wait_ge(num_parts, j + 1)
                num, nb = sa[:, 0:T], sa[:, T + 2:2 * T + 2]
                den, db = sbk[:, 0:T], sbk[:, T + 2:2 * T + 2]
                step = j * 6 + INIT
                V.tensor_tensor(num, num, nb, ALU.add).then_inc(comb_step, 1)
                dve.wait_ge(den_parts, j + 1)
                V.tensor_tensor(den, den, db, ALU.add).then_inc(comb_step, 1)
                dve.wait_ge(own_num, j + 1)
                dve.wait_ge(comb_step, step + 2)
                V.tensor_tensor(den, den, halves(mix[par])[:, 2], ALU.add).then_inc(comb_step, 1)
                V.tensor_tensor(num, num, peak[par], ALU.add).then_inc(comb_step, 1)
                dve.wait_ge(comb_step, step + 4)
                V.reciprocal(halves(decay[par])[:, 0], den).then_inc(comb_step, 1)
                dve.wait_ge(comb_step, step + 5)
                V.tensor_tensor(slot(k_all, j), num, halves(decay[par])[:, 0], ALU.mult).then_inc(y_ready, 1)
                dve.wait_ge(y_ready, j + 1)
                V.memset(sa[:, 0:1], 0.0)
                V.memset(sa[:, 2 * T + 1:2 * T + 2], 0.0)
                V.memset(sbk[:, 0:1], 0.0)
                V.memset(sbk[:, 2 * T + 1:2 * T + 2], 0.0).then_inc(comb_step, 1)

            envelopes(0, 0)
            with dve.Fori(0, SLOTS // 2 - 1) as i:
                envelopes(i * 2 + 1, 1)
                combine(i * 2, 0)
                envelopes(i * 2 + 2, 0)
                combine(i * 2 + 1, 1)
            envelopes(SLOTS - 1, 1)
            combine(SLOTS - 2, 0)
            combine(SLOTS - 1, 1)

            def gate_y(n, half):
                first = isinstance(n, int) and n == 0
                dve.wait_ge(y_ready, SLOTS)
                if not first:
                    dve.wait_ge(attn_done, n)
                if first:
                    V.scalar_tensor_tensor(img_cols(rya[:, 0:P])[:, 0], img_slots(r_all)[:, 0], 1.0, img_slots(k_all)[:, 0], ALU.add, ALU.mult)
                    V.scalar_tensor_tensor(img_cols(rya[:, 0:P])[:, 1], img_slots(r_all)[:, 1], 1.0, img_slots(k_all)[:, 1], ALU.add, ALU.mult)
                    V.scalar_tensor_tensor(ryb[:, 0:64].rearrange("p (g t) -> p g t", g=PAIRS), img_b(r_all), 1.0, img_b(k_all), ALU.add, ALU.mult).then_inc(ry_ready, 1)
                else:
                    b = n - 1
                    V.scalar_tensor_tensor(rya, slot(r_all, b)[:, IMG:T], 1.0, slot(k_all, b)[:, IMG:T], ALU.add, ALU.mult)
                    s = half[1]
                    V.scalar_tensor_tensor(ryb[half[0]:half[0] + CB], slot(r_all, s)[half[0]:half[0] + CB, IMG:T], 1.0,
                                           slot(k_all, s)[half[0]:half[0] + CB, IMG:T], ALU.add, ALU.mult).then_inc(ry_ready, 1)

            def residual2(n):
                nt, t0 = tiles_of(n), tile0(n)

                def x2(q):
                    if q % 2 == 0:
                        dve.wait_ge(attn_done, n + 1)
                    V.scalar_tensor_tensor(tile(x1, t0 + q), bank[6 if q < 2 else 7][:, (q % 2) * C:(q % 2 + 1) * C], 0.5,
                                           tile(x1, t0 + q), ALU.mult, ALU.add).then_inc(x2_ready, 1)
                    hold(dve, x2_ready, t0 + q + 1)
                statistics(n, 0, x2, stat2_step, stats2_ready, x1)

            def normalize2(n):
                if not (isinstance(n, int) and n == 0):
                    dve.wait_ge(z2_turned, n)
                dve.wait_ge(powers2_ready, n + 1)
                write_z(x1, tile0(n), tiles_of(n), 0, 0).then_inc(z2_ready, 1)

            def squares(n):
                nw = width(n)
                for g in range(G):
                    dve.wait_ge(kf_relu, n * G + g + 1)
                    V.tensor_tensor(kf[:, g, 0:nw], kf[:, g, 0:nw], kf[:, g, 0:nw], ALU.mult).then_inc(kf_ready, 1)

            def residual3(n):
                nt, t0 = tiles_of(n), tile0(n)

                def h3(q):
                    dve.wait_ge(gate_tanh, t0 + q + 1)
                    ps = bank[2 + q % 2]
                    V.scalar_tensor_tensor(gv[:, q % 2], th[:, q % 2], 1.0, ps[:, 0:C], ALU.add, ALU.mult).then_inc(gated, 1)
                    dve.wait_ge(gated, t0 + q + 1)
                    dve.wait_ge(hx_ready, t0 + q + 1)
                    V.scalar_tensor_tensor(tile(hid, t0 + q), gv[:, q % 2], 0.5, tile(hid, t0 + q), ALU.mult, ALU.add).then_inc(h3_ready, 1)
                    hold(dve, h3_ready, t0 + q + 1)
                statistics(n, 1, h3, stat3_step, stats3_ready, hid)
                dve.wait_ge(powers3_ready, n + 1)
                for q in range(nt):
                    ins = V.tensor_scalar(xs[:, q], tile(hid, t0 + q), mv2[:, 1, q, 0:1], rs2[:, 1, 0, q:q + 1], ALU.subtract, ALU.mult)
                    ins.then_inc(xs_ready, 1)
                dve.wait_ge(xs_ready, t0 + nt)
                V.tensor_scalar(xs[:, 0:nt], xs[:, 0:nt], QP, QN, ALU.min, ALU.max).then_inc(xs_clipped, 1)
                dve.wait_ge(xs_clipped, n + 1)
                if not (isinstance(n, int) and n == 0):
                    dve.wait_ge(xq_turned, n)
                V.tensor_scalar(xq[:, 0:nt, 0], xs[:, 0:nt, 0:CA], MAGIC, MAGIC, ALU.add, ALU.subtract)
                for twin in range(2):
                    ins = V.tensor_scalar(xq[:, 0:nt, 1, twin * CB:(twin + 1) * CB], xs[:, 0:nt, CA:C], MAGIC, MAGIC, ALU.add, ALU.subtract)
                ins.then_inc(xq_ready, 1)

            def turned(n):
                nw = width(n)
                dve.wait_ge(xq_turned, n + 1)
                V.tensor_copy(xqt[:, :, 0:nw], bank[1][:].bitcast(BF16).rearrange("p (a n) -> p a n", a=2)[:, :, 0:nw]).then_inc(xqt_ready, 1)

            def round_hidden(n):
                nw = width(n)
                for g in range(0, G, 2):
                    dve.wait_ge(gelu_ready, n * G + g + 2)
                    V.tensor_scalar(ge[:, g:g + 2, 0:nw], ge[:, g:g + 2, 0:nw], aq[:, 3:4], aq[:, 4:5], ALU.mult, ALU.min).then_inc(ge_scaled, 1)
                    dve.wait_ge(ge_scaled, n * (G // 2) + g // 2 + 1)
                    V.tensor_scalar(ge[:, g:g + 2, 0:nw], ge[:, g:g + 2, 0:nw], aq[:, 5:6], MAGIC, ALU.max, ALU.add).then_inc(ge_rounded, 1)

            def scaled_out(n):
                nt, t0 = tiles_of(n), tile0(n)
                for q in range(nt):
                    dve.wait_ge(down_done, t0 + q + 1)
                    if not (isinstance(n, int) and n == 0):
                        dve.wait_ge(out_ready, two_before(t0 + q))
                    V.tensor_tensor(y2[:, q % 2], bank[q % 2][:, 0:C], scale2[:], ALU.mult).then_inc(y2_ready, 1)

            def main(n, half, m):
                gate_y(n, half)
                residual2(n)
                if m is not None:
                    turned(m)
                normalize2(n)
                low_half(n, hi2_ready, lo2_ready, width(n))
                if m is not None:
                    round_hidden(m)
                squares(n)
                if m is not None:
                    scaled_out(m)
                residual3(n)

            def tail(m):
                turned(m)
                round_hidden(m)
                scaled_out(m)

            main(0, None, None)
            main(1, (0, B), 0)
            with dve.Fori(0, PAIRS - 1) as p:
                main(p * 2 + 2, (CB, p + B), p * 2 + 1)
                main(p * 2 + 3, (0, p + B + 1), p * 2 + 2)
            main(B, (CB, B + PAIRS - 1), B - 1)
            tail(B)

        @block.scalar
        def _(act):
            A = nc.scalar
            for dst, src in ((col[:], cols), (wa_raw, attn_w)):
                act.dma_start(dst, src).then_inc(attn_loaded, 16)
            for dst, src in ((kf_raw, kf_src), (rf_raw, rf_src), (wo_w[:], wo_src), (vf_w[:], vf_src)):
                act.dma_start(dst, src).then_inc(mlp_loaded, 16)
            for dst, src in ((row, rows.to_broadcast([P, NROW])), (w1_raw, w1), (w2_raw, w2)):
                act.dma_start(dst, src).then_inc(ffn_loaded, 16)

            def high_half(n, turned, hi, nw, used):
                act.wait_ge(turned, n + 1)
                used()
                A.activation(za[:, 0, 0:nw], bank[0][:, 0:nw], ACT.Identity)
                A.activation(zb[:, 0:nw], bank[1][:, 0:nw], ACT.Identity).then_inc(hi, 1)

            def project(n):
                first = isinstance(n, int) and n == 0
                high_half(n, z_turned, hi_ready, width(n), lambda: None if first else act.wait_ge(projected, n))
                if first:
                    act.wait_ge(bias_copied, 1)
                    act.wait_ge(ka_done, 1)
                    A.activation(img_slots(k_all), img_cols(bank[2][:, 0:P]), ACT.Identity, bias=bias[:, 0:1], scale=1 / WSCALE).then_inc(k_stored, 1)
                    act.wait_ge(ra_done, 1)
                    act.wait_ge(constants_ready, 1)
                    A.activation(img_slots(r_all), img_cols(bank[4][:, 0:P]), ACT.Tanh, bias=bias[:, 12:13], scale=0.5 / WSCALE).then_inc(r_stored, 1)
                    act.wait_ge(kb_done, 1)
                    A.activation(img_b(k_all), bank[5][:, 0:64].rearrange("p (g t) -> p g t", g=PAIRS), ACT.Identity, bias=bias[:, 3:4], scale=1 / WSCALE).then_inc(k_stored, 1)
                    act.wait_ge(projected, 1)
                    A.activation(img_b(r_all), bank[7][:, 0:64].rearrange("p (g t) -> p g t", g=PAIRS), ACT.Tanh, bias=bias[:, 13:14], scale=0.5 / WSCALE).then_inc(r_stored, 1)
                else:
                    act.wait_ge(ka_done, n + 1)
                    A.activation(k_all[:, bass.ds(n - 1, 1), IMG:T].rearrange("p a t -> p (a t)"), bank[2][:], ACT.Identity, bias=bias[:, 0:1], scale=1 / WSCALE).then_inc(k_stored, 1)
                    act.wait_ge(ra_done, n + 1)
                    A.activation(r_all[:, bass.ds(n - 1, 1), IMG:T].rearrange("p a t -> p (a t)"), bank[4][:], ACT.Tanh, bias=bias[:, 12:13], scale=0.5 / WSCALE).then_inc(r_stored, 1)

            project(0)
            with act.Fori(0, PAIRS) as p:
                project(p * 2 + 1)
                project(p * 2 + 2)
                act.wait_ge(kb_done, p + 2)
                A.activation(k_all[:, bass.ds(p + B, 1), IMG:T].rearrange("p a t -> p (a t)"), bank[5][:], ACT.Identity, bias=bias[:, 3:4], scale=1 / WSCALE).then_inc(k_stored, 1)
                act.wait_ge(projected, p * 2 + 3)
                A.activation(r_all[:, bass.ds(p + B, 1), IMG:T].rearrange("p a t -> p (a t)"), bank[7][:], ACT.Tanh, bias=bias[:, 13:14], scale=0.5 / WSCALE).then_inc(r_stored, 1)

            def exponentials(j, par):
                act.wait_ge(decay_arg, j + 1)
                A.activation(decay[par], decay[par], ACT.Exp, bias=rate[:, 0, bass.ds(j, 1)]).then_inc(decay_exp, 1)
                act.wait_ge(gain_arg, j + 1)
                A.activation(gain[par], gain[par], ACT.Exp).then_inc(gain_exp, 1)
                act.wait_ge(mix_arg, j + 1)
                act.wait_ge(peak_ready, j + 1)
                A.activation(mix[par], mix[par], ACT.Exp).then_inc(mix_exp, 1)

            def copy_k(j, par):
                if not (isinstance(j, int) and j < 2):
                    act.wait_ge(sums_a_ready, j - 1)
                A.activation(gain[par][:, T:2 * T], k_all[:, bass.ds(j, 1), :].rearrange("p a t -> p (a t)"), ACT.Copy).then_inc(k_copied, 1)

            act.wait_ge(k_stored, 2 + B + PAIRS)
            act.wait_ge(projected, 1 + B)
            copy_k(0, 0)
            copy_k(1, 1)
            with act.Fori(0, SLOTS // 2 - 1) as i:
                for par in range(2):
                    exponentials(i * 2 + par, par)
                    copy_k(i * 2 + par + 2, par)
            exponentials(SLOTS - 2, 0)
            exponentials(SLOTS - 1, 1)

            def relus(n):
                nw = width(n)
                for g in range(G):
                    act.wait_ge(kf_done, n * G + g + 1)
                    if g == 0 and not (isinstance(n, int) and n == 0):
                        act.wait_ge(gate_done, tile0(n))
                    A.activation(kf[:, g, 0:nw], bank[4 + g % 2][:, 0:nw], ACT.Relu, bias=bias[:, 6 + g:7 + g], scale=1 / WSCALE).then_inc(kf_relu, 1)

            def gates(n):
                nt, t0 = tiles_of(n), tile0(n)
                for q in range(nt):
                    act.wait_ge(gate_done, t0 + q + 1)
                    if not (isinstance(n, int) and n == 0):
                        act.wait_ge(gated, two_before(t0 + q))
                    A.activation(th[:, q % 2], bank[2 + q % 2][:, 256:256 + C], ACT.Tanh, scale=0.5 / WSCALE).then_inc(gate_tanh, 1)

            def gelus(n):
                nw = width(n)
                for g in range(G):
                    act.wait_ge(up_done, n * G + g + 1)
                    if g == 0 and not (isinstance(n, int) and n == 0):
                        act.wait_ge(hq_ready, n * (G // 2))
                    A.activation(ge[:, g, 0:nw], bank[4 + g % 2][:, 0:nw], ACT.Gelu, bias=b1s[:, g:g + 1], scale=scale1[:, g:g + 1]).then_inc(gelu_ready, 1)

            def hidden(n):
                nw, t0 = width(n), tile0(n)
                for g in range(0, G, 2):
                    act.wait_ge(ge_rounded, n * (G // 2) + g // 2 + 1)
                    if g == 0 and not (isinstance(n, int) and n == 0):
                        act.wait_ge(down_done, t0)
                    A.activation(hq[:, g:g + 2, 0:nw], ge[:, g:g + 2, 0:nw], ACT.Copy, bias=-MAGIC).then_inc(hq_ready, 1)

            def main(n, m):
                if m is not None:
                    gelus(m)
                high_half(n, z2_turned, hi2_ready, width(n), lambda: None if isinstance(n, int) and n == 0 else act.wait_ge(gate_done, tile0(n)))
                if m is not None:
                    hidden(m)
                relus(n)
                gates(n)

            act.wait_ge(y_ready, SLOTS)
            main(0, None)
            main(1, 0)
            with act.Fori(0, PAIRS - 1) as p:
                main(p * 2 + 2, p * 2 + 1)
                main(p * 2 + 3, p * 2 + 2)
            main(B, B - 1)
            gelus(B)
            hidden(B)

        @block.tensor
        def _(pe):
            pe.wait_ge(tok_loaded, 64)
            for h in range(2):
                for a in range(2):
                    mm = pe.matmul(bank[h][:, 0:3 * PATCHES], kron_sb[:, a, h * P:(h + 1) * P], xt_sb[:, a], start=a == 0, stop=a == 1)
                mm.then_inc(dct_done, 1)
            pe.wait_ge(dct_copied, 2)
            for c in range(3):
                for h in range(2):
                    mm = pe.matmul(bank[2][:, 0:C], yt[:, h, c], tokw_sb[:, 2 * c + h], start=c + h == 0, stop=c + h == 3)
            mm.then_inc(img_done, 1)

            pe.wait_ge(attn_loaded, 16 * 2)
            pe.wait_ge(mlp_loaded, 16 * 4)

            def bias_column(dst, raw, cols, b):
                pe.matmul(dst, raw[:, 0, cols], vec(b), start=True, stop=False)
                pe.matmul(dst, raw[0:CB, 1, cols], vec(b + "b")[0:CB], start=False, stop=True)

            for j in range(3):
                bias_column(bank[3][:, j:j + 1], wa_raw, slice(j * CA, (j + 1) * CA), "ln1_b")
                for half in (0, CB):
                    bias_column(bank[3][half:half + CB, 3 + j:4 + j], wa_raw, slice(GB + j * CB, GB + (j + 1) * CB), "ln1_b")
            for g in range(G):
                bias_column(bank[3][:, 6 + g:7 + g], kf_raw, slice(g * P, (g + 1) * P), "ln2_b")
            pe.matmul(bank[4][:, 0:C], vec("ln2_b").to_broadcast([P, P]), rf_raw[:, 0], start=True, stop=False)
            pe.matmul(bank[4][:, 0:C], vec("ln2_bb")[0:CB].to_broadcast([CB, P]), rf_raw[0:CB, 1], start=False, stop=True).then_inc(bias_done, 1)

            def turn(n, done):
                nt = tiles_of(n)
                for q in range(nt):
                    for a in range(2):
                        mm = pe.transpose(bank[a][:, q * P:(q + 1) * P], z[:, q, a], id32[:])
                mm.then_inc(done, 1)

            def group(dst, w, cols, rhs):
                for i, (ww, zz) in enumerate(((w[:, 0, cols], za[:, 0]), (w[:, 0, cols], za[:, 1]), (w[:, 1, cols], za[:, 0]),
                                              (w[:, 2, cols], zb[:]), (w[:, 3, cols], zb[:]))):
                    mm = pe.matmul(dst, ww, zz[:, rhs], start=i == 0, stop=i == 4)
                return mm

            def project(n, half, p):
                first = isinstance(n, int) and n == 0
                if first:
                    pe.wait_ge(bias_copied, 1)
                    pe.wait_ge(constants_ready, 1)
                pe.wait_ge(z_ready, n + 1)
                if not first:
                    pe.wait_ge(lo_ready, n)
                turn(n, z_turned)
                pe.wait_ge(lo_ready, n + 1)
                nw = width(n)
                for j, (stored, done) in enumerate(((k_stored, ka_done), (v_stored, va_done), (r_stored, ra_done))):
                    if not first:
                        pe.wait_ge(stored, p * 3 + (3 if half else 1))
                    group(bank[2 + j][:, 0:nw], kvr_w, slice(j * CA, (j + 1) * CA), slice(0, nw)).then_inc(done, 1)
                for j, (stored, done) in enumerate(((k_stored, kb_done), (v_stored, vb_done), (r_stored, projected))):
                    wcols = slice(GB + j * CB, GB + (j + 1) * CB)
                    if first:
                        group(bank[5 + j][0:CB, 0:64], kvr_w, wcols, slice(0, 64))
                        group(bank[5 + j][CB:P, 0:64], kvr_w, wcols, slice(64, 128)).then_inc(done, 1)
                    else:
                        if not half:
                            pe.wait_ge(stored, p * 3 + 2)
                        mm = group(bank[5 + j][half:half + CB], kvr_w, wcols, slice(0, nw))
                        if half or j == 2:
                            mm.then_inc(done, 1)

            project(0, 0, None)
            with pe.Fori(0, PAIRS) as p:
                project(p * 2 + 1, 0, p)
                project(p * 2 + 2, CB, p)

            def attention_out(n, half):
                nt = tiles_of(n)
                first = isinstance(n, int) and n == 0
                pe.wait_ge(ry_ready, n + 1)
                if not first:
                    pe.wait_ge(x2_ready, tile0(n))
                if first:
                    for a in range(2):
                        rows = slice(a * 64, a * 64 + 64)
                        pe.matmul(bank[6][rows, 0:C], rya[:, rows], wo_w[:, 0], start=True, stop=False)
                        mm = pe.matmul(bank[6][rows, 0:C], ryb[rows, 0:64], wo_w[rows, 1], start=False, stop=True)
                else:
                    for q in range(nt):
                        cols = slice(q * P, (q + 1) * P)
                        dst = bank[6 if q < 2 else 7][:, (q % 2) * C:(q % 2 + 1) * C]
                        pe.matmul(dst, rya[:, cols], wo_w[:, 0], start=True, stop=False)
                        mm = pe.matmul(dst, ryb[half:half + CB, cols], wo_w[half:half + CB, 1], start=False, stop=True)
                mm.then_inc(attn_done, 1)

            def squared_in(n, m):
                nw = width(n)
                pe.wait_ge(z2_ready, n + 1)
                turn(n, z2_turned)
                pe.wait_ge(lo2_ready, n + 1)
                for g in range(G):
                    if g < 2:
                        if m is not None:
                            pe.wait_ge(gelu_ready, m * G + G)
                    else:
                        pe.wait_ge(kf_relu, n * G + g - 1)
                    group(bank[4 + g % 2][:, 0:nw], kf_w, slice(g * P, (g + 1) * P), slice(0, nw)).then_inc(kf_done, 1)

            def gated_out(n):
                nt, t0 = tiles_of(n), tile0(n)
                pe.wait_ge(kf_ready, n * G + G)
                for q in range(nt):
                    cols = slice(q * P, (q + 1) * P)
                    if not (isinstance(n, int) and n == 0):
                        pe.wait_ge(gated, two_before(t0 + q))
                    ps = bank[2 + q % 2]
                    for g in range(G):
                        pe.matmul(ps[:, 0:C], kf[:, g, cols], vf_w[:, g], start=g == 0, stop=g == G - 1)
                    dst = ps[:, 256:256 + C]
                    for i, (zz, ww) in enumerate(((za[:, 0], rf_w[:, 0]), (za[:, 1], rf_w[:, 0]), (za[:, 0], rf_w[:, 1]),
                                                  (zb[:], rf_w[:, 2]), (zb[:], rf_w[:, 3]))):
                        pe.matmul(dst, zz[:, cols], ww, start=i == 0, stop=False)
                    pe.matmul(dst, id16[:], rf_bias[:, 0], start=False, stop=False)
                    pe.matmul(dst, id16[:], rf_bias[:, 1], start=False, stop=True).then_inc(gate_done, 1)

            def up(m):
                nw, nt = width(m), tiles_of(m)
                ps = bank[1][:].bitcast(BF16).rearrange("p (a n) -> p a n", a=2)
                pe.wait_ge(xq_ready, m + 1)
                if not (isinstance(m, int) and m == 0):
                    pe.wait_ge(y2_ready, tile0(m))
                for q in range(nt):
                    cols = slice(q * P, (q + 1) * P)
                    for a in range(2):
                        mm = pe.transpose(ps[:, a, cols], xq[:, q, a], idb[:])
                mm.then_inc(xq_turned, 1)
                pe.wait_ge(xqt_ready, m + 1)
                for g in range(G):
                    if g < 2:
                        pe.wait_ge(kf_relu, m * G + G)
                    else:
                        pe.wait_ge(gelu_ready, m * G + g - 1)
                    cols = slice(g * P, (g + 1) * P)
                    pe.matmul(bank[4 + g % 2][:, 0:nw], q1_w[:, 0, cols], xqt[:, 0, 0:nw], start=True, stop=False)
                    pe.matmul(bank[4 + g % 2][:, 0:nw], q1_w[0:CB, 1, cols], xqt[0:CB, 1, 0:nw], start=False, stop=True).then_inc(up_done, 1)

            def down(m):
                nt, t0 = tiles_of(m), tile0(m)
                pe.wait_ge(hq_ready, m * (G // 2) + G // 2)
                for q in range(nt):
                    cols = slice(q * P, (q + 1) * P)
                    if not (isinstance(m, int) and m == 0):
                        pe.wait_ge(y2_ready, two_before(t0 + q))
                    for g in range(G):
                        mm = pe.matmul(bank[q % 2][:, 0:C], hq[:, g, cols], q2_w[:, g], start=g == 0, stop=g == G - 1)
                    mm.then_inc(down_done, 1)

            def main(n, half, m):
                attention_out(n, half)
                if m is not None:
                    up(m)
                squared_in(n, m)
                if m is not None:
                    down(m)
                gated_out(n)

            main(0, None, None)
            main(1, 0, 0)
            with pe.Fori(0, PAIRS - 1) as p:
                main(p * 2 + 2, CB, p * 2 + 1)
                main(p * 2 + 3, 0, p * 2 + 2)
            main(B, CB, B - 1)
            up(B)
            down(B)


def kernel(**inputs):
    import numpy as np
    import concourse.bacc as bacc
    from concourse.bass_utils import run_bass_kernel_spmd

    a = {n: np.asarray(x) for n, x in inputs.items()}
    at = {n[len("L0_attn_"):]: x for n, x in a.items() if n.startswith("L0_attn_")}

    xt = a["x"].reshape(PAIRS, 2, 3, 4, 16, 4, 16).transpose(4, 6, 2, 1, 0, 3, 5).reshape(2, P, 3, PATCHES).transpose(1, 0, 2, 3)
    k = np.arange(16.0)
    dct = 2.0 * np.cos(np.pi * (2.0 * k + 1.0) * k[:, None] / 32.0)
    kron = np.kron(dct, dct).T.astype(np.float32).reshape(2, P, 256).transpose(1, 0, 2)
    tok_w = a["L0_tok_W"].T.reshape(6, P, C).transpose(1, 0, 2)

    def rows2(w):
        return np.stack([w[0:CA], np.concatenate([w[CA:C], w[CA:C]])], axis=1)

    kvr = [at["Wk_a"], at["Wv_a"], at["Wr_a"]]
    attn_w = rows2(np.concatenate([w[0:CA].T for w in kvr] + [w[CA:C].T for w in kvr], axis=1))
    vectors = [at[n] for n in ("ln1_w", "ln1_b", "ln2_w", "ln2_b", "decay", "first")]
    cols = np.concatenate([rows2(v[:, None])[:, :, 0] for v in vectors]
                          + [a["L0_ffn_alpha_w1"].reshape(G, P).T, a["L0_ffn_b1"].reshape(G, P).T], axis=1)
    rows = np.concatenate([a["L0_ffn_" + n] for n in ROWS])[None]
    arrays = {
        "txt": a["txt"], "xt": xt, "kron": kron, "tok_w": tok_w, "ident": np.eye(P, dtype=np.float32),
        "cols": cols, "rows": rows, "attn_w": attn_w,
        "kf_src": rows2(at["Wk_f"].T), "rf_src": rows2(at["Wr_f"].T), "wo_src": rows2(at["Wo_a"].T),
        "vf_src": at["Wv_f"].T.reshape(G, P, C).transpose(1, 0, 2),
        "w1": rows2(a["L0_ffn_w1"].T), "w2": a["L0_ffn_w2"].T.reshape(G, P, C).transpose(1, 0, 2),
    }
    arrays = {n: np.ascontiguousarray(x) for n, x in arrays.items()}
    nc = bacc.Bacc("TRN2", target_bir_lowering=False, num_devices=1)
    args = {n: nc.dram_tensor(n, x.shape, mybir.dt.from_np(x.dtype), kind="ExternalInput").ap() for n, x in arrays.items()}
    out = nc.dram_tensor("out", (B, T, C), F32, kind="ExternalOutput").ap()
    fusion_kernel(nc, **args, out=out)
    return run_bass_kernel_spmd(nc, [arrays], core_ids=[0]).results[0]["out"]
```

```python
from contextlib import ExitStack

import concourse.bass as bass
from concourse import mybir

F32 = mybir.dt.float32
F16 = mybir.dt.float16
BF16 = mybir.dt.bfloat16
ALU = mybir.AluOpType
ACT = mybir.ActivationFunctionType
AX_X = mybir.AxisListType.X

P = 128
B, TXT, C, HID = 8, 512, 192, 768
IMG = 16
T = IMG + TXT
CA, CB = 128, C - 128
PAIRS = B // 2
SLOTS = B + PAIRS
QT = TXT // P
TILES = 1 + B * QT
G = HID // P
EPS = 1e-5
WSCALE = 256.0
MAGIC = 1.5 * 2.0 ** 23
QN, QP = -8.0, 7.0
POOL_SQUARES = (2, 5)
CLIP = 10.0
NEG = -1e38
KVR = 3 * C
GB = 3 * CA
PATCHES = P


COLS = {name: i for i, name in enumerate(
    ["ln1_w", "ln1_wb", "ln1_b", "ln1_bb", "ln2_w", "ln2_wb", "ln2_b", "ln2_bb", "decay", "decay_b", "first", "first_b"])}
NCOL = len(COLS) + 2 * G
ROWS = {"alpha_w1": (0, HID), "alpha_a2": (HID, HID), "alpha_a1": (2 * HID, C),
        "alpha_w2": (2 * HID + C, C), "b2": (2 * HID + 2 * C, C)}
NROW = 2 * HID + 3 * C


def fusion_kernel(nc, txt, xt, kron, tok_w, ident, cols, rows, attn_w, kf_src, rf_src, wo_src, vf_src, w1, w2, out):
    with ExitStack() as ctx:
        def sb(name, shape, dt=F32):
            return ctx.enter_context(nc.sbuf_tensor(name, shape, dt))

        def sem(name):
            return ctx.enter_context(nc.semaphore(name))

        hid = sb("hid", [P, TILES, C])
        x1 = sb("x1", [P, TILES, C])
        k_all = sb("k_all", [P, SLOTS, T])
        v_all = sb("v_all", [P, SLOTS, T])
        r_all = sb("r_all", [P, SLOTS, T])

        id32 = sb("id32", [P, P])
        id16 = sb("id16", [P, P], F16)
        idb = sb("idb", [P, P], BF16)
        kvr_w = sb("kvr_w", [P, 4, KVR], F16)
        kf_w = sb("kf_w", [P, 4, HID], F16)
        rf_w = sb("rf_w", [P, 4, C], F16)
        rf_bias = sb("rf_bias", [P, 2, C], F16)
        vf_w = sb("vf_w", [P, G, C])
        wo_w = sb("wo_w", [P, 2, C])
        q1_w = sb("q1_w", [P, 2, HID], BF16)
        q2_w = sb("q2_w", [P, G, C], BF16)
        col = sb("col", [P, NCOL])
        lnw = sb("lnw", [P, 4])
        rate = sb("rate", [P, 2, SLOTS])
        bias = sb("bias", [P, 16])
        aw1c = col[:, len(COLS):len(COLS) + G]
        b1s = col[:, len(COLS) + G:NCOL]
        scale1 = sb("scale1", [P, G])
        scale2 = sb("scale2", [P, C])
        b2s = sb("b2s", [P, C])
        aq = sb("aq", [P, 8])
        minus_half = sb("minus_half", [P, 2 * QT])

        st = sb("st", [P, 2, QT, 6])
        mv2 = sb("mv2", [P, 2, QT, 2])
        rs2 = sb("rs2", [P, 2, 2, QT])
        z = sb("z", [P, QT, 2, P])
        za = sb("za", [P, 2, TXT], F16)
        zb = sb("zb", [P, TXT], F16)

        ARENA = 12688
        arena = sb("arena", [P, ARENA])

        class Carve:
            def __init__(self):
                self.at = 0

            def __call__(self, n):
                self.at += n
                assert self.at <= ARENA
                return arena[:, self.at - n:self.at]

        carve = Carve()
        xt_sb = carve(2 * 3 * PATCHES).rearrange("p (a n) -> p a n", a=2)
        kron_sb = carve(2 * 256).rearrange("p (a n) -> p a n", a=2)
        tokw_sb = carve(6 * C).rearrange("p (a n) -> p a n", a=6)
        yt = carve(2 * 3 * PATCHES).rearrange("p (a c n) -> p a c n", a=2, c=3)
        wa_raw = carve(2 * KVR).rearrange("p (a n) -> p a n", a=2)
        kf_raw = carve(2 * HID).rearrange("p (a n) -> p a n", a=2)
        rf_raw = carve(2 * C).rearrange("p (a n) -> p a n", a=2)
        wtmp = z[:].rearrange("p q a n -> p (q a n)")[:, 0:HID]
        w1_raw = carve(2 * HID).rearrange("p (a n) -> p a n", a=2)
        w2_raw = carve(G * C).rearrange("p (a n) -> p a n", a=G)
        row = carve(NROW)
        aw1_row, a2_row, a1_row, aw2, b2_row = (row[:, a:a + n] for a, n in ROWS.values())
        inv_row = carve(HID)
        inv2_row = carve(C)

        carve = Carve()
        W2 = 2 * (T + 1)
        env = [carve(W2) for _ in range(2)]
        sa = carve(W2)
        sbk = carve(W2)
        decay = [carve(2 * T) for _ in range(2)]
        gain = [carve(2 * T) for _ in range(2)]
        peak = [carve(T) for _ in range(2)]
        mix = [carve(3 * T) for _ in range(2)]
        gain_v = kvr_w[:].rearrange("p a n -> p (a n)").bitcast(F32)[:, 0:2 * T]

        carve = Carve()
        kf = carve(G * TXT).rearrange("p (g n) -> p g n", g=G)
        ge = carve(G * TXT).rearrange("p (g n) -> p g n", g=G)
        hq = carve(G * TXT // 2).bitcast(BF16).rearrange("p (g n) -> p g n", g=G)
        rya = carve(TXT)
        ryb = carve(TXT)
        th = carve(2 * C).rearrange("p (a n) -> p a n", a=2)
        gv = carve(2 * C).rearrange("p (a n) -> p a n", a=2)
        xs = carve(QT * C).rearrange("p (q n) -> p q n", q=QT)
        xq = carve(QT * P).bitcast(BF16).rearrange("p (q a n) -> p q a n", q=QT, a=2)
        xqt = carve(TXT).bitcast(BF16).rearrange("p (a n) -> p a n", a=2)
        y2 = carve(QT * C).rearrange("p (q n) -> p q n", q=QT)

        bank = [ctx.enter_context(nc.psum_tensor(f"bank{i}", [P, 512], F32)) for i in range(8)]

        tok_loaded, attn_loaded, mlp_loaded, ffn_loaded = (sem(n) for n in ("tok_loaded", "attn_loaded", "mlp_loaded", "ffn_loaded"))
        text_even_loaded, text_odd_loaded = sem("text_even_loaded"), sem("text_odd_loaded")
        setup_dve, setup_pool, constants_ready = sem("setup_dve"), sem("setup_pool"), sem("constants_ready")
        dct_done, dct_copied, img_done, img_copied = (sem(n) for n in ("dct_done", "dct_copied", "img_done", "img_copied"))
        bias_done, bias_copied = sem("bias_done"), sem("bias_copied")
        stat_step, stats_ready, power_step, powers_ready, z_ready, z_turned = (
            sem(n) for n in ("stat_step", "stats_ready", "power_step", "powers_ready", "z_ready", "z_turned"))
        hi_ready, lo_ready = sem("hi_ready"), sem("lo_ready")
        ka_done, va_done, ra_done, kb_done, vb_done, projected = (
            sem(n) for n in ("ka_done", "va_done", "ra_done", "kb_done", "vb_done", "projected"))
        k_stored, v_stored, r_stored = sem("k_stored"), sem("v_stored"), sem("r_stored")
        k_copied, env_ready, peak_step, peak_ready = sem("k_copied"), sem("env_ready"), sem("peak_step"), sem("peak_ready")
        decay_arg, gain_arg, mix_arg = sem("decay_arg"), sem("gain_arg"), sem("mix_arg")
        decay_exp, gain_exp, mix_exp = sem("decay_exp"), sem("gain_exp"), sem("mix_exp")
        gain_v_ready, sums_b_ready, sums_a_ready = sem("gain_v_ready"), sem("sums_b_ready"), sem("sums_a_ready")
        den_parts, num_parts, own_num, comb_step, y_ready = (sem(n) for n in ("den_parts", "num_parts", "own_num", "comb_step", "y_ready"))
        ry_ready, attn_done, x2_ready, hx_ready = (sem(n) for n in ("ry_ready", "attn_done", "x2_ready", "hx_ready"))
        z2_ready, z2_turned, hi2_ready, lo2_ready = (sem(n) for n in ("z2_ready", "z2_turned", "hi2_ready", "lo2_ready"))
        stat2_step, stats2_ready, power2_step, powers2_ready = (sem(n) for n in ("stat2_step", "stats2_ready", "power2_step", "powers2_ready"))
        kf_done, kf_relu, kf_ready, gate_done, gate_tanh, gated, h3_ready = (
            sem(n) for n in ("kf_done", "kf_relu", "kf_ready", "gate_done", "gate_tanh", "gated", "h3_ready"))
        stat3_step, stats3_ready, power3_step, powers3_ready, xs_ready, xs_clipped, xq_ready = (
            sem(n) for n in ("stat3_step", "stats3_ready", "power3_step", "powers3_ready", "xs_ready", "xs_clipped", "xq_ready"))
        xq_turned, xqt_ready, up_done, gelu_ready, ge_scaled, ge_rounded, hq_ready = (
            sem(n) for n in ("xq_turned", "xqt_ready", "up_done", "gelu_ready", "ge_scaled", "ge_rounded", "hq_ready"))
        held = sem("held")
        h3b_ready, down_done, y2_ready, out_ready, stored = (
            sem(n) for n in ("h3b_ready", "down_done", "y2_ready", "out_ready", "stored"))

        class Step:

            def __init__(self, n, b, pair=None, odd=0, tiles_before=None):
                self.n, self.b, self.pair, self.half = n, b, pair, CB * odd
                self.image = b is None
                self.nt = 1 if self.image else QT
                self.nw = P * self.nt
                self.tile = TILES - 1 if self.image else b * QT
                self.first = isinstance(n, int) and n == 0
                self.before = self.tile if tiles_before is None else tiles_before

        def projection(b, pair=None, odd=0):
            return Step(0, None, tiles_before=0) if b is None else Step(b + 1, b, pair, odd, b * QT + 1)

        def mlp(b, pair=None, odd=0):
            return Step(B, None) if b is None else Step(b, b, pair, odd)

        def tile(a, t):
            return a[:, bass.ds(t, 1), :].rearrange("p a c -> p (a c)")

        def slot(a, j):
            return a[:, bass.ds(j, 1), :].rearrange("p a t -> p (a t)")

        def excl(buf):
            return _two(buf, 0, T + 2)

        def incl(buf):
            return _two(buf, 1, T)

        def _two(buf, at, step):
            return bass.AP(buf.tensor, buf.offset + at, [list(buf.ap[0]), [step, 2], [1, T]])

        def vec(name):
            return col[:, COLS[name]:COLS[name] + 1]

        def at_least(eng, semaphore, value):
            if not isinstance(value, int) or value > 0:
                eng.wait_ge(semaphore, value)

        def twice(ap):
            return bass.AP(ap.tensor, ap.offset, [list(ap.ap[0]), [0, 2], list(ap.ap[1])])

        def halves(ap, n=T):
            return ap.rearrange("p (a n) -> p a n", n=n)

        def img_slots(a):
            return a[:, 0:B, 0:IMG].rearrange("p (g a) t -> p a g t", a=2)

        def img_cols(ps):
            return ps.rearrange("p (a g t) -> p a g t", a=2, g=PAIRS)

        def img_b(a):
            return a[:, B:SLOTS, 0:IMG]

        def hold(eng, semaphore, value):
            eng.wait_ge(semaphore, value)
            if not isinstance(value, int):
                eng.sem_inc(held, 1)

        def schedule(eng, round_of):
            round_of(None, None, mlp(0, 0, 0))
            round_of(mlp(0, 0, 0), None, mlp(1, 0, 1))
            round_of(mlp(1, 0, 1), mlp(0, 0, 0), mlp(2, 1, 0))
            with eng.Fori(1, PAIRS - 1) as p:
                round_of(mlp(p * 2, p, 0), mlp(p * 2 - 1, p - 1, 1), mlp(p * 2 + 1, p, 1))
                round_of(mlp(p * 2 + 1, p, 1), mlp(p * 2, p, 0), mlp(p * 2 + 2, p + 1, 0))
            last = PAIRS - 1
            round_of(mlp(B - 2, last, 0), mlp(B - 3, last - 1, 1), mlp(B - 1, last, 1))
            round_of(mlp(B - 1, last, 1), mlp(B - 2, last, 0), mlp(None))
            round_of(mlp(None), mlp(B - 1, last, 1), None)
            round_of(None, mlp(None), None)

        block = ctx.enter_context(nc.Block())

        @block.sync
        def _(sp):
            for dst, src in ((xt_sb, xt), (kron_sb, kron), (tokw_sb, tok_w), (id32[:], ident)):
                sp.dma_start(dst, src).then_inc(tok_loaded, 16)
            with sp.Fori(0, PAIRS) as p:
                for parity, loaded in ((0, text_even_loaded), (1, text_odd_loaded)):
                    b = p * 2 + parity
                    sp.dma_start(hid[:, bass.ds(b * QT, QT), :],
                                 txt[bass.ds(b, 1)].rearrange("a (q p) c -> p (a q) c", p=P)).then_inc(loaded, 16)
                    hold(sp, loaded, p * 16 + 16)
            with sp.Fori(0, B) as b:
                hold(sp, out_ready, b * QT + QT)
                sp.dma_start(out[bass.ds(b, 1), IMG:T, :].rearrange("a (q p) c -> p (a q) c", p=P),
                             hid[:, bass.ds(b * QT, QT), :]).then_inc(stored, 16)
            sp.wait_ge(out_ready, TILES)
            for parity in range(2):
                for g in range(PAIRS):
                    at = 64 * parity + IMG * g
                    sp.dma_start(out[2 * g + parity, 0:IMG, :], hid[at:at + IMG, TILES - 1, :]).then_inc(stored, 16)
            sp.wait_ge(stored, 16 * (B + B))

        @block.gpsimd
        def _(pool):
            nc.gpsimd.memset(minus_half[:], -0.5).then_inc(setup_pool, 1)
            pool.wait_ge(setup_pool, 1)

            def powers(n, par):
                nt = 1 if isinstance(n, int) and n == 0 else QT
                var, rs = mv2[:, par, 0:nt, 1], rs2[:, par]
                hold(pool, stats_ready, n + 1)
                nc.gpsimd.tensor_scalar(rs[:, 0, 0:nt], var, EPS, None, ALU.add).then_inc(power_step, 1)
                nc.gpsimd.tensor_scalar(rs[:, 1, 0:nt], var, 1.0 + EPS, EPS * EPS, ALU.mult, ALU.add).then_inc(power_step, 1)
                pool.wait_ge(power_step, 2 * n + 2)
                nc.gpsimd.tensor_tensor(rs[:, :, 0:nt], rs[:, :, 0:nt],
                                        minus_half[:].rearrange("p (a n) -> p a n", a=2)[:, :, 0:nt], ALU.pow).then_inc(powers_ready, 1)

            powers(0, 0)
            with pool.Fori(0, PAIRS) as p:
                powers(p * 2 + 1, 1)
                powers(p * 2 + 2, 0)

            def arguments(j, par):
                pool.wait_ge(env_ready, j + 1)
                k_t = slot(k_all, j)
                nc.gpsimd.tensor_tensor(halves(decay[par]), excl(env[par]), incl(env[par]), ALU.subtract).then_inc(decay_arg, 1)
                nc.gpsimd.tensor_tensor(halves(gain[par]), twice(k_t), incl(env[par]), ALU.subtract).then_inc(gain_arg, 1)
                pool.wait_ge(peak_ready, j + 1)
                nc.gpsimd.tensor_tensor(halves(mix[par])[:, 0:2], excl(env[par]), twice(peak[par]), ALU.subtract).then_inc(mix_arg, 1)

            def products(j, par):
                pool.wait_ge(mix_exp, j + 1)
                m = halves(mix[par])
                pool.wait_ge(sums_b_ready, j + 1)
                nc.gpsimd.tensor_tensor(excl(sbk), m[:, 0:2], excl(sbk), ALU.mult).then_inc(den_parts, 1)
                nc.gpsimd.tensor_tensor(peak[par], m[:, 2], slot(v_all, j), ALU.mult).then_inc(own_num, 1)

            pool.wait_ge(k_stored, 2 + B + PAIRS)
            pool.wait_ge(v_stored, 2 + B + PAIRS)
            arguments(0, 0)
            with pool.Fori(0, SLOTS // 2 - 1) as i:
                arguments(i * 2 + 1, 1)
                products(i * 2, 0)
                arguments(i * 2 + 2, 0)
                products(i * 2 + 1, 1)
            arguments(SLOTS - 1, 1)
            products(SLOTS - 2, 0)
            products(SLOTS - 1, 1)

            def powers2(s):
                hold(pool, stats2_ready, s.n + 1)
                rs = rs2[:, 0, 0, 0:s.nt]
                nc.gpsimd.tensor_scalar(rs, mv2[:, 0, 0:s.nt, 1], EPS, None, ALU.add).then_inc(power2_step, 1)
                pool.wait_ge(power2_step, s.n + 1)
                nc.gpsimd.tensor_tensor(rs, rs, minus_half[:, 0:s.nt], ALU.pow).then_inc(powers2_ready, 1)
                for q in range(s.nt):
                    nc.gpsimd.tensor_tensor(tile(hid, s.tile + q), tile(hid, s.tile + q), tile(x1, s.tile + q), ALU.add).then_inc(hx_ready, 1)

            def powers3(s):
                rs = rs2[:, 1, 0, 0:s.nt]
                hold(pool, stats3_ready, s.n + 1)
                nc.gpsimd.tensor_scalar(rs, mv2[:, 1, 0:s.nt, 1], EPS, None, ALU.add).then_inc(power3_step, 1)
                pool.wait_ge(power3_step, s.n * 2 + 1)
                nc.gpsimd.tensor_tensor(rs, rs, minus_half[:, 0:s.nt], ALU.pow).then_inc(power3_step, 1)
                hold(pool, power3_step, s.n * 2 + 2)
                nc.gpsimd.tensor_scalar(rs, rs, aq[:, 1:2], None, ALU.mult).then_inc(powers3_ready, 1)
                hold(pool, xs_ready, s.before + s.nt)
                for q in range(s.nt):
                    nc.gpsimd.tensor_tensor(tile(hid, s.tile + q), tile(hid, s.tile + q), b2s[:], ALU.add).then_inc(h3b_ready, 1)

            def finish(s):
                for q in range(s.nt):
                    pool.wait_ge(y2_ready, s.before + q + 1)
                    hold(pool, h3b_ready, s.before + q + 1)
                    nc.gpsimd.tensor_tensor(tile(hid, s.tile + q), tile(hid, s.tile + q), y2[:, q], ALU.add).then_inc(out_ready, 1)

            def square(s, g):
                pool.wait_ge(kf_relu, s.n * G + g + 1)
                nc.gpsimd.tensor_tensor(kf[:, g, 0:s.nw], kf[:, g, 0:s.nw], kf[:, g, 0:s.nw], ALU.mult).then_inc(kf_ready, 1)

            def round_of(now, last, then):
                if last:
                    powers3(last)
                if now:
                    for g in POOL_SQUARES:
                        square(now, g)
                if then:
                    powers2(then)
                if last:
                    finish(last)

            pool.wait_ge(constants_ready, 1)
            schedule(pool, round_of)

        @block.vector
        def _(dve):
            count = [0]

            def did(ins):
                count[0] += 1
                ins.then_inc(setup_dve, 1)

            def settled():
                dve.wait_ge(setup_dve, count[0])

            V = nc.vector
            dve.wait_ge(tok_loaded, 64)
            did(V.tensor_copy(id16[:], id32[:]))
            did(V.tensor_copy(idb[:], id32[:]))

            def split(raw, lw, dst, n):
                did(V.tensor_scalar(wtmp[:, 0:n], raw, lw, None, ALU.mult))
                settled()
                did(V.tensor_copy(dst[:, 0], wtmp[:, 0:n]))
                settled()
                did(V.tensor_tensor(dst[:, 1], wtmp[:, 0:n], dst[:, 0], ALU.subtract))
                settled()

            dve.wait_ge(attn_loaded, 16 * 2)
            for j, name in enumerate(("ln1_w", "ln1_wb", "ln2_w", "ln2_wb")):
                did(V.tensor_scalar(lnw[:, j:j + 1], vec(name), WSCALE, None, ALU.mult))
            settled()
            for h in range(2):
                split(wa_raw[:, h], lnw[:, h:h + 1], kvr_w[:, 2 * h:2 * h + 2], KVR)
            for h in range(2):
                dve.wait_ge(dct_done, h + 1)
                V.tensor_copy(yt[:, h].rearrange("p c n -> p (c n)"), bank[h][:, 0:3 * PATCHES]).then_inc(dct_copied, 1)
            dve.wait_ge(img_done, 1)
            V.tensor_copy(hid[:, TILES - 1], bank[2][:, 0:C]).then_inc(img_copied, 1)

            dve.wait_ge(mlp_loaded, 16 * 4)
            for h in range(2):
                split(kf_raw[:, h], lnw[:, 2 + h:3 + h], kf_w[:, 2 * h:2 * h + 2], HID)
                split(rf_raw[:, h], lnw[:, 2 + h:3 + h], rf_w[:, 2 * h:2 * h + 2], C)
            dve.wait_ge(bias_done, 1)
            V.tensor_copy(bias[:, 0:12], bank[3][:, 0:12]).then_inc(bias_copied, 1)
            dve.wait_ge(bias_copied, 1)
            did(V.tensor_scalar(bias[:, 12:13], bias[:, 2:3], 0.5, None, ALU.mult))
            did(V.tensor_scalar(bias[:, 13:14], bias[:, 5:6], 0.5, None, ALU.mult))
            did(V.tensor_scalar(wtmp[:, 0:C], bank[4][:, 0:C], WSCALE, None, ALU.mult))
            settled()
            did(V.tensor_copy(rf_bias[:, 0], wtmp[:, 0:C]))
            settled()
            did(V.tensor_tensor(rf_bias[:, 1], wtmp[:, 0:C], rf_bias[:, 0], ALU.subtract))
            for which, name in enumerate(("decay", "first")):
                for at, n, tail_ in ((0, B, ""), (B, PAIRS, "_b")):
                    did(V.tensor_scalar(rate[:, which, at:at + n], vec(name + tail_).to_broadcast([P, n]), 1.0 / T, None, ALU.mult))

            dve.wait_ge(ffn_loaded, 16 * 3)
            did(V.reciprocal(inv_row, aw1_row))
            did(V.reciprocal(inv2_row, aw2))
            settled()

            def quantize(dst, raw, inv):
                did(V.tensor_tensor(raw, raw, inv, ALU.mult))
                settled()
                did(V.tensor_scalar(raw, raw, QP, QN, ALU.min, ALU.max))
                settled()
                did(V.tensor_scalar(dst, raw, MAGIC, MAGIC, ALU.add, ALU.subtract))

            for h in range(2):
                quantize(q1_w[:, h], w1_raw[:, h], inv_row)
            quantize(q2_w[:], w2_raw, bass.AP(inv2_row.tensor, inv2_row.offset, [list(inv2_row.ap[0]), [0, G], [1, C]]))
            did(V.reduce_sum(aq[:, 0:1], a1_row, AX_X))
            did(V.reduce_sum(aq[:, 2:3], a2_row, AX_X))
            settled()
            did(V.tensor_scalar(aq[:, 0:1], aq[:, 0:1], 1.0 / C, None, ALU.mult))
            did(V.tensor_scalar(aq[:, 2:3], aq[:, 2:3], 1.0 / HID, None, ALU.mult))
            settled()
            did(V.reciprocal(aq[:, 1:2], aq[:, 0:1]))
            did(V.reciprocal(aq[:, 3:4], aq[:, 2:3]))
            did(V.tensor_copy(b2s[:], b2_row))
            did(V.tensor_scalar(scale1[:], aw1c, aq[:, 0:1], None, ALU.mult))
            did(V.tensor_scalar(scale2[:], aw2, aq[:, 2:3], None, ALU.mult))
            settled()
            did(V.tensor_scalar(aq[:, 7:8], aq[:, 3:4], CLIP, None, ALU.mult))
            settled()
            did(V.scalar_tensor_tensor(aq[:, 6:7], aq[:, 3:4], -CLIP, aq[:, 7:8], ALU.mult, ALU.max))
            settled()
            did(V.tensor_scalar(aq[:, 4:5], aq[:, 6:7], QP, None, ALU.min))
            settled()
            V.tensor_scalar(aq[:, 5:6], aq[:, 6:7], -1.0, QN, ALU.mult, ALU.max).then_inc(constants_ready, 1)
            dve.wait_ge(constants_ready, 1)

            def statistics(s, par, step, ready, data):
                for q in range(s.nt):
                    V.bn_stats(st[:, par, q], tile(data, s.tile + q)).then_inc(step, 1)
                hold(dve, step, s.before + s.nt)
                for q in range(s.nt):
                    ins = V.bn_aggr(mv2[:, par, q], st[:, par, q])
                ins.then_inc(ready, 1)

            def write_z(src, s, par, which):
                for q in range(s.nt):
                    x = tile(src, s.tile + q)
                    V.tensor_scalar(z[:, q, 0], x[:, 0:CA], mv2[:, par, q, 0:1], rs2[:, par, which, q:q + 1], ALU.subtract, ALU.mult)
                    ins = V.tensor_scalar(z[:, q, 1].rearrange("p (a c) -> p a c", a=2), twice(x[:, CA:C]),
                                          mv2[:, par, q, 0:1], rs2[:, par, which, q:q + 1], ALU.subtract, ALU.mult)
                return ins

            def low_half(s, hi, lo):
                dve.wait_ge(hi, s.n + 1)
                V.tensor_tensor(za[:, 1, 0:s.nw], bank[0][:, 0:s.nw], za[:, 0, 0:s.nw], ALU.subtract)
                V.tensor_tensor(zb[CB:P, 0:s.nw], bank[1][CB:P, 0:s.nw], zb[CB:P, 0:s.nw], ALU.subtract).then_inc(lo, 1)

            def project(s, par):
                if not s.first:
                    dve.wait_ge(z_turned, s.n)
                dve.wait_ge(powers_ready, s.n + 1)
                write_z(hid, s, par, 1).then_inc(z_ready, 1)
                for q in range(s.nt):
                    V.tensor_scalar(tile(x1, s.tile + q), tile(hid, s.tile + q), mv2[:, par, q, 0:1], rs2[:, par, 0, q:q + 1],
                                    ALU.subtract, ALU.mult)
                low_half(s, hi_ready, lo_ready)
                dve.wait_ge(va_done, s.n + 1)
                if s.image:
                    V.tensor_scalar(img_slots(v_all), img_cols(bank[3][:, 0:P]), 1 / WSCALE, bias[:, 1:2], ALU.mult, ALU.add).then_inc(v_stored, 1)
                    dve.wait_ge(vb_done, 1)
                    V.tensor_scalar(img_b(v_all), bank[6][:, 0:64].rearrange("p (g t) -> p g t", g=PAIRS),
                                    1 / WSCALE, bias[:, 4:5], ALU.mult, ALU.add).then_inc(v_stored, 1)
                else:
                    V.tensor_scalar(slot(v_all, s.b)[:, IMG:T], bank[3][:],
                                    1 / WSCALE, bias[:, 1:2], ALU.mult, ALU.add).then_inc(v_stored, 1)

            def project_b(p):
                dve.wait_ge(vb_done, p + 2)
                V.tensor_scalar(v_all[:, bass.ds(p + B, 1), IMG:T].rearrange("p a t -> p (a t)"), bank[6][:],
                                1 / WSCALE, bias[:, 4:5], ALU.mult, ALU.add).then_inc(v_stored, 1)

            def measure(s, par):
                statistics(s, par, stat_step, stats_ready, hid)

            def even_loaded(p):
                hold(dve, text_even_loaded, p * 16 + 16)

            def odd_loaded(p):
                hold(dve, text_odd_loaded, p * 16 + 16)

            dve.wait_ge(img_copied, 1)
            measure(projection(None), 0)
            even_loaded(0)
            measure(projection(0), 1)
            project(projection(None), 0)
            with dve.Fori(0, PAIRS - 1) as p:
                odd_loaded(p)
                measure(projection(p * 2 + 1), 0)
                project(projection(p * 2), 1)
                even_loaded(p + 1)
                measure(projection(p * 2 + 2), 1)
                project(projection(p * 2 + 1), 0)
                project_b(p)
            odd_loaded(PAIRS - 1)
            measure(projection(B - 1), 0)
            project(projection(B - 2), 1)
            project(projection(B - 1), 0)
            project_b(PAIRS - 1)

            F0, B0 = 1, T + 1
            dve.wait_ge(projected, 1 + B)
            for buf, val in ((env[0], NEG), (env[1], NEG), (sa, 0.0), (sbk, 0.0)):
                V.memset(buf[:, 0:1], val).then_inc(comb_step, 1)
                V.memset(buf[:, 2 * T + 1:2 * T + 2], val).then_inc(comb_step, 1)
            INIT = 8
            dve.wait_ge(comb_step, INIT)
            dve.wait_ge(k_stored, 2 + B + PAIRS)

            def envelopes(j, par):
                w = rate[:, 0, bass.ds(j, 1)]
                k_t = slot(k_all, j)
                wb = w.to_broadcast([P, T])
                V.tensor_tensor_scan(env[par][:, F0:F0 + T], wb, k_t, NEG, ALU.add, ALU.max)
                dve.wait_ge(k_copied, j + 1)
                V.tensor_tensor_scan(env[par][:, B0:B0 + T][:, ::-1], wb, gain[par][:, T:2 * T][:, ::-1], NEG, ALU.add, ALU.max).then_inc(env_ready, 1)
                dve.wait_ge(env_ready, j + 1)
                V.tensor_tensor(peak[par], env[par][:, 0:T], env[par][:, T + 2:2 * T + 2], ALU.max).then_inc(peak_step, 1)
                dve.wait_ge(peak_step, j * 2 + 1)
                u = rate[:, 1, bass.ds(j, 1)]
                V.scalar_tensor_tensor(peak[par], k_t, u, peak[par], ALU.add, ALU.max).then_inc(peak_step, 1)
                dve.wait_ge(peak_step, j * 2 + 2)
                V.scalar_tensor_tensor(halves(mix[par])[:, 2], k_t, u, peak[par], ALU.add, ALU.subtract).then_inc(peak_ready, 1)

            def combine(j, par):
                v_t = slot(v_all, j)
                dve.wait_ge(gain_exp, j + 1)
                V.tensor_tensor(halves(gain_v), halves(gain[par]), twice(v_t), ALU.mult).then_inc(gain_v_ready, 1)
                dve.wait_ge(decay_exp, j + 1)
                d, g = halves(decay[par]), halves(gain[par])
                V.tensor_tensor_scan(sbk[:, F0:F0 + T], d[:, 0], g[:, 0], 0.0, ALU.mult, ALU.add)
                V.tensor_tensor_scan(sbk[:, B0:B0 + T][:, ::-1], d[:, 1][:, ::-1], g[:, 1][:, ::-1], 0.0, ALU.mult, ALU.add).then_inc(sums_b_ready, 1)
                dve.wait_ge(gain_v_ready, j + 1)
                gv2 = halves(gain_v)
                V.tensor_tensor_scan(sa[:, F0:F0 + T], d[:, 0], gv2[:, 0], 0.0, ALU.mult, ALU.add)
                V.tensor_tensor_scan(sa[:, B0:B0 + T][:, ::-1], d[:, 1][:, ::-1], gv2[:, 1][:, ::-1], 0.0, ALU.mult, ALU.add).then_inc(sums_a_ready, 1)
                dve.wait_ge(sums_a_ready, j + 1)
                dve.wait_ge(mix_exp, j + 1)
                V.tensor_tensor(excl(sa), halves(mix[par])[:, 0:2], excl(sa), ALU.mult).then_inc(num_parts, 1)
                dve.wait_ge(num_parts, j + 1)
                num, nb = sa[:, 0:T], sa[:, T + 2:2 * T + 2]
                den, db = sbk[:, 0:T], sbk[:, T + 2:2 * T + 2]
                step = j * 6 + INIT
                V.tensor_tensor(num, num, nb, ALU.add).then_inc(comb_step, 1)
                dve.wait_ge(den_parts, j + 1)
                V.tensor_tensor(den, den, db, ALU.add).then_inc(comb_step, 1)
                dve.wait_ge(own_num, j + 1)
                dve.wait_ge(comb_step, step + 2)
                V.tensor_tensor(den, den, halves(mix[par])[:, 2], ALU.add).then_inc(comb_step, 1)
                V.tensor_tensor(num, num, peak[par], ALU.add).then_inc(comb_step, 1)
                dve.wait_ge(comb_step, step + 4)
                V.reciprocal(halves(decay[par])[:, 0], den).then_inc(comb_step, 1)
                dve.wait_ge(comb_step, step + 5)
                V.tensor_tensor(slot(k_all, j), num, halves(decay[par])[:, 0], ALU.mult).then_inc(y_ready, 1)
                dve.wait_ge(y_ready, j + 1)
                V.memset(sa[:, 0:1], 0.0)
                V.memset(sa[:, 2 * T + 1:2 * T + 2], 0.0)
                V.memset(sbk[:, 0:1], 0.0)
                V.memset(sbk[:, 2 * T + 1:2 * T + 2], 0.0).then_inc(comb_step, 1)

            envelopes(0, 0)
            with dve.Fori(0, SLOTS // 2 - 1) as i:
                envelopes(i * 2 + 1, 1)
                combine(i * 2, 0)
                envelopes(i * 2 + 2, 0)
                combine(i * 2 + 1, 1)
            envelopes(SLOTS - 1, 1)
            combine(SLOTS - 2, 0)
            combine(SLOTS - 1, 1)

            def gate_y(s):
                at_least(dve, attn_done, s.n)
                if s.image:
                    for a in range(2):
                        V.scalar_tensor_tensor(img_cols(rya[:, 0:P])[:, a], img_slots(r_all)[:, a], 1.0, img_slots(k_all)[:, a], ALU.add, ALU.mult)
                    V.scalar_tensor_tensor(ryb[:, 0:64].rearrange("p (g t) -> p g t", g=PAIRS), img_b(r_all), 1.0, img_b(k_all), ALU.add, ALU.mult).then_inc(ry_ready, 1)
                else:
                    rows, at = slice(s.half, s.half + CB), s.pair + B
                    V.scalar_tensor_tensor(rya, slot(r_all, s.b)[:, IMG:T], 1.0, slot(k_all, s.b)[:, IMG:T], ALU.add, ALU.mult)
                    V.scalar_tensor_tensor(ryb[rows], slot(r_all, at)[rows, IMG:T], 1.0, slot(k_all, at)[rows, IMG:T],
                                           ALU.add, ALU.mult).then_inc(ry_ready, 1)

            def residual2(s):
                dve.wait_ge(attn_done, s.n + 1)
                for q in range(s.nt):
                    V.scalar_tensor_tensor(tile(x1, s.tile + q), bank[6 + q // 2][:, (q % 2) * C:(q % 2 + 1) * C], 0.5,
                                           tile(x1, s.tile + q), ALU.mult, ALU.add).then_inc(x2_ready, 1)
                hold(dve, x2_ready, s.before + s.nt)
                statistics(s, 0, stat2_step, stats2_ready, x1)

            def normalize2(s):
                at_least(dve, z2_turned, s.n)
                dve.wait_ge(powers2_ready, s.n + 1)
                write_z(x1, s, 0, 0).then_inc(z2_ready, 1)

            def squares(s, groups):
                for g in groups:
                    dve.wait_ge(kf_relu, s.n * G + g + 1)
                    V.tensor_tensor(kf[:, g, 0:s.nw], kf[:, g, 0:s.nw], kf[:, g, 0:s.nw], ALU.mult).then_inc(kf_ready, 1)

            def gate(s, q):
                dve.wait_ge(gate_tanh, s.before + q + 1)
                V.scalar_tensor_tensor(gv[:, q % 2], th[:, q % 2], 1.0, bank[2 + q % 2][:, 0:C], ALU.add, ALU.mult).then_inc(gated, 1)

            def residual3(s, q):
                dve.wait_ge(gated, s.before + q + 1)
                dve.wait_ge(hx_ready, s.before + q + 1)
                V.scalar_tensor_tensor(tile(hid, s.tile + q), gv[:, q % 2], 0.5, tile(hid, s.tile + q), ALU.mult, ALU.add).then_inc(h3_ready, 1)

            def statistics3(s, q):
                hold(dve, h3_ready, s.before + q + 1)
                V.bn_stats(st[:, 1, q], tile(hid, s.tile + q)).then_inc(stat3_step, 1)
                if q == s.nt - 1:
                    hold(dve, stat3_step, s.before + s.nt)
                    for t in range(s.nt):
                        ins = V.bn_aggr(mv2[:, 1, t], st[:, 1, t])
                    ins.then_inc(stats3_ready, 1)

            def quantize_x(s):
                dve.wait_ge(powers3_ready, s.n + 1)
                for q in range(s.nt):
                    V.tensor_scalar(xs[:, q], tile(hid, s.tile + q), mv2[:, 1, q, 0:1], rs2[:, 1, 0, q:q + 1],
                                    ALU.subtract, ALU.mult).then_inc(xs_ready, 1)
                dve.wait_ge(xs_ready, s.before + s.nt)
                V.tensor_scalar(xs[:, 0:s.nt], xs[:, 0:s.nt], QP, QN, ALU.min, ALU.max).then_inc(xs_clipped, 1)
                dve.wait_ge(xs_clipped, s.n + 1)
                at_least(dve, xq_turned, s.n)
                V.tensor_scalar(xq[:, 0:s.nt, 0], xs[:, 0:s.nt, 0:CA], MAGIC, MAGIC, ALU.add, ALU.subtract)
                for twin in range(2):
                    ins = V.tensor_scalar(xq[:, 0:s.nt, 1, twin * CB:(twin + 1) * CB], xs[:, 0:s.nt, CA:C], MAGIC, MAGIC, ALU.add, ALU.subtract)
                ins.then_inc(xq_ready, 1)

            def turned(s):
                dve.wait_ge(xq_turned, s.n + 1)
                at_least(dve, up_done, s.n * G)
                V.tensor_copy(xqt[:, :, 0:s.nw], bank[1][:].bitcast(BF16).rearrange("p (a n) -> p a n", a=2)[:, :, 0:s.nw]).then_inc(xqt_ready, 1)

            def scale_hidden(s, pair):
                g = 2 * pair
                dve.wait_ge(gelu_ready, s.n * G + g + 2)
                V.tensor_scalar(ge[:, g:g + 2, 0:s.nw], ge[:, g:g + 2, 0:s.nw], aq[:, 3:4], aq[:, 4:5], ALU.mult, ALU.min).then_inc(ge_scaled, 1)

            def round_hidden(s, pair):
                g = 2 * pair
                dve.wait_ge(ge_scaled, s.n * (G // 2) + pair + 1)
                V.tensor_scalar(ge[:, g:g + 2, 0:s.nw], ge[:, g:g + 2, 0:s.nw], aq[:, 5:6], MAGIC, ALU.max, ALU.add).then_inc(ge_rounded, 1)

            def scaled_out(s):
                at_least(dve, out_ready, s.before)
                for q in range(s.nt):
                    dve.wait_ge(down_done, s.before + q + 1)
                    V.tensor_tensor(y2[:, q], bank[6 + q % 2][:, 0:C], scale2[:], ALU.mult).then_inc(y2_ready, 1)

            def round_of(now, last, then):
                mine = [g for g in range(G) if g not in POOL_SQUARES]
                if now:
                    low_half(now, hi2_ready, lo2_ready)
                if last:
                    quantize_x(last)
                if now:
                    squares(now, mine[:2])
                if then:
                    gate_y(then)
                if last:
                    turned(last)
                if now:
                    squares(now, mine[2:])
                if then:
                    residual2(then)
                if last:
                    scale_hidden(last, 0)
                    scale_hidden(last, 1)
                    round_hidden(last, 0)
                for q in range(QT):
                    if now and q < now.nt:
                        gate(now, q)
                    if last and q == 0:
                        round_hidden(last, 1)
                    if last and q == 1:
                        scale_hidden(last, 2)
                    if last and q == 2:
                        round_hidden(last, 2)
                    if now and 0 < q <= now.nt:
                        statistics3(now, q - 1)
                    if now and q < now.nt:
                        residual3(now, q)
                    if then and q == 1:
                        normalize2(then)
                if now and now.nt == QT:
                    statistics3(now, QT - 1)
                if last:
                    scaled_out(last)

            dve.wait_ge(y_ready, SLOTS)
            schedule(dve, round_of)

        @block.scalar
        def _(act):
            A = nc.scalar
            for dst, src in ((col[:], cols), (wa_raw, attn_w)):
                act.dma_start(dst, src).then_inc(attn_loaded, 16)
            for dst, src in ((kf_raw, kf_src), (rf_raw, rf_src), (wo_w[:], wo_src), (vf_w[:], vf_src)):
                act.dma_start(dst, src).then_inc(mlp_loaded, 16)
            for dst, src in ((row, rows.to_broadcast([P, NROW])), (w1_raw, w1), (w2_raw, w2)):
                act.dma_start(dst, src).then_inc(ffn_loaded, 16)

            def high_half(s, turned, hi, used):
                act.wait_ge(turned, s.n + 1)
                used()
                A.activation(za[:, 0, 0:s.nw], bank[0][:, 0:s.nw], ACT.Identity)
                A.activation(zb[:, 0:s.nw], bank[1][:, 0:s.nw], ACT.Identity).then_inc(hi, 1)

            def store(dst, src, func, column, semaphore):
                scale = 1 / WSCALE if func == ACT.Identity else 0.5 / WSCALE
                A.activation(dst, src, func, bias=bias[:, column:column + 1], scale=scale).then_inc(semaphore, 1)

            def project(s):
                high_half(s, z_turned, hi_ready, lambda: at_least(act, projected, s.n))
                if s.image:
                    act.wait_ge(bias_copied, 1)
                    act.wait_ge(ka_done, 1)
                    store(img_slots(k_all), img_cols(bank[2][:, 0:P]), ACT.Identity, 0, k_stored)
                    act.wait_ge(ra_done, 1)
                    act.wait_ge(constants_ready, 1)
                    store(img_slots(r_all), img_cols(bank[4][:, 0:P]), ACT.Tanh, 12, r_stored)
                    act.wait_ge(kb_done, 1)
                    store(img_b(k_all), bank[5][:, 0:64].rearrange("p (g t) -> p g t", g=PAIRS), ACT.Identity, 3, k_stored)
                    act.wait_ge(projected, 1)
                    store(img_b(r_all), bank[7][:, 0:64].rearrange("p (g t) -> p g t", g=PAIRS), ACT.Tanh, 13, r_stored)
                else:
                    hold(act, ka_done, s.n + 1)
                    store(slot(k_all, s.b)[:, IMG:T], bank[2][:], ACT.Identity, 0, k_stored)
                    hold(act, ra_done, s.n + 1)
                    store(slot(r_all, s.b)[:, IMG:T], bank[4][:], ACT.Tanh, 12, r_stored)

            project(projection(None))
            with act.Fori(0, PAIRS) as p:
                project(projection(p * 2))
                project(projection(p * 2 + 1))
                hold(act, kb_done, p + 2)
                store(slot(k_all, p + B)[:, IMG:T], bank[5][:], ACT.Identity, 3, k_stored)
                hold(act, projected, p * 2 + 3)
                store(slot(r_all, p + B)[:, IMG:T], bank[7][:], ACT.Tanh, 13, r_stored)

            def exponentials(j, par):
                act.wait_ge(decay_arg, j + 1)
                A.activation(decay[par], decay[par], ACT.Exp, bias=rate[:, 0, bass.ds(j, 1)]).then_inc(decay_exp, 1)
                act.wait_ge(gain_arg, j + 1)
                A.activation(gain[par], gain[par], ACT.Exp).then_inc(gain_exp, 1)
                act.wait_ge(mix_arg, j + 1)
                act.wait_ge(peak_ready, j + 1)
                A.activation(mix[par], mix[par], ACT.Exp).then_inc(mix_exp, 1)

            def copy_k(j, par):
                if not (isinstance(j, int) and j < 2):
                    act.wait_ge(sums_a_ready, j - 1)
                A.activation(gain[par][:, T:2 * T], k_all[:, bass.ds(j, 1), :].rearrange("p a t -> p (a t)"), ACT.Copy).then_inc(k_copied, 1)

            act.wait_ge(k_stored, 2 + B + PAIRS)
            act.wait_ge(projected, 1 + B)
            copy_k(0, 0)
            copy_k(1, 1)
            with act.Fori(0, SLOTS // 2 - 1) as i:
                for par in range(2):
                    exponentials(i * 2 + par, par)
                    copy_k(i * 2 + par + 2, par)
            exponentials(SLOTS - 2, 0)
            exponentials(SLOTS - 1, 1)

            def relus(s):
                at_least(act, gate_done, s.before)
                for g in range(G):
                    act.wait_ge(kf_done, s.n * G + g + 1)
                    A.activation(kf[:, g, 0:s.nw], bank[4 + g % 2][:, 0:s.nw], ACT.Relu, bias=bias[:, 6 + g:7 + g], scale=1 / WSCALE).then_inc(kf_relu, 1)

            def gate(s, q):
                act.wait_ge(gate_done, s.before + q + 1)
                at_least(act, gated, s.before + q - 1)
                A.activation(th[:, q % 2], bank[2 + q % 2][:, 256:256 + C], ACT.Tanh, scale=0.5 / WSCALE).then_inc(gate_tanh, 1)

            def gelus(s):
                at_least(act, hq_ready, s.n * (G // 2))
                for g in range(G):
                    act.wait_ge(up_done, s.n * G + g + 1)
                    A.activation(ge[:, g, 0:s.nw], bank[4 + g % 2][:, 0:s.nw], ACT.Gelu, bias=b1s[:, g:g + 1], scale=scale1[:, g:g + 1]).then_inc(gelu_ready, 1)

            def hidden(s, pair):
                g = 2 * pair
                act.wait_ge(ge_rounded, s.n * (G // 2) + pair + 1)
                if pair == 0:
                    at_least(act, down_done, s.before)
                A.activation(hq[:, g:g + 2, 0:s.nw], ge[:, g:g + 2, 0:s.nw], ACT.Copy, bias=-MAGIC).then_inc(hq_ready, 1)

            def round_of(now, last, then):
                if now:
                    relus(now)
                if last:
                    gelus(last)
                for q in range(QT):
                    if now and q < now.nt:
                        gate(now, q)
                    if last and q < G // 2:
                        hidden(last, q)
                if then:
                    high_half(then, z2_turned, hi2_ready, lambda: at_least(act, gate_done, then.before))

            act.wait_ge(y_ready, SLOTS)
            schedule(act, round_of)

        @block.tensor
        def _(pe):
            pe.wait_ge(tok_loaded, 64)
            for h in range(2):
                for a in range(2):
                    mm = pe.matmul(bank[h][:, 0:3 * PATCHES], kron_sb[:, a, h * P:(h + 1) * P], xt_sb[:, a], start=a == 0, stop=a == 1)
                mm.then_inc(dct_done, 1)
            pe.wait_ge(dct_copied, 2)
            for c in range(3):
                for h in range(2):
                    mm = pe.matmul(bank[2][:, 0:C], yt[:, h, c], tokw_sb[:, 2 * c + h], start=c + h == 0, stop=c + h == 3)
            mm.then_inc(img_done, 1)

            pe.wait_ge(attn_loaded, 16 * 2)
            pe.wait_ge(mlp_loaded, 16 * 4)

            def bias_column(dst, raw, cols, b):
                pe.matmul(dst, raw[:, 0, cols], vec(b), start=True, stop=False)
                pe.matmul(dst, raw[0:CB, 1, cols], vec(b + "b")[0:CB], start=False, stop=True)

            for j in range(3):
                bias_column(bank[3][:, j:j + 1], wa_raw, slice(j * CA, (j + 1) * CA), "ln1_b")
                for half in (0, CB):
                    bias_column(bank[3][half:half + CB, 3 + j:4 + j], wa_raw, slice(GB + j * CB, GB + (j + 1) * CB), "ln1_b")
            for g in range(G):
                bias_column(bank[3][:, 6 + g:7 + g], kf_raw, slice(g * P, (g + 1) * P), "ln2_b")
            pe.matmul(bank[4][:, 0:C], vec("ln2_b").to_broadcast([P, P]), rf_raw[:, 0], start=True, stop=False)
            pe.matmul(bank[4][:, 0:C], vec("ln2_bb")[0:CB].to_broadcast([CB, P]), rf_raw[0:CB, 1], start=False, stop=True).then_inc(bias_done, 1)

            def turn(s, done):
                for q in range(s.nt):
                    for a in range(2):
                        mm = pe.transpose(bank[a][:, q * P:(q + 1) * P], z[:, q, a], id32[:])
                mm.then_inc(done, 1)

            def group(dst, w, cols, rhs):
                for i, (ww, zz) in enumerate(((w[:, 0, cols], za[:, 0]), (w[:, 0, cols], za[:, 1]), (w[:, 1, cols], za[:, 0]),
                                              (w[:, 2, cols], zb[:]), (w[:, 3, cols], zb[:]))):
                    mm = pe.matmul(dst, ww, zz[:, rhs], start=i == 0, stop=i == 4)
                return mm

            def project(s):
                n, nw, half, p, first = s.n, s.nw, s.half, s.pair, s.image
                if first:
                    pe.wait_ge(bias_copied, 1)
                    pe.wait_ge(constants_ready, 1)
                pe.wait_ge(z_ready, n + 1)
                if not first:
                    pe.wait_ge(lo_ready, n)
                turn(s, z_turned)
                pe.wait_ge(lo_ready, n + 1)
                for j, (stored, done) in enumerate(((k_stored, ka_done), (v_stored, va_done), (r_stored, ra_done))):
                    if not first:
                        pe.wait_ge(stored, p * 3 + (3 if half else 1))
                    group(bank[2 + j][:, 0:nw], kvr_w, slice(j * CA, (j + 1) * CA), slice(0, nw)).then_inc(done, 1)
                for j, (stored, done) in enumerate(((k_stored, kb_done), (v_stored, vb_done), (r_stored, projected))):
                    wcols = slice(GB + j * CB, GB + (j + 1) * CB)
                    if first:
                        group(bank[5 + j][0:CB, 0:64], kvr_w, wcols, slice(0, 64))
                        group(bank[5 + j][CB:P, 0:64], kvr_w, wcols, slice(64, 128)).then_inc(done, 1)
                    else:
                        if not half:
                            pe.wait_ge(stored, p * 3 + 2)
                        mm = group(bank[5 + j][half:half + CB], kvr_w, wcols, slice(0, nw))
                        if half or j == 2:
                            mm.then_inc(done, 1)

            project(projection(None))
            with pe.Fori(0, PAIRS) as p:
                project(projection(p * 2, p, 0))
                project(projection(p * 2 + 1, p, 1))

            def attention_out(s):
                pe.wait_ge(ry_ready, s.n + 1)
                if not (isinstance(s.n, int) and s.n < 3):
                    pe.wait_ge(y2_ready, s.before - 2 * QT)
                if s.image:
                    for a in range(2):
                        rows = slice(a * 64, a * 64 + 64)
                        pe.matmul(bank[6][rows, 0:C], rya[:, rows], wo_w[:, 0], start=True, stop=False)
                        mm = pe.matmul(bank[6][rows, 0:C], ryb[rows, 0:64], wo_w[rows, 1], start=False, stop=True)
                else:
                    for q in range(QT):
                        cols = slice(q * P, (q + 1) * P)
                        dst = bank[6 + q // 2][:, (q % 2) * C:(q % 2 + 1) * C]
                        rows = slice(s.half, s.half + CB)
                        pe.matmul(dst, rya[:, cols], wo_w[:, 0], start=True, stop=False)
                        mm = pe.matmul(dst, ryb[rows, cols], wo_w[rows, 1], start=False, stop=True)
                mm.then_inc(attn_done, 1)

            def turn_z(s):
                pe.wait_ge(z2_ready, s.n + 1)
                turn(s, z2_turned)

            def squared_in(s):
                pe.wait_ge(lo2_ready, s.n + 1)
                for g in range(G):
                    if g < 2:
                        if isinstance(s.n, int) and s.n < 2:
                            pass
                        else:
                            pe.wait_ge(gelu_ready, s.n * G - G)
                    else:
                        pe.wait_ge(kf_relu, s.n * G + g - 1)
                    group(bank[4 + g % 2][:, 0:s.nw], kf_w, slice(g * P, (g + 1) * P), slice(0, s.nw)).then_inc(kf_done, 1)

            def gated_out(s):
                pe.wait_ge(kf_ready, s.n * G + G)
                for q in range(s.nt):
                    cols = slice(q * P, (q + 1) * P)
                    at_least(pe, gated, s.before + q - 1)
                    ps = bank[2 + q % 2]
                    for g in range(G):
                        pe.matmul(ps[:, 0:C], kf[:, g, cols], vf_w[:, g], start=g == 0, stop=g == G - 1)
                    dst = ps[:, 256:256 + C]
                    for i, (zz, ww) in enumerate(((za[:, 0], rf_w[:, 0]), (za[:, 1], rf_w[:, 0]), (za[:, 0], rf_w[:, 1]),
                                                  (zb[:], rf_w[:, 2]), (zb[:], rf_w[:, 3]))):
                        pe.matmul(dst, zz[:, cols], ww, start=i == 0, stop=False)
                    pe.matmul(dst, id16[:], rf_bias[:, 0], start=False, stop=False)
                    pe.matmul(dst, id16[:], rf_bias[:, 1], start=False, stop=True).then_inc(gate_done, 1)

            def turn_x(s):
                pe.wait_ge(xq_ready, s.n + 1)
                ps = bank[1][:].bitcast(BF16).rearrange("p (a n) -> p a n", a=2)
                for q in range(s.nt):
                    for a in range(2):
                        mm = pe.transpose(ps[:, a, q * P:(q + 1) * P], xq[:, q, a], idb[:])
                mm.then_inc(xq_turned, 1)

            def up(s, now):
                pe.wait_ge(xqt_ready, s.n + 1)
                for g in range(G):
                    if g < 2:
                        if now:
                            pe.wait_ge(kf_relu, now.n * G + G)
                        else:
                            pe.wait_ge(gelu_ready, s.n * G)
                    else:
                        pe.wait_ge(gelu_ready, s.n * G + g - 1)
                    cols = slice(g * P, (g + 1) * P)
                    dst = bank[4 + g % 2][:, 0:s.nw]
                    pe.matmul(dst, q1_w[:, 0, cols], xqt[:, 0, 0:s.nw], start=True, stop=False)
                    pe.matmul(dst, q1_w[0:CB, 1, cols], xqt[0:CB, 1, 0:s.nw], start=False, stop=True).then_inc(up_done, 1)

            def down(s, then):
                if then:
                    pe.wait_ge(x2_ready, then.before + then.nt)
                pe.wait_ge(hq_ready, s.n * (G // 2) + G // 2)
                for q in range(s.nt):
                    if q >= 2 or not then:
                        at_least(pe, y2_ready, s.before + q - 1)
                    for g in range(G):
                        mm = pe.matmul(bank[6 + q % 2][:, 0:C], hq[:, g, q * P:(q + 1) * P], q2_w[:, g], start=g == 0, stop=g == G - 1)
                    mm.then_inc(down_done, 1)

            def round_of(now, last, then):
                if now:
                    squared_in(now)
                if last:
                    turn_x(last)
                if then:
                    attention_out(then)
                if last:
                    up(last, now)
                if now:
                    gated_out(now)
                if then:
                    turn_z(then)
                if last:
                    down(last, then)

            schedule(pe, round_of)


def kernel(**inputs):
    import numpy as np
    import concourse.bacc as bacc
    from concourse.bass_utils import run_bass_kernel_spmd

    a = {n: np.asarray(x) for n, x in inputs.items()}
    at = {n[len("L0_attn_"):]: x for n, x in a.items() if n.startswith("L0_attn_")}

    xt = a["x"].reshape(PAIRS, 2, 3, 4, 16, 4, 16).transpose(4, 6, 2, 1, 0, 3, 5).reshape(2, P, 3, PATCHES).transpose(1, 0, 2, 3)
    k = np.arange(16.0)
    dct = 2.0 * np.cos(np.pi * (2.0 * k + 1.0) * k[:, None] / 32.0)
    kron = np.kron(dct, dct).T.astype(np.float32).reshape(2, P, 256).transpose(1, 0, 2)
    tok_w = a["L0_tok_W"].T.reshape(6, P, C).transpose(1, 0, 2)

    def rows2(w):
        return np.stack([w[0:CA], np.concatenate([w[CA:C], w[CA:C]])], axis=1)

    kvr = [at["Wk_a"], at["Wv_a"], at["Wr_a"]]
    attn_w = rows2(np.concatenate([w[0:CA].T for w in kvr] + [w[CA:C].T for w in kvr], axis=1))
    vectors = [at[n] for n in ("ln1_w", "ln1_b", "ln2_w", "ln2_b", "decay", "first")]
    cols = np.concatenate([rows2(v[:, None])[:, :, 0] for v in vectors]
                          + [a["L0_ffn_alpha_w1"].reshape(G, P).T, a["L0_ffn_b1"].reshape(G, P).T], axis=1)
    rows = np.concatenate([a["L0_ffn_" + n] for n in ROWS])[None]
    arrays = {
        "txt": a["txt"], "xt": xt, "kron": kron, "tok_w": tok_w, "ident": np.eye(P, dtype=np.float32),
        "cols": cols, "rows": rows, "attn_w": attn_w,
        "kf_src": rows2(at["Wk_f"].T), "rf_src": rows2(at["Wr_f"].T), "wo_src": rows2(at["Wo_a"].T),
        "vf_src": at["Wv_f"].T.reshape(G, P, C).transpose(1, 0, 2),
        "w1": rows2(a["L0_ffn_w1"].T), "w2": a["L0_ffn_w2"].T.reshape(G, P, C).transpose(1, 0, 2),
    }
    arrays = {n: np.ascontiguousarray(x) for n, x in arrays.items()}
    nc = bacc.Bacc("TRN2", target_bir_lowering=False, num_devices=1)
    args = {n: nc.dram_tensor(n, x.shape, mybir.dt.from_np(x.dtype), kind="ExternalInput").ap() for n, x in arrays.items()}
    out = nc.dram_tensor("out", (B, T, C), F32, kind="ExternalOutput").ap()
    fusion_kernel(nc, **args, out=out)
    return run_bass_kernel_spmd(nc, [arrays], core_ids=[0]).results[0]["out"]
```

```python
from contextlib import ExitStack

import concourse.bass as bass
from concourse import mybir

F32 = mybir.dt.float32
F16 = mybir.dt.float16
BF16 = mybir.dt.bfloat16
ALU = mybir.AluOpType
ACT = mybir.ActivationFunctionType
AX_X = mybir.AxisListType.X

P = 128
B, TXT, C, HID = 8, 512, 192, 768
IMG = 16
T = IMG + TXT
CA, CB = 128, C - 128
PAIRS = B // 2
SLOTS = B + PAIRS
QT = TXT // P
TILES = 1 + B * QT
G = HID // P
EPS = 1e-5
WSCALE = 256.0
MAGIC = 1.5 * 2.0 ** 23
QN, QP = -8.0, 7.0
POOL_SQUARES = (2, 5)
UP_BANK = (2, 3, 4, 5, 0, 1)
CLIP = 10.0
NEG = -1e38
KVR = 3 * C
GB = 3 * CA
PATCHES = P


COLS = {name: i for i, name in enumerate(
    ["ln1_w", "ln1_wb", "ln1_b", "ln1_bb", "ln2_w", "ln2_wb", "ln2_b", "ln2_bb", "decay", "decay_b", "first", "first_b",
     "alpha_w2", "alpha_w2b"])}
NCOL = len(COLS) + 2 * G
ROWS = {"alpha_a2": (0, HID), "alpha_a1": (HID, C), "alpha_w2": (HID + C, C), "b2": (HID + 2 * C, C)}
NROW = HID + 3 * C


def fusion_kernel(nc, txt, xt, kron, tok_w, ident, cols, rows, attn_w, kf_src, rf_src, wo_src, vf_src, w1, w2, out):
    with ExitStack() as ctx:
        def sb(name, shape, dt=F32):
            return ctx.enter_context(nc.sbuf_tensor(name, shape, dt))

        def sem(name):
            return ctx.enter_context(nc.semaphore(name))

        hid = sb("hid", [P, TILES, C])
        x1 = sb("x1", [P, TILES, C])
        k_all = sb("k_all", [P, SLOTS, T])
        v_all = sb("v_all", [P, SLOTS, T])
        r_all = sb("r_all", [P, SLOTS, T])

        id32 = sb("id32", [P, P])
        id16 = sb("id16", [P, P], F16)
        idb = sb("idb", [P, P], BF16)
        pick = sb("pick", [P, P], F16)
        kvr_w = sb("kvr_w", [P, 4, KVR], F16)
        kf_w = sb("kf_w", [P, 4, HID], F16)
        rf_w = sb("rf_w", [P, 4, C], F16)
        rf_bias = sb("rf_bias", [P, C], F16)
        vf_w = sb("vf_w", [P, G, C])
        wo_w = sb("wo_w", [P, 2, C])
        q1_w = sb("q1_w", [P, 2, HID], BF16)
        q2_w = sb("q2_w", [P, G, C], BF16)
        col = sb("col", [P, NCOL])
        lnw = sb("lnw", [P, 4])
        rate = sb("rate", [P, 2, SLOTS])
        bias = sb("bias", [P, 16])
        aw1c = col[:, len(COLS):len(COLS) + G]
        b1s = col[:, len(COLS) + G:NCOL]
        scale1 = sb("scale1", [P, G])
        scale2 = sb("scale2", [P, C])
        b2s = sb("b2s", [P, C])
        aq = sb("aq", [P, 8])
        inverses = sb("inverses", [P, G + 2])
        minus_half = sb("minus_half", [P, 2 * QT])

        st = sb("st", [P, 2, QT, 6])
        mv2 = sb("mv2", [P, 2, QT, 2])
        rs2 = sb("rs2", [P, 2, 2, QT])
        z = sb("z", [P, QT, C])
        z16 = sb("z16", [P, 3, TXT], F16)
        HI, LO_B, LO_A, SPLIT = 0, C, C + CB, 2 * C

        ARENA = 12688
        arena = sb("arena", [P, ARENA])

        class Carve:
            def __init__(self):
                self.at = 0

            def __call__(self, n):
                self.at += n
                assert self.at <= ARENA
                return arena[:, self.at - n:self.at]

        carve = Carve()
        proj_z16 = z16, carve(3 * TXT // 2).bitcast(F16).rearrange("p (a n) -> p a n", a=3)
        halves1 = carve(QT * SPLIT // 2).bitcast(F16).rearrange("p (q n) -> p q n", q=QT)
        xt_sb = carve(2 * 3 * PATCHES).rearrange("p (a n) -> p a n", a=2)
        kron_sb = carve(2 * 256).rearrange("p (a n) -> p a n", a=2)
        tokw_sb = carve(6 * C).rearrange("p (a n) -> p a n", a=6)
        yt = carve(2 * 3 * PATCHES).rearrange("p (a c n) -> p a c n", a=2, c=3)
        wa_raw = carve(2 * KVR).rearrange("p (a n) -> p a n", a=2)
        kf_raw = carve(2 * HID).rearrange("p (a n) -> p a n", a=2)
        rf_raw = carve(2 * C).rearrange("p (a n) -> p a n", a=2)
        kf_scaled = carve(2 * HID).rearrange("p (a n) -> p a n", a=2)
        rf_scaled = carve(2 * C).rearrange("p (a n) -> p a n", a=2)
        wtmp = carve(KVR)

        carve = Carve()
        W2 = 2 * (T + 1)
        env = [carve(W2) for _ in range(2)]
        sa = carve(W2)
        sbk = carve(W2)
        decay = [carve(2 * T) for _ in range(2)]
        gain = [carve(2 * T) for _ in range(2)]
        peak = [carve(T) for _ in range(2)]
        mix = [carve(3 * T) for _ in range(2)]
        inverse, minus_id = (z[:].rearrange("p q n -> p (q n)")[:, a:a + n] for a, n in ((0, T), (T, P)))
        own_part = z16[:].rearrange("p a n -> p (a n)").bitcast(F32)[:, 0:T]
        gain_v = kvr_w[:].rearrange("p a n -> p (a n)").bitcast(F32)[:, 0:2 * T]

        carve = Carve()
        rya = carve(TXT)
        ryb = carve(TXT)
        kf = carve(G * TXT).rearrange("p (g n) -> p g n", g=G)
        ge = carve(G * TXT).rearrange("p (g n) -> p g n", g=G)
        hq = carve(G * TXT // 2).bitcast(BF16).rearrange("p (g n) -> p g n", g=G)
        th = carve(2 * C).rearrange("p (a n) -> p a n", a=2)
        gv = carve(2 * C).rearrange("p (a n) -> p a n", a=2)
        xs = carve(QT * C).rearrange("p (q n) -> p q n", q=QT)
        xq = carve(QT * C // 2).bitcast(BF16).rearrange("p (q n) -> p q n", q=QT)
        halves2 = carve(QT * SPLIT // 2).bitcast(F16).rearrange("p (q n) -> p q n", q=QT)
        xqt = carve(TXT).bitcast(BF16).rearrange("p (a n) -> p a n", a=2)
        y2 = carve(QT * C).rearrange("p (q n) -> p q n", q=QT)
        mlp_z16 = z16, kvr_w[:].rearrange("p a n -> p (a n)")[:, 0:3 * TXT].rearrange("p (a n) -> p a n", a=3)
        w1_raw = ge.rearrange("p g n -> p (g n)")[:, 0:2 * HID].rearrange("p (a n) -> p a n", a=2)
        w2_raw = ge.rearrange("p g n -> p (g n)")[:, 2 * HID:2 * HID + G * C].rearrange("p (a n) -> p a n", a=G)
        row = hq.rearrange("p g n -> p (g n)").bitcast(F32)[:, 0:NROW]
        a2_row, a1_row, aw2, b2_row = (row[:, a:a + n] for a, n in ROWS.values())
        inv_row = y2.rearrange("p q n -> p (q n)")
        inv2_row = xs[:, 0]

        psum = ctx.enter_context(nc.psum_tensor("psum", [P, 8, 512], F32))
        bank = [psum[:, i] for i in range(8)]
        TH = T // 2
        den_sum, num_sum, gain_args = (psum[:, a:a + n, 0:TH] for a, n in ((0, 2), (2, 2), (4, 4)))

        turned_z = bank[0].bitcast(F16).rearrange("p (a n) -> p a n", a=2)
        turned_zb = bank[1].bitcast(F16)[:, 0:TXT]
        inv_psum = psum[:, 4:6].rearrange("p a n -> p (a n)")

        def tile_pair(i):
            return bank[6 + i][:, 0:2 * C].rearrange("p (a n) -> p a n", a=2)

        ident_loaded, dct_loaded, late_biases_done = sem("ident_loaded"), sem("dct_loaded"), sem("late_biases_done")
        tok_loaded, attn_loaded, mlp_loaded, ffn_loaded = (sem(n) for n in ("tok_loaded", "attn_loaded", "mlp_loaded", "ffn_loaded"))
        text_even_loaded, text_odd_loaded = sem("text_even_loaded"), sem("text_odd_loaded")
        setup_dve, setup_pool, constants_ready = sem("setup_dve"), sem("setup_pool"), sem("constants_ready")
        dct_done, dct_copied, img_done, img_copied = (sem(n) for n in ("dct_done", "dct_copied", "img_done", "img_copied"))
        bias_done, bias_copied = sem("bias_done"), sem("bias_copied")
        stat_step, stats_ready, power_step, powers_ready, z_ready, z_turned = (
            sem(n) for n in ("stat_step", "stats_ready", "power_step", "powers_ready", "z_ready", "z_turned"))
        hi_ready, lo_ready, z16_ready = sem("hi_ready"), sem("lo_ready"), sem("z16_ready")
        lnw_ready, mlp_scaled, mlp_hi_ready, mlp_split = (sem(n) for n in ("lnw_ready", "mlp_scaled", "mlp_hi_ready", "mlp_split"))
        inv_spread, inv_copied = sem("inv_spread"), sem("inv_copied")
        ka_done, va_done, ra_done, kb_done, vb_done, projected = (
            sem(n) for n in ("ka_done", "va_done", "ra_done", "kb_done", "vb_done", "projected"))
        k_stored, v_stored, r_stored = sem("k_stored"), sem("v_stored"), sem("r_stored")
        k_copied, env_ready, peak_step, peak_ready, own_arg = (sem(n) for n in ("k_copied", "env_ready", "peak_step", "peak_ready", "own_arg"))
        decay_arg, gain_arg, mix_arg = sem("decay_arg"), sem("gain_arg"), sem("mix_arg")
        decay_exp, gain_exp, mix_exp = sem("decay_exp"), sem("gain_exp"), sem("mix_exp")
        gain_v_ready, sums_b_ready, sums_a_ready = sem("gain_v_ready"), sem("sums_b_ready"), sem("sums_a_ready")
        edges_ready, den_parts, num_parts, own_num = (sem(n) for n in ("edges_ready", "den_parts", "num_parts", "own_num"))
        den_summed, num_summed, den_log, inverse_ready, y_scaled, y_ready = (
            sem(n) for n in ("den_summed", "num_summed", "den_log", "inverse_ready", "y_scaled", "y_ready"))
        ry_ready, attn_done, x2_ready, hx_ready = (sem(n) for n in ("ry_ready", "attn_done", "x2_ready", "hx_ready"))
        z2_ready, z2_turned, hi2_ready, lo2_ready, z16b_ready = (
            sem(n) for n in ("z2_ready", "z2_turned", "hi2_ready", "lo2_ready", "z16b_ready"))
        stat2_step, stats2_ready, power2_step, powers2_ready = (sem(n) for n in ("stat2_step", "stats2_ready", "power2_step", "powers2_ready"))
        kf_done, kf_relu, kf_ready, gate_done, gate_tanh, gated, h3_ready = (
            sem(n) for n in ("kf_done", "kf_relu", "kf_ready", "gate_done", "gate_tanh", "gated", "h3_ready"))
        stat3_step, stats3_ready, power3_step, powers3_ready, xs_ready, xs_clipped, xq_ready = (
            sem(n) for n in ("stat3_step", "stats3_ready", "power3_step", "powers3_ready", "xs_ready", "xs_clipped", "xq_ready"))
        xq_turned, xqt_ready, up_done, gelu_ready, ge_scaled, ge_rounded, hq_ready = (
            sem(n) for n in ("xq_turned", "xqt_ready", "up_done", "gelu_ready", "ge_scaled", "ge_rounded", "hq_ready"))
        held = sem("held")
        h3b_ready, down_done, y2_ready, out_ready, stored = (
            sem(n) for n in ("h3b_ready", "down_done", "y2_ready", "out_ready", "stored"))

        class Step:

            def __init__(self, b, pair=None, odd=0):
                self.image = b is None
                self.b, self.pair, self.par, self.half = b, pair, odd, CB * odd
                self.n = B if self.image else b
                self.nt = 1 if self.image else QT
                self.nw = P * self.nt
                self.tile = B * QT if self.image else b * QT
                self.before = self.tile

        def mlp(b, pair=None, odd=0):
            s = Step(b, pair, odd)
            if s.image:
                s.n, s.before, s.par = 1, QT, 1
            elif not (isinstance(b, int) and b == 0):
                s.n, s.before, s.par = b + 1, b * QT + 1, 1 - odd
            s.before_two = QT if isinstance(s.n, int) and s.n == 3 else s.before - 2 * QT
            return s

        def tile(a, t):
            return a[:, bass.ds(t, 1), :].rearrange("p a c -> p (a c)")

        def slot(a, j):
            return a[:, bass.ds(j, 1), :].rearrange("p a t -> p (a t)")

        def excl(buf):
            return _two(buf, 0, T + 2)

        def incl(buf):
            return _two(buf, 1, T)

        def _two(buf, at, step):
            return bass.AP(buf.tensor, buf.offset + at, [list(buf.ap[0]), [step, 2], [1, T]])

        def vec(name):
            return col[:, COLS[name]:COLS[name] + 1]

        def at_least(eng, semaphore, value):
            if not isinstance(value, int) or value > 0:
                eng.wait_ge(semaphore, value)

        def twice(ap):
            return bass.AP(ap.tensor, ap.offset, [list(ap.ap[0]), [0, 2], list(ap.ap[1])])

        def halves(ap, n=T):
            return ap.rearrange("p (a n) -> p a n", n=n)

        def img_slots(a):
            return a[:, 0:B, 0:IMG].rearrange("p (g a) t -> p a g t", a=2)

        def img_cols(ps):
            return ps.rearrange("p (a g t) -> p a g t", a=2, g=PAIRS)

        def img_b(a):
            return a[:, B:SLOTS, 0:IMG]

        def hold(eng, semaphore, value):
            eng.wait_ge(semaphore, value)
            if not isinstance(value, int):
                eng.sem_inc(held, 1)

        def projection_schedule(eng, round_of):
            round_of(None, Step(0, 0, 0), Step(1, 0, 1))
            round_of(Step(0, 0, 0), Step(1, 0, 1), Step(2, 1, 0))
            round_of(Step(1, 0, 1), Step(2, 1, 0), Step(3, 1, 1))
            with eng.Fori(1, PAIRS - 1) as p:
                round_of(Step(p * 2, p, 0), Step(p * 2 + 1, p, 1), Step(p * 2 + 2, p + 1, 0))
                round_of(Step(p * 2 + 1, p, 1), Step(p * 2 + 2, p + 1, 0), Step(p * 2 + 3, p + 1, 1))
            last = PAIRS - 1
            round_of(Step(B - 2, last, 0), Step(B - 1, last, 1), Step(None))
            round_of(Step(B - 1, last, 1), Step(None), None)
            round_of(Step(None), None, None)

        def done_pair(now):
            if not now or now.par or (isinstance(now.n, int) and now.n == 0):
                return None
            return PAIRS - 1 if now.image else now.pair - 1

        def mlp_schedule(eng, round_of):
            round_of(None, None, mlp(0, 0, 0))
            round_of(mlp(0, 0, 0), None, mlp(None))
            round_of(mlp(None), mlp(0, 0, 0), mlp(1, 0, 1))
            round_of(mlp(1, 0, 1), mlp(None), mlp(2, 1, 0))
            with eng.Fori(1, PAIRS - 1) as p:
                round_of(mlp(p * 2, p, 0), mlp(p * 2 - 1, p - 1, 1), mlp(p * 2 + 1, p, 1))
                round_of(mlp(p * 2 + 1, p, 1), mlp(p * 2, p, 0), mlp(p * 2 + 2, p + 1, 0))
            end = PAIRS - 1
            round_of(mlp(B - 2, end, 0), mlp(B - 3, end - 1, 1), mlp(B - 1, end, 1))
            round_of(mlp(B - 1, end, 1), mlp(B - 2, end, 0), None)
            round_of(None, mlp(B - 1, end, 1), None)

        def wkv_schedule(eng, round_of, before_last=None):
            round_of(0, 0, 2)
            with eng.Fori(0, (SLOTS - 4) // 2) as i:
                round_of(i * 2 + 1, 1, 2)
                round_of(i * 2 + 2, 0, 2)
            for j in range(SLOTS - 3, SLOTS):
                if j == SLOTS - 1 and before_last:
                    before_last()
                round_of(j, j % 2, min(2, SLOTS - 1 - j))

        block = ctx.enter_context(nc.Block())

        @block.sync
        def _(sp):
            def load_text(b, loaded):
                sp.dma_start(hid[:, bass.ds(b * QT, QT), :],
                             txt[bass.ds(b, 1)].rearrange("a (q p) c -> p (a q) c", p=P)).then_inc(loaded, 16)

            load_text(0, text_even_loaded)
            sp.dma_start(id32[:], ident).then_inc(ident_loaded, 16)
            for dst, src in ((xt_sb, xt), (kron_sb, kron)):
                sp.dma_start(dst, src).then_inc(dct_loaded, 16)
            sp.dma_start(tokw_sb, tok_w).then_inc(tok_loaded, 16)
            load_text(1, text_odd_loaded)
            with sp.Fori(1, PAIRS) as p:
                for parity, loaded in ((0, text_even_loaded), (1, text_odd_loaded)):
                    hold(sp, loaded, p * 16)
                    load_text(p * 2 + parity, loaded)
            sp.wait_ge(text_even_loaded, PAIRS * 16)
            sp.wait_ge(text_odd_loaded, PAIRS * 16)
            sp.wait_ge(y_ready, SLOTS)
            for dst, src in ((row, rows.to_broadcast([P, NROW])), (w1_raw, w1), (w2_raw, w2)):
                sp.dma_start(dst, src).then_inc(ffn_loaded, 16)

            def store_text(b, tiles_done):
                hold(sp, out_ready, tiles_done)
                sp.dma_start(out[bass.ds(b, 1), IMG:T, :].rearrange("a (q p) c -> p (a q) c", p=P),
                             hid[:, bass.ds(b * QT, QT), :]).then_inc(stored, 16)

            store_text(0, QT)
            sp.wait_ge(out_ready, QT + 1)
            for parity in range(2):
                for g in range(PAIRS):
                    at = 64 * parity + IMG * g
                    sp.dma_start(out[2 * g + parity, 0:IMG, :], hid[at:at + IMG, TILES - 1, :]).then_inc(stored, 16)
            with sp.Fori(1, B) as b:
                store_text(b, b * QT + QT + 1)
            sp.wait_ge(stored, 16 * (B + B))

        @block.gpsimd
        def _(pool):
            nc.gpsimd.memset(minus_half[:], -0.5).then_inc(setup_pool, 1)
            pool.wait_ge(setup_pool, 1)

            def powers(s):
                n = s.n
                var, rs = mv2[:, s.par, 0:s.nt, 1], rs2[:, s.par]
                hold(pool, stats_ready, n + 1)
                nc.gpsimd.tensor_scalar(rs[:, 0, 0:s.nt], var, EPS, None, ALU.add).then_inc(power_step, 1)
                nc.gpsimd.tensor_scalar(rs[:, 1, 0:s.nt], var, 1.0 + EPS, EPS * EPS, ALU.mult, ALU.add).then_inc(power_step, 1)
                pool.wait_ge(power_step, 2 * n + 2)
                nc.gpsimd.tensor_tensor(rs[:, :, 0:s.nt], rs[:, :, 0:s.nt],
                                        minus_half[:].rearrange("p (a n) -> p a n", a=2)[:, :, 0:s.nt], ALU.pow).then_inc(powers_ready, 1)

            powers(Step(0, 0, 0))

            def projection_round(now, then, after):
                if after:
                    powers(after)
                if isinstance(now and now.n, int) and now.n == 1:
                    for i, (scaled, w) in enumerate(((kf_scaled, kf_w), (rf_scaled, rf_w))):
                        pool.wait_ge(mlp_hi_ready, i + 1)
                        for h in range(2):
                            nc.gpsimd.tensor_tensor(w[:, 2 * h + 1], scaled[:, h], w[:, 2 * h], ALU.subtract).then_inc(mlp_split, 1)

            projection_schedule(pool, projection_round)

            def own(j, par):
                if not (isinstance(j, int) and j == 0):
                    hold(pool, num_summed, j)
                nc.gpsimd.tensor_tensor(own_part, halves(mix[par])[:, 2], slot(v_all, j), ALU.mult).then_inc(own_num, 1)

            def arguments(j, par):
                pool.wait_ge(env_ready, j + 1)
                nc.gpsimd.tensor_tensor(halves(decay[par]), excl(env[par]), incl(env[par]), ALU.subtract).then_inc(decay_arg, 1)
                if not (isinstance(j, int) and j < 2):
                    hold(pool, den_parts, j - 1)
                pool.wait_ge(peak_ready, j + 1)
                nc.gpsimd.tensor_tensor(halves(mix[par])[:, 0:2], excl(env[par]), twice(peak[par]), ALU.subtract).then_inc(mix_arg, 1)

            def weighted(j, par):
                pool.wait_ge(mix_exp, j + 1)
                pool.wait_ge(sums_b_ready, j + 1)
                nc.gpsimd.tensor_tensor(excl(sbk), halves(mix[par])[:, 0:2], excl(sbk), ALU.mult).then_inc(den_parts, 1)

            def wkv_round(j, par, ahead):
                weighted(j, par)
                own(j, par)
                if ahead == 2:
                    arguments(j + 2, par)

            pool.wait_ge(k_stored, 2 + B + PAIRS)
            pool.wait_ge(v_stored, 2 + B + PAIRS)
            arguments(0, 0)
            arguments(1, 1)
            wkv_schedule(pool, wkv_round)

            def powers2(s):
                hold(pool, stats2_ready, s.n + 1)
                rs = rs2[:, 0, 0, 0:s.nt]
                nc.gpsimd.tensor_scalar(rs, mv2[:, 0, 0:s.nt, 1], EPS, None, ALU.add).then_inc(power2_step, 1)
                pool.wait_ge(power2_step, s.n + 1)
                nc.gpsimd.tensor_tensor(rs, rs, minus_half[:, 0:s.nt], ALU.pow).then_inc(powers2_ready, 1)

            def add_x2(s):
                for q in range(s.nt):
                    nc.gpsimd.tensor_tensor(tile(hid, s.tile + q), tile(hid, s.tile + q), tile(x1, s.tile + q), ALU.add).then_inc(hx_ready, 1)

            def powers3(s, end):
                rs = rs2[:, 1, 0, 0:s.nt]
                hold(pool, stats3_ready, s.n + 1)
                nc.gpsimd.tensor_scalar(rs, mv2[:, 1, 0:s.nt, 1], EPS, None, ALU.add).then_inc(power3_step, 1)
                pool.wait_ge(power3_step, s.n * 2 + 1)
                nc.gpsimd.tensor_tensor(rs, rs, minus_half[:, 0:s.nt], ALU.pow).then_inc(power3_step, 1)
                hold(pool, power3_step, s.n * 2 + 2)
                nc.gpsimd.tensor_scalar(rs, rs, aq[:, 1:2], None, ALU.mult).then_inc(powers3_ready, 1)
                if end:
                    finish(mlp(B - 2, PAIRS - 1, 0))
                hold(pool, xs_ready, s.before + s.nt)
                for q in range(s.nt):
                    nc.gpsimd.tensor_tensor(tile(hid, s.tile + q), tile(hid, s.tile + q), b2s[:], ALU.add).then_inc(h3b_ready, 1)

            def finish(s):
                for q in range(s.nt):
                    pool.wait_ge(y2_ready, s.before + min(s.nt, q // 2 * 2 + 2))
                    hold(pool, h3b_ready, s.before + q + 1)
                    nc.gpsimd.tensor_tensor(tile(hid, s.tile + q), tile(hid, s.tile + q), y2[:, q], ALU.add).then_inc(out_ready, 1)

            def square(s, g):
                pool.wait_ge(kf_relu, s.n * G + g + 1)
                nc.gpsimd.tensor_tensor(kf[:, g, 0:s.nw], kf[:, g, 0:s.nw], kf[:, g, 0:s.nw], ALU.mult).then_inc(kf_ready, 1)

            def round_of(now, last, then):
                end = not (now or then)
                if last:
                    powers3(last, end)
                if now:
                    for g in POOL_SQUARES:
                        square(now, g)
                if then:
                    powers2(then)
                    add_x2(then)
                if last and (then or end):
                    finish(last)

            pool.wait_ge(constants_ready, 1)
            mlp_schedule(pool, round_of)

        @block.vector
        def _(dve):
            count = [0]

            def did(ins):
                count[0] += 1
                ins.then_inc(setup_dve, 1)

            def settled():
                dve.wait_ge(setup_dve, count[0])

            V = nc.vector

            def statistics(s, par, step, ready, data):
                for q in range(s.nt):
                    V.bn_stats(st[:, par, q], tile(data, s.tile + q)).then_inc(step, 1)
                hold(dve, step, s.before + s.nt)
                for q in range(s.nt):
                    ins = V.bn_aggr(mv2[:, par, q], st[:, par, q])
                ins.then_inc(ready, 1)

            def measure(s):
                if s.image:
                    dve.wait_ge(img_copied, 1)
                elif s.par:
                    hold(dve, text_odd_loaded, s.pair * 16 + 16)
                else:
                    hold(dve, text_even_loaded, s.pair * 16 + 16)
                statistics(s, s.par, stat_step, stats_ready, hid)

            dve.wait_ge(attn_loaded, 16 * 2)
            for j, name in enumerate(("ln1_w", "ln1_wb", "ln2_w", "ln2_wb")):
                V.tensor_scalar(lnw[:, j:j + 1], vec(name), WSCALE, None, ALU.mult).then_inc(lnw_ready, 1)
            measure(Step(0, 0, 0))
            dve.wait_ge(lnw_ready, 4)

            for h in range(2):
                did(V.tensor_scalar(wtmp, wa_raw[:, h], lnw[:, h:h + 1], None, ALU.mult))
                settled()
                did(V.tensor_copy(kvr_w[:, 2 * h], wtmp))
                settled()
                did(V.tensor_tensor(kvr_w[:, 2 * h + 1], wtmp, kvr_w[:, 2 * h], ALU.subtract))
                settled()
            dve.wait_ge(ident_loaded, 16)
            did(V.tensor_copy(id16[:], id32[:]))
            did(V.tensor_copy(idb[:], id32[:]))
            did(V.memset(pick[:], 0.0))
            for which, name in enumerate(("decay", "first")):
                for at, n, tail_ in ((0, B, ""), (B, PAIRS, "_b")):
                    did(V.tensor_scalar(rate[:, which, at:at + n], vec(name + tail_).to_broadcast([P, n]), 1.0 / T, None, ALU.mult))
            did(V.reciprocal(inverses[:, 0:G], aw1c))
            did(V.reciprocal(inverses[:, G:G + 2], col[:, COLS["alpha_w2"]:COLS["alpha_w2"] + 2]))
            settled()
            for r in (0, CB):
                did(V.memset(pick[r:r + 1], 1.0))
            dve.wait_ge(bias_done, 1)
            V.tensor_copy(bias[:, 0:6], bank[3][:, 0:6]).then_inc(bias_copied, 1)
            dve.wait_ge(bias_copied, 1)
            did(V.tensor_scalar(bias[:, 12:13], bias[:, 2:3], 0.5, None, ALU.mult))
            settled()
            V.tensor_scalar(bias[:, 13:14], bias[:, 5:6], 0.5, None, ALU.mult).then_inc(constants_ready, 1)

            def image_tokens():
                for h in range(2):
                    dve.wait_ge(dct_done, h + 1)
                    V.tensor_copy(yt[:, h].rearrange("p c n -> p (c n)"), bank[5 + h][:, 0:3 * PATCHES]).then_inc(dct_copied, 1)
                dve.wait_ge(img_done, 1)
                V.tensor_copy(hid[:, TILES - 1], bank[7][:, 0:C]).then_inc(img_copied, 1)
                dve.wait_ge(late_biases_done, 1)
                did(V.tensor_copy(bias[:, 6:6 + G], bank[6][:, 0:G]))
                did(V.tensor_scalar(wtmp[:, 0:C], bank[6][:, 256:256 + C], WSCALE, None, ALU.mult))
                settled()
                did(V.tensor_copy(rf_bias[:], wtmp[:, 0:C]))
                settled()
                V.tensor_tensor(rf_bias[CB:P], wtmp[CB:P, 0:C], rf_bias[CB:P], ALU.subtract).then_inc(bias_copied, 1)
                dve.wait_ge(bias_copied, 2)

            def write_z(src, s, par, which):
                for q in range(s.nt):
                    ins = V.tensor_scalar(z[:, q], tile(src, s.tile + q), mv2[:, par, q, 0:1], rs2[:, par, which, q:q + 1],
                                          ALU.subtract, ALU.mult)
                return ins

            def low_half(s, halves_, hi, lo):
                dve.wait_ge(hi, s.n + 1)
                h = halves_[:, 0:s.nt]
                V.tensor_tensor(h[:, :, LO_A:SPLIT], z[:, 0:s.nt, 0:CA], h[:, :, 0:CA], ALU.subtract)
                V.tensor_tensor(h[:, :, LO_B:LO_A], z[:, 0:s.nt, CA:C], h[:, :, CA:C], ALU.subtract).then_inc(lo, 1)

            def projection_round(now, then, after):
                if then:
                    dve.wait_ge(powers_ready, then.n + 1)
                    at_least(dve, lo_ready, then.n)
                    write_z(hid, then, then.par, 1).then_inc(z_ready, 1)
                if after:
                    measure(after)
                pair = done_pair(now)
                if pair is not None:
                    dve.wait_ge(vb_done, pair + 1)
                    V.tensor_scalar(v_all[:, bass.ds(pair + B, 1), IMG:T].rearrange("p a t -> p (a t)"), bank[6][:],
                                    1 / WSCALE, bias[:, 4:5], ALU.mult, ALU.add).then_inc(v_stored, 1)
                if then:
                    low_half(then, halves1, hi_ready, lo_ready)
                    for q in range(then.nt):
                        V.tensor_scalar(tile(x1, then.tile + q), tile(hid, then.tile + q), mv2[:, then.par, q, 0:1],
                                        rs2[:, then.par, 0, q:q + 1], ALU.subtract, ALU.mult)
                if now and isinstance(now.n, int) and now.n == 0:
                    image_tokens()
                if now:
                    dve.wait_ge(va_done, now.n + 1)
                    if now.image:
                        V.tensor_scalar(img_slots(v_all), img_cols(bank[3][:, 0:P]), 1 / WSCALE, bias[:, 1:2], ALU.mult, ALU.add).then_inc(v_stored, 1)
                        dve.wait_ge(vb_done, PAIRS + 1)
                        V.tensor_scalar(img_b(v_all), bank[6][:, 0:64].rearrange("p (g t) -> p g t", g=PAIRS),
                                        1 / WSCALE, bias[:, 4:5], ALU.mult, ALU.add).then_inc(v_stored, 1)
                    else:
                        V.tensor_scalar(slot(v_all, now.b)[:, IMG:T], bank[3][:],
                                        1 / WSCALE, bias[:, 1:2], ALU.mult, ALU.add).then_inc(v_stored, 1)

            projection_schedule(dve, projection_round)

            F0, B0 = 1, T + 1
            dve.wait_ge(projected, 1 + B)
            dve.wait_ge(mlp_split, 4)
            for buf, val in ((env[0], NEG), (env[1], NEG), (sa, 0.0), (sbk, 0.0)):
                V.memset(buf[:, 0:1], val).then_inc(edges_ready, 1)
                V.memset(buf[:, 2 * T + 1:2 * T + 2], val).then_inc(edges_ready, 1)
            V.tensor_scalar(minus_id, id32[:], -1.0, None, ALU.mult).then_inc(edges_ready, 1)
            dve.wait_ge(edges_ready, 9)
            dve.wait_ge(k_stored, 2 + B + PAIRS)

            def maxima(j, par):
                wb = rate[:, 0, bass.ds(j, 1)].to_broadcast([P, T])
                if not (isinstance(j, int) and j < 2):
                    dve.wait_ge(mix_arg, j - 1)
                V.tensor_tensor_scan(env[par][:, F0:F0 + T], wb, slot(k_all, j), NEG, ALU.add, ALU.max)
                dve.wait_ge(k_copied, j + 1)
                V.tensor_tensor_scan(env[par][:, B0:B0 + T][:, ::-1], wb, gain[par][:, T:2 * T][:, ::-1], NEG, ALU.add, ALU.max).then_inc(env_ready, 1)

            def peaks(j, par):
                dve.wait_ge(env_ready, j + 1)
                V.tensor_tensor(peak[par], env[par][:, 0:T], env[par][:, T + 2:2 * T + 2], ALU.max).then_inc(peak_step, 1)

            def peaks_2(j, par):
                u = rate[:, 1, bass.ds(j, 1)]
                k_t = slot(k_all, j)
                dve.wait_ge(peak_step, j + 1)
                V.scalar_tensor_tensor(peak[par], k_t, u, peak[par], ALU.add, ALU.max).then_inc(peak_ready, 1)

            def own_argument(j, par):
                if not (isinstance(j, int) and j < 2):
                    dve.wait_ge(den_summed, j - 1)
                dve.wait_ge(peak_ready, j + 1)
                V.tensor_tensor(halves(mix[par])[:, 2], slot(k_all, j), peak[par], ALU.subtract).then_inc(own_arg, 1)

            def gain_values(j, par):
                dve.wait_ge(gain_exp, j + 1)
                V.tensor_tensor(halves(gain_v), halves(gain[par]), twice(slot(v_all, j)), ALU.mult).then_inc(gain_v_ready, 1)

            def sums_b(j, par):
                dve.wait_ge(decay_exp, j + 1)
                if not (isinstance(j, int) and j == 0):
                    dve.wait_ge(den_summed, j)
                d, g = halves(decay[par]), halves(gain[par])
                V.tensor_tensor_scan(sbk[:, F0:F0 + T], d[:, 0], g[:, 0], 0.0, ALU.mult, ALU.add)
                V.tensor_tensor_scan(sbk[:, B0:B0 + T][:, ::-1], d[:, 1][:, ::-1], g[:, 1][:, ::-1], 0.0, ALU.mult, ALU.add).then_inc(sums_b_ready, 1)

            def sums_a(j, par):
                d, gv2 = halves(decay[par]), halves(gain_v)
                dve.wait_ge(gain_v_ready, j + 1)
                if not (isinstance(j, int) and j == 0):
                    dve.wait_ge(num_summed, j)
                V.tensor_tensor_scan(sa[:, F0:F0 + T], d[:, 0], gv2[:, 0], 0.0, ALU.mult, ALU.add)
                V.tensor_tensor_scan(sa[:, B0:B0 + T][:, ::-1], d[:, 1][:, ::-1], gv2[:, 1][:, ::-1], 0.0, ALU.mult, ALU.add).then_inc(sums_a_ready, 1)

            def weighted(j, par):
                dve.wait_ge(sums_a_ready, j + 1)
                dve.wait_ge(mix_exp, j + 1)
                V.tensor_tensor(excl(sa), halves(mix[par])[:, 0:2], excl(sa), ALU.mult).then_inc(num_parts, 1)

            def finish(j):
                dve.wait_ge(inverse_ready, j + 1)
                V.tensor_tensor(den_sum, den_sum, halves(inverse, TH), ALU.mult)
                dve.wait_ge(num_summed, j + 1)
                V.tensor_tensor(halves(inverse, TH), num_sum, halves(inverse, TH), ALU.mult).then_inc(y_scaled, 1)

            def finish_2(j):
                dve.wait_ge(y_scaled, j + 1)
                V.scalar_tensor_tensor(halves(slot(k_all, j), TH), den_sum, 2.0, halves(inverse, TH), ALU.subtract, ALU.mult).then_inc(y_ready, 1)

            def wkv_round(j, par, ahead):
                if ahead:
                    peaks(j + 1, 1 - par)
                if isinstance(j, int) and j == 0:
                    peaks_2(1, 1)
                    own_argument(1, 1)
                    gain_values(0, 0)
                    sums_b(0, 0)
                else:
                    gain_values(j, par)
                    if ahead:
                        peaks_2(j + 1, 1 - par)
                    sums_b(j, par)
                    finish(j - 1)
                    if ahead:
                        own_argument(j + 1, 1 - par)
                    finish_2(j - 1)
                sums_a(j, par)
                if ahead == 2:
                    maxima(j + 2, par)
                weighted(j, par)

            def gate_y(s):
                at_least(dve, attn_done, s.n)
                if s.image:
                    for a in range(2):
                        V.scalar_tensor_tensor(img_cols(rya[:, 0:P])[:, a], img_slots(r_all)[:, a], 1.0, img_slots(k_all)[:, a], ALU.add, ALU.mult)
                    V.scalar_tensor_tensor(ryb[:, 0:64].rearrange("p (g t) -> p g t", g=PAIRS), img_b(r_all), 1.0, img_b(k_all), ALU.add, ALU.mult).then_inc(ry_ready, 1)
                else:
                    rows, at = slice(s.half, s.half + CB), s.pair + B
                    V.scalar_tensor_tensor(rya, slot(r_all, s.b)[:, IMG:T], 1.0, slot(k_all, s.b)[:, IMG:T], ALU.add, ALU.mult)
                    V.scalar_tensor_tensor(ryb[rows], slot(r_all, at)[rows, IMG:T], 1.0, slot(k_all, at)[rows, IMG:T],
                                           ALU.add, ALU.mult).then_inc(ry_ready, 1)

            def residual2(s):
                dve.wait_ge(attn_done, s.n + 1)
                for q in range(s.nt):
                    V.scalar_tensor_tensor(tile(x1, s.tile + q), tile_pair(q // 2)[:, q % 2], -0.5,
                                           tile(x1, s.tile + q), ALU.mult, ALU.add).then_inc(x2_ready, 1)
                hold(dve, x2_ready, s.before + s.nt)
                statistics(s, 0, stat2_step, stats2_ready, x1)

            maxima(0, 0)
            peaks(0, 0)
            peaks_2(0, 0)
            own_argument(0, 0)
            maxima(1, 1)

            def start_mlps():
                dve.wait_ge(y_ready, B + 1)
                gate_y(mlp(0, 0, 0))

            wkv_schedule(dve, wkv_round, start_mlps)
            residual2(mlp(0, 0, 0))
            finish(SLOTS - 1)
            finish_2(SLOTS - 1)

            def normalize2(s):
                at_least(dve, lo2_ready, s.n)
                dve.wait_ge(powers2_ready, s.n + 1)
                write_z(x1, s, 0, 0).then_inc(z2_ready, 1)

            def squares(s, groups):
                for g in groups:
                    dve.wait_ge(kf_relu, s.n * G + g + 1)
                    V.tensor_tensor(kf[:, g, 0:s.nw], kf[:, g, 0:s.nw], kf[:, g, 0:s.nw], ALU.mult).then_inc(kf_ready, 1)

            def gate(s, q):
                dve.wait_ge(gate_tanh, s.before + q + 1)
                V.scalar_tensor_tensor(gv[:, q % 2], th[:, q % 2], 1.0, bank[2 + q % 2][:, 0:C], ALU.add, ALU.mult).then_inc(gated, 1)

            def residual3(s, q):
                dve.wait_ge(gated, s.before + q + 1)
                dve.wait_ge(hx_ready, s.before + q + 1)
                V.scalar_tensor_tensor(tile(hid, s.tile + q), gv[:, q % 2], 0.5, tile(hid, s.tile + q), ALU.mult, ALU.add).then_inc(h3_ready, 1)

            def statistics3(s, q):
                hold(dve, h3_ready, s.before + q + 1)
                V.bn_stats(st[:, 1, q], tile(hid, s.tile + q)).then_inc(stat3_step, 1)
                if q == s.nt - 1:
                    hold(dve, stat3_step, s.before + s.nt)
                    for t in range(s.nt):
                        ins = V.bn_aggr(mv2[:, 1, t], st[:, 1, t])
                    ins.then_inc(stats3_ready, 1)

            def quantize_x(s):
                dve.wait_ge(powers3_ready, s.n + 1)
                for q in range(s.nt):
                    V.tensor_scalar(xs[:, q], tile(hid, s.tile + q), mv2[:, 1, q, 0:1], rs2[:, 1, 0, q:q + 1],
                                    ALU.subtract, ALU.mult).then_inc(xs_ready, 1)
                dve.wait_ge(xs_ready, s.before + s.nt)
                V.tensor_scalar(xs[:, 0:s.nt], xs[:, 0:s.nt], QP, QN, ALU.min, ALU.max).then_inc(xs_clipped, 1)
                dve.wait_ge(xs_clipped, s.n + 1)
                at_least(dve, xq_turned, s.n)
                V.tensor_scalar(xq[:, 0:s.nt], xs[:, 0:s.nt], MAGIC, MAGIC, ALU.add, ALU.subtract).then_inc(xq_ready, 1)

            def turned(s):
                dve.wait_ge(xq_turned, s.n + 1)
                at_least(dve, up_done, s.n * G)
                ps = bank[1][:].bitcast(BF16).rearrange("p (a n) -> p a n", a=2)
                V.tensor_copy(xqt[:, 0, 0:s.nw], ps[:, 0, 0:s.nw])
                V.tensor_copy(xqt[0:CB, 1, 0:s.nw], ps[0:CB, 1, 0:s.nw]).then_inc(xqt_ready, 1)

            def quantize(dst, raw, inv):
                did(V.tensor_tensor(raw, raw, inv, ALU.mult))
                settled()
                did(V.tensor_scalar(raw, raw, QP, QN, ALU.min, ALU.max))
                settled()
                did(V.tensor_scalar(dst, raw, MAGIC, MAGIC, ALU.add, ALU.subtract))

            def prepare_ffn_1():
                dve.wait_ge(ffn_loaded, 16 * 3)
                dve.wait_ge(inv_copied, 2)
                quantize(q1_w[:], w1_raw, twice(inv_row))

            def prepare_ffn_2():
                quantize(q2_w[:], w2_raw, bass.AP(inv2_row.tensor, inv2_row.offset, [list(inv2_row.ap[0]), [0, G], [1, C]]))

            def prepare_scales():
                did(V.reduce_sum(aq[:, 0:1], a1_row, AX_X))
                did(V.reduce_sum(aq[:, 2:3], a2_row, AX_X))
                settled()
                did(V.tensor_scalar(aq[:, 0:1], aq[:, 0:1], 1.0 / C, None, ALU.mult))
                did(V.tensor_scalar(aq[:, 2:3], aq[:, 2:3], 1.0 / HID, None, ALU.mult))
                settled()
                did(V.reciprocal(aq[:, 1:2], aq[:, 0:1]))
                did(V.reciprocal(aq[:, 3:4], aq[:, 2:3]))
                did(V.tensor_copy(b2s[:], b2_row))
                did(V.tensor_scalar(scale1[:], aw1c, aq[:, 0:1], None, ALU.mult))
                did(V.tensor_scalar(scale2[:], aw2, aq[:, 2:3], None, ALU.mult))
                settled()
                did(V.tensor_scalar(aq[:, 7:8], aq[:, 3:4], CLIP, None, ALU.mult))
                settled()
                did(V.scalar_tensor_tensor(aq[:, 6:7], aq[:, 3:4], -CLIP, aq[:, 7:8], ALU.mult, ALU.max))
                settled()
                did(V.tensor_scalar(aq[:, 4:5], aq[:, 6:7], QP, None, ALU.min))
                did(V.tensor_scalar(aq[:, 5:6], aq[:, 6:7], -1.0, QN, ALU.mult, ALU.max))
                settled()

            def scale_hidden(s, pair):
                g = 2 * pair
                dve.wait_ge(gelu_ready, s.n * G + g + 2)
                V.tensor_scalar(ge[:, g:g + 2, 0:s.nw], ge[:, g:g + 2, 0:s.nw], aq[:, 3:4], aq[:, 4:5], ALU.mult, ALU.min).then_inc(ge_scaled, 1)

            def round_hidden(s, pair):
                g = 2 * pair
                dve.wait_ge(ge_scaled, s.n * (G // 2) + pair + 1)
                V.tensor_scalar(ge[:, g:g + 2, 0:s.nw], ge[:, g:g + 2, 0:s.nw], aq[:, 5:6], MAGIC, ALU.max, ALU.add).then_inc(ge_rounded, 1)

            def scaled_out(s):
                at_least(dve, out_ready, s.before)
                for q in range(0, s.nt, 2):
                    n = min(2, s.nt)
                    dve.wait_ge(down_done, s.before + q + n)
                    V.tensor_tensor(y2[:, q:q + n], tile_pair(q // 2)[:, 0:n], twice(scale2[:])[:, 0:n], ALU.mult).then_inc(y2_ready, n)

            def round_of(now, last, then):
                mine = [g for g in range(G) if g not in POOL_SQUARES]
                first = not (now or last)
                short = now and now.image
                if then and not first:
                    gate_y(then)
                if now and not last:
                    prepare_ffn_1()
                if last:
                    quantize_x(last)
                if now:
                    squares(now, mine[:2])
                if then and short:
                    residual2(then)
                if last:
                    turned(last)
                if now and not last:
                    prepare_ffn_2()
                if now:
                    squares(now, mine[2:])
                if now and not last:
                    prepare_scales()
                if then and not (first or short):
                    residual2(then)
                if last:
                    scale_hidden(last, 0)
                    scale_hidden(last, 1)
                    round_hidden(last, 0)
                for q in range(QT):
                    if now and q < now.nt:
                        gate(now, q)
                    if last and q == 0:
                        round_hidden(last, 1)
                        scale_hidden(last, 2)
                    if last and q == 1:
                        round_hidden(last, 2)
                    if now and 0 < q <= now.nt:
                        statistics3(now, q - 1)
                    if now and q < now.nt:
                        residual3(now, q)
                    if then and q == 0:
                        normalize2(then)
                    if then and q == 1:
                        low_half(then, halves2, hi2_ready, lo2_ready)
                if now and now.nt == QT:
                    statistics3(now, QT - 1)
                if last:
                    scaled_out(last)

            dve.wait_ge(y_ready, SLOTS)
            mlp_schedule(dve, round_of)

        @block.scalar
        def _(act):
            A = nc.scalar
            for dst, src in ((col[:], cols), (wa_raw, attn_w)):
                act.dma_start(dst, src).then_inc(attn_loaded, 16)
            for dst, src in ((kf_raw, kf_src), (rf_raw, rf_src), (wo_w[:], wo_src), (vf_w[:], vf_src)):
                act.dma_start(dst, src).then_inc(mlp_loaded, 16)

            def high_half(s, halves_, z_written, turned_, hi):
                act.wait_ge(z_written, s.n + 1)
                at_least(act, turned_, s.n)
                A.activation(halves_[:, 0:s.nt, 0:C], z[:, 0:s.nt], ACT.Identity).then_inc(hi, 1)

            def take_turned(s, dst, turned_, ready):
                act.wait_ge(turned_, s.n + 1)
                A.activation(dst[:, 0:2, 0:s.nw], turned_z[:, :, 0:s.nw], ACT.Identity)
                A.activation(dst[:, 2, 0:s.nw], turned_zb[:, 0:s.nw], ACT.Identity).then_inc(ready, 1)

            def store(dst, src, func, column, semaphore):
                scale = 1 / WSCALE if func == ACT.Identity else 0.5 / WSCALE
                A.activation(dst, src, func, bias=bias[:, column:column + 1], scale=scale).then_inc(semaphore, 1)

            def split_mlp_weights():
                act.wait_ge(lnw_ready, 4)
                act.wait_ge(mlp_loaded, 16 * 4)
                for i, (raw, scaled, w) in enumerate(((kf_raw, kf_scaled, kf_w), (rf_raw, rf_scaled, rf_w))):
                    for h in range(2):
                        A.activation(scaled[:, h], raw[:, h], ACT.Identity, scale=lnw[:, 2 + h:3 + h]).then_inc(mlp_scaled, 1)
                    act.wait_ge(mlp_scaled, 2 * i + 2)
                    A.activation(w[:, 0::2], scaled, ACT.Identity).then_inc(mlp_hi_ready, 1)

            def projection_round(now, then, after):
                if then:
                    high_half(then, halves1, z_ready, z_turned, hi_ready)
                pair = done_pair(now)
                if pair is not None:
                    hold(act, kb_done, pair + 1)
                    store(slot(k_all, pair + B)[:, IMG:T], bank[5][:], ACT.Identity, 3, k_stored)
                    hold(act, projected, pair * 2 + 2)
                    store(slot(r_all, pair + B)[:, IMG:T], bank[7][:], ACT.Tanh, 13, r_stored)
                if now:
                    hold(act, ka_done, now.n + 1)
                    if now.image:
                        store(img_slots(k_all), img_cols(bank[2][:, 0:P]), ACT.Identity, 0, k_stored)
                    else:
                        store(slot(k_all, now.b)[:, IMG:T], bank[2][:], ACT.Identity, 0, k_stored)
                if then:
                    if not now:
                        act.wait_ge(constants_ready, 1)
                    take_turned(then, proj_z16[then.par], z_turned, z16_ready)
                if now:
                    hold(act, ra_done, now.n + 1)
                    if now.image:
                        store(img_slots(r_all), img_cols(bank[4][:, 0:P]), ACT.Tanh, 12, r_stored)
                    else:
                        store(slot(r_all, now.b)[:, IMG:T], bank[4][:], ACT.Tanh, 12, r_stored)
                if now and isinstance(now.n, int) and now.n == 0:
                    split_mlp_weights()
                if now and now.image:
                    act.wait_ge(kb_done, PAIRS + 1)
                    store(img_b(k_all), bank[5][:, 0:64].rearrange("p (g t) -> p g t", g=PAIRS), ACT.Identity, 3, k_stored)
                    act.wait_ge(projected, B + 1)
                    store(img_b(r_all), bank[7][:, 0:64].rearrange("p (g t) -> p g t", g=PAIRS), ACT.Tanh, 13, r_stored)

            projection_schedule(act, projection_round)

            def decays(j, par):
                act.wait_ge(decay_arg, j + 1)
                A.activation(decay[par], decay[par], ACT.Exp, bias=rate[:, 0, bass.ds(j, 1)]).then_inc(decay_exp, 1)

            def mixes(j, par):
                act.wait_ge(mix_arg, j + 1)
                A.activation(mix[par][:, 0:2 * T], mix[par][:, 0:2 * T], ACT.Exp)
                act.wait_ge(own_arg, j + 1)
                A.activation(mix[par][:, 2 * T:3 * T], mix[par][:, 2 * T:3 * T], ACT.Exp, bias=rate[:, 1, bass.ds(j, 1)]).then_inc(mix_exp, 1)

            def gains(j, par):
                act.wait_ge(gain_arg, j + 1)
                A.activation(halves(gain[par], TH), gain_args, ACT.Exp).then_inc(gain_exp, 1)

            def invert(j):
                act.wait_ge(den_summed, j + 1)
                if not (isinstance(j, int) and j == 0):
                    act.wait_ge(y_ready, j)
                A.activation(halves(inverse, TH), den_sum, ACT.Ln).then_inc(den_log, 1)
                act.wait_ge(den_log, j + 1)
                A.activation(inverse, inverse, ACT.Exp, scale=-1.0).then_inc(inverse_ready, 1)

            def copy_k(j, par):
                if not (isinstance(j, int) and j < 2):
                    hold(act, gain_v_ready, j - 1)
                    hold(act, sums_b_ready, j - 1)
                A.activation(gain[par][:, T:2 * T], slot(k_all, j), ACT.Copy).then_inc(k_copied, 1)

            def wkv_round(j, par, ahead):
                if not (isinstance(j, int) and j == 0):
                    invert(j - 1)
                if ahead:
                    decays(j + 1, 1 - par)
                if ahead == 2:
                    copy_k(j + 2, par)
                if ahead:
                    gains(j + 1, 1 - par)
                    mixes(j + 1, 1 - par)

            act.wait_ge(k_stored, 2 + B + PAIRS)
            act.wait_ge(projected, 1 + B)
            act.wait_ge(mlp_split, 4)
            act.preload_act_table_set("natural_log_exp_and_others")
            copy_k(0, 0)
            copy_k(1, 1)
            decays(0, 0)
            gains(0, 0)
            mixes(0, 0)
            wkv_schedule(act, wkv_round)
            invert(SLOTS - 1)

            def relus(s):
                at_least(act, gate_done, s.before)
                for g in range(G):
                    act.wait_ge(kf_done, s.n * G + g + 1)
                    A.activation(kf[:, g, 0:s.nw], bank[4 + g % 2][:, 0:s.nw], ACT.Relu, bias=bias[:, 6 + g:7 + g], scale=1 / WSCALE).then_inc(kf_relu, 1)

            def gate(s, q):
                act.wait_ge(gate_done, s.before + q + 1)
                at_least(act, gated, s.before + max(q - 1, 0))
                A.activation(th[:, q % 2], bank[2 + q % 2][:, 256:256 + C], ACT.Tanh, scale=0.5 / WSCALE).then_inc(gate_tanh, 1)

            def gelus(s):
                at_least(act, hq_ready, s.n * (G // 2))
                for g in range(G):
                    act.wait_ge(up_done, s.n * G + g + 1)
                    A.activation(ge[:, g, 0:s.nw], bank[UP_BANK[g]][:, 0:s.nw], ACT.Gelu, bias=b1s[:, g:g + 1], scale=scale1[:, g:g + 1]).then_inc(gelu_ready, 1)

            def hidden(s, pair):
                g = 2 * pair
                act.wait_ge(ge_rounded, s.n * (G // 2) + pair + 1)
                if pair == 0:
                    at_least(act, down_done, s.before)
                A.activation(hq[:, g:g + 2, 0:s.nw], ge[:, g:g + 2, 0:s.nw], ACT.Copy, bias=-MAGIC).then_inc(hq_ready, 1)

            def round_of(now, last, then):
                if now:
                    relus(now)
                if last:
                    gelus(last)
                for q in range(QT):
                    if now and q < now.nt:
                        gate(now, q)
                    if last and q < G // 2:
                        hidden(last, q)
                    if then and q == 0:
                        high_half(then, halves2, z2_ready, z2_turned, hi2_ready)
                if then:
                    take_turned(then, mlp_z16[then.par], z2_turned, z16b_ready)

            act.preload_act_table_set("gelu_and_others")
            act.wait_ge(y_ready, SLOTS)
            act.wait_ge(inv_spread, 1)
            A.activation(inv_row, inv_psum[:, 0:HID], ACT.Identity).then_inc(inv_copied, 1)
            A.activation(inv2_row, inv_psum[:, HID:HID + C], ACT.Identity).then_inc(inv_copied, 1)
            mlp_schedule(act, round_of)

        @block.tensor
        def _(pe):
            def bias_column(dst, raw, cols, b):
                pe.matmul(dst, raw[:, 0, cols], vec(b), start=True, stop=False)
                return pe.matmul(dst, raw[0:CB, 1, cols], vec(b + "b")[0:CB], start=False, stop=True)

            pe.wait_ge(attn_loaded, 16 * 2)
            for j in range(3):
                bias_column(bank[3][:, j:j + 1], wa_raw, slice(j * CA, (j + 1) * CA), "ln1_b")
                for half in (0, CB):
                    mm = bias_column(bank[3][half:half + CB, 3 + j:4 + j], wa_raw, slice(GB + j * CB, GB + (j + 1) * CB), "ln1_b")
            mm.then_inc(bias_done, 1)
            pe.wait_ge(dct_loaded, 32)
            for h in range(2):
                for a in range(2):
                    mm = pe.matmul(bank[5 + h][:, 0:3 * PATCHES], kron_sb[:, a, h * P:(h + 1) * P], xt_sb[:, a], start=a == 0, stop=a == 1)
                mm.then_inc(dct_done, 1)

            def image_tokens():
                pe.wait_ge(dct_copied, 2)
                pe.wait_ge(tok_loaded, 16)
                for c in range(3):
                    for h in range(2):
                        mm = pe.matmul(bank[7][:, 0:C], yt[:, h, c], tokw_sb[:, 2 * c + h], start=c + h == 0, stop=c + h == 3)
                mm.then_inc(img_done, 1)
                pe.wait_ge(mlp_loaded, 16 * 4)
                for g in range(G):
                    bias_column(bank[6][:, g:g + 1], kf_raw, slice(g * P, (g + 1) * P), "ln2_b")
                dst = bank[6][:, 256:256 + C]
                pe.matmul(dst, vec("ln2_b").to_broadcast([P, P]), rf_raw[:, 0], start=True, stop=False)
                pe.matmul(dst, vec("ln2_bb")[0:CB].to_broadcast([CB, P]), rf_raw[0:CB, 1], start=False, stop=True).then_inc(late_biases_done, 1)
                pe.wait_ge(bias_copied, 2)

            def turn(s, halves_, done):
                for q in range(s.nt):
                    cols = slice(q * P, (q + 1) * P)
                    for dst, at in ((turned_z[:, 0], HI), (turned_z[:, 1], LO_A), (turned_zb, CA)):
                        mm = pe.transpose(dst[:, cols], halves_[:, q, at:at + P], id16[:])
                mm.then_inc(done, 1)

            def group(dst, w, cols, zt, rhs):
                for i, (ww, zz) in enumerate(((0, 0), (0, 1), (1, 0), (2, 2), (3, 2))):
                    mm = pe.matmul(dst, w[:, ww, cols], zt[:, zz, rhs], start=i == 0, stop=i == 4)
                return mm

            def project_a(s, j, stored, done):
                if s.image:
                    pe.wait_ge(stored, 3 * PAIRS - 1)
                elif s.par:
                    pe.wait_ge(stored, s.pair * 3 + 1)
                elif not (isinstance(s.pair, int) and s.pair == 0):
                    pe.wait_ge(stored, s.pair * 3 - 1)
                group(bank[2 + j][:, 0:s.nw], kvr_w, slice(j * CA, (j + 1) * CA), proj_z16[s.par], slice(0, s.nw)).then_inc(done, 1)

            def projection_round(now, then, after):
                if now:
                    pe.wait_ge(z16_ready, now.n + 1)
                    project_a(now, 0, k_stored, ka_done)
                    project_a(now, 1, v_stored, va_done)
                if then:
                    pe.wait_ge(lo_ready, then.n + 1)
                    if not now:
                        pe.wait_ge(constants_ready, 1)
                    turn(then, halves1, z_turned)
                if now:
                    project_a(now, 2, r_stored, ra_done)
                if now and isinstance(now.n, int) and now.n == 0:
                    image_tokens()
                if now:
                    zt, p = proj_z16[now.par], now.pair
                    for j, (stored, done) in enumerate(((k_stored, kb_done), (v_stored, vb_done), (r_stored, projected))):
                        wcols = slice(GB + j * CB, GB + (j + 1) * CB)
                        if now.image:
                            pe.wait_ge(stored, 3 * PAIRS)
                            group(bank[5 + j][0:CB, 0:64], kvr_w, wcols, zt, slice(0, 64))
                            group(bank[5 + j][CB:P, 0:64], kvr_w, wcols, zt, slice(64, 128)).then_inc(done, 1)
                        else:
                            if not now.par:
                                at_least(pe, stored, p * 3)
                            mm = group(bank[5 + j][now.half:now.half + CB], kvr_w, wcols, zt, slice(0, now.nw))
                            if now.par or j == 2:
                                mm.then_inc(done, 1)

            projection_schedule(pe, projection_round)

            def gain_arguments(j, par):
                hold(pe, env_ready, j + 1)
                if not (isinstance(j, int) and j == 0):
                    hold(pe, gain_exp, j)
                for i in range(4):
                    at = i % 2 * TH
                    pe.matmul(gain_args[:, i], id32[:], gain[par][:, T + at:T + at + TH], start=True, stop=False)
                    mm = pe.matmul(gain_args[:, i], minus_id[:], incl(env[par])[:, i // 2, at:at + TH], start=False, stop=True)
                mm.then_inc(gain_arg, 1)

            def summed(dst, states, own, done):
                for h in range(2):
                    cols = slice(h * TH, (h + 1) * TH)
                    for i, part in enumerate((excl(states)[:, 0, cols], excl(states)[:, 1, cols], own[:, cols])):
                        mm = pe.matmul(dst[:, h], id32[:], part, start=i == 0, stop=i == 2)
                mm.then_inc(done, 1)

            def sums(j, par):
                hold(pe, den_parts, j + 1)
                if not (isinstance(j, int) and j == 0):
                    hold(pe, y_ready, j)
                summed(den_sum, sbk, mix[par][:, 2 * T:3 * T], den_summed)
                hold(pe, own_num, j + 1)
                hold(pe, num_parts, j + 1)
                summed(num_sum, sa, own_part, num_summed)

            def wkv_round(j, par, ahead):
                sums(j, par)
                if ahead == 2:
                    gain_arguments(j + 2, par)

            def attention_out(s):
                pe.wait_ge(ry_ready, s.n + 1)
                if not (isinstance(s.n, int) and s.n < 3):
                    pe.wait_ge(y2_ready, s.before_two)
                if s.image:
                    for a in range(2):
                        rows = slice(a * 64, a * 64 + 64)
                        pe.matmul(tile_pair(0)[rows, 0], rya[:, rows], wo_w[:, 0], start=True, stop=False)
                        mm = pe.matmul(tile_pair(0)[rows, 0], ryb[rows, 0:64], wo_w[rows, 1], start=False, stop=True)
                else:
                    for q in range(QT):
                        cols = slice(q * P, (q + 1) * P)
                        dst = tile_pair(q // 2)[:, q % 2]
                        rows = slice(s.half, s.half + CB)
                        pe.matmul(dst, rya[:, cols], wo_w[:, 0], start=True, stop=False)
                        mm = pe.matmul(dst, ryb[rows, cols], wo_w[rows, 1], start=False, stop=True)
                mm.then_inc(attn_done, 1)

            pe.wait_ge(edges_ready, 9)
            gain_arguments(0, 0)
            gain_arguments(1, 1)
            def start_mlps():
                pe.wait_ge(gain_exp, SLOTS)
                attention_out(mlp(0, 0, 0))

            wkv_schedule(pe, wkv_round, start_mlps)

            def turn_z(s, last):
                if last:
                    pe.wait_ge(gelu_ready, last.n * G + G)
                pe.wait_ge(lo2_ready, s.n + 1)
                turn(s, halves2, z2_turned)

            def squared_in(s):
                pe.wait_ge(z16b_ready, s.n + 1)
                for g in range(G):
                    if g < 2:
                        if isinstance(s.n, int) and s.n < 2:
                            pe.wait_ge(inv_copied, 2)
                        else:
                            pe.wait_ge(gelu_ready, s.n * G - G)
                    else:
                        pe.wait_ge(kf_relu, s.n * G + g - 1)
                    group(bank[4 + g % 2][:, 0:s.nw], kf_w, slice(g * P, (g + 1) * P), mlp_z16[s.par], slice(0, s.nw)).then_inc(kf_done, 1)

            def gated_out(s, last):
                pe.wait_ge(kf_ready, s.n * G + G)
                if last:
                    pe.wait_ge(gelu_ready, last.n * G + 2)
                for q in range(s.nt):
                    cols = slice(q * P, (q + 1) * P)
                    at_least(pe, gated, s.before + max(q - 1, 0))
                    ps = bank[2 + q % 2]
                    for g in range(G):
                        pe.matmul(ps[:, 0:C], kf[:, g, cols], vf_w[:, g], start=g == 0, stop=g == G - 1)
                    dst = ps[:, 256:256 + C]
                    zt = mlp_z16[s.par]
                    for i, (zz, ww) in enumerate(((0, 0), (1, 0), (0, 1), (2, 2), (2, 3))):
                        pe.matmul(dst, zt[:, zz, cols], rf_w[:, ww], start=i == 0, stop=False)
                    pe.matmul(dst, pick[:], rf_bias[:], start=False, stop=True).then_inc(gate_done, 1)

            def turn_x(s):
                pe.wait_ge(xq_ready, s.n + 1)
                ps = bank[1][:].bitcast(BF16).rearrange("p (a n) -> p a n", a=2)
                for q in range(s.nt):
                    cols = slice(q * P, (q + 1) * P)
                    pe.transpose(ps[:, 0, cols], xq[:, q, 0:CA], idb[:])
                    mm = pe.transpose(ps[0:CB, 1, cols], xq[:, q, CA:C], idb[:])
                mm.then_inc(xq_turned, 1)

            def up(s, now):
                pe.wait_ge(xqt_ready, s.n + 1)
                for g in range(G):
                    if g == 0:
                        at_least(pe, gated, s.before + s.nt)
                        at_least(pe, gelu_ready, s.n * G)
                    elif g == 2 and now:
                        pe.wait_ge(kf_relu, now.n * G + G)
                    cols = slice(g * P, (g + 1) * P)
                    dst = bank[UP_BANK[g]][:, 0:s.nw]
                    pe.matmul(dst, q1_w[:, 0, cols], xqt[:, 0, 0:s.nw], start=True, stop=False)
                    pe.matmul(dst, q1_w[0:CB, 1, cols], xqt[0:CB, 1, 0:s.nw], start=False, stop=True).then_inc(up_done, 1)

            def down(s, then):
                if then:
                    pe.wait_ge(x2_ready, then.before + then.nt)
                pe.wait_ge(hq_ready, s.n * (G // 2) + G // 2)
                if not then:
                    at_least(pe, y2_ready, s.before)
                for q in range(s.nt):
                    for g in range(G):
                        mm = pe.matmul(tile_pair(q // 2)[:, q % 2], hq[:, g, q * P:(q + 1) * P], q2_w[:, g], start=g == 0, stop=g == G - 1)
                    mm.then_inc(down_done, 1)

            def round_of(now, last, then):
                short = now and now.image
                if now:
                    squared_in(now)
                if then and short:
                    attention_out(then)
                if last:
                    turn_x(last)
                if then and (now or last) and not short:
                    attention_out(then)
                if last:
                    up(last, now)
                if now:
                    gated_out(now, last)
                if then:
                    turn_z(then, last)
                if last:
                    down(last, then)

            pe.wait_ge(y_ready, SLOTS)
            for g in range(G):
                pe.matmul(inv_psum[:, g * P:(g + 1) * P], inverses[:, g:g + 1].to_broadcast([P, P]), id32[:], start=True, stop=True)
            pe.matmul(inv_psum[:, HID:HID + CA], inverses[:, G:G + 1].to_broadcast([P, P]), id32[:], start=True, stop=True)
            pe.matmul(inv_psum[:, HID + CA:HID + C], inverses[0:CB, G + 1:G + 2].to_broadcast([CB, P]), id32[0:CB, 0:CB],
                      start=True, stop=True).then_inc(inv_spread, 1)
            mlp_schedule(pe, round_of)


def kernel(**inputs):
    import numpy as np
    import concourse.bacc as bacc
    from concourse.bass_utils import run_bass_kernel_spmd

    a = {n: np.asarray(x) for n, x in inputs.items()}
    at = {n[len("L0_attn_"):]: x for n, x in a.items() if n.startswith("L0_attn_")}

    xt = a["x"].reshape(PAIRS, 2, 3, 4, 16, 4, 16).transpose(4, 6, 2, 1, 0, 3, 5).reshape(2, P, 3, PATCHES).transpose(1, 0, 2, 3)
    k = np.arange(16.0)
    dct = 2.0 * np.cos(np.pi * (2.0 * k + 1.0) * k[:, None] / 32.0)
    kron = np.kron(dct, dct).T.astype(np.float32).reshape(2, P, 256).transpose(1, 0, 2)
    tok_w = a["L0_tok_W"].T.reshape(6, P, C).transpose(1, 0, 2)

    def rows2(w):
        return np.stack([w[0:CA], np.concatenate([w[CA:C], w[CA:C]])], axis=1)

    kvr = [at["Wk_a"], at["Wv_a"], at["Wr_a"]]
    attn_w = rows2(np.concatenate([w[0:CA].T for w in kvr] + [w[CA:C].T for w in kvr], axis=1))
    vectors = [at[n] for n in ("ln1_w", "ln1_b", "ln2_w", "ln2_b", "decay", "first")] + [a["L0_ffn_alpha_w2"]]
    cols = np.concatenate([rows2(v[:, None])[:, :, 0] for v in vectors]
                          + [a["L0_ffn_alpha_w1"].reshape(G, P).T, a["L0_ffn_b1"].reshape(G, P).T], axis=1)
    rows = np.concatenate([a["L0_ffn_" + n] for n in ROWS])[None]
    arrays = {
        "txt": a["txt"], "xt": xt, "kron": kron, "tok_w": tok_w, "ident": np.eye(P, dtype=np.float32),
        "cols": cols, "rows": rows, "attn_w": attn_w,
        "kf_src": rows2(at["Wk_f"].T), "rf_src": rows2(at["Wr_f"].T), "wo_src": rows2(at["Wo_a"].T),
        "vf_src": at["Wv_f"].T.reshape(G, P, C).transpose(1, 0, 2),
        "w1": rows2(a["L0_ffn_w1"].T), "w2": a["L0_ffn_w2"].T.reshape(G, P, C).transpose(1, 0, 2),
    }
    arrays = {n: np.ascontiguousarray(x) for n, x in arrays.items()}
    nc = bacc.Bacc("TRN2", target_bir_lowering=False, num_devices=1)
    args = {n: nc.dram_tensor(n, x.shape, mybir.dt.from_np(x.dtype), kind="ExternalInput").ap() for n, x in arrays.items()}
    out = nc.dram_tensor("out", (B, T, C), F32, kind="ExternalOutput").ap()
    fusion_kernel(nc, **args, out=out)
    return run_bass_kernel_spmd(nc, [arrays], core_ids=[0]).results[0]["out"]
```
